# Optimizing a Trainium2 kernel written in Bass

```python
import numpy as np
import jax
import jax.numpy as jnp

def _softmax(x, axis=-1):
    return jax.nn.softmax(x, axis=axis)

def _gelu(x):
    return jax.nn.gelu(x, approximate=True)

def _silu(x):
    return jax.nn.silu(x)

def _sigmoid(x):
    return jax.nn.sigmoid(x)

def _layernorm(x, axis=-1, eps=1e-05):
    m = jnp.mean(x, axis=axis, keepdims=True)
    v = jnp.var(x, axis=axis, keepdims=True)
    return (x - m) / jnp.sqrt(v + eps)

def _scatter_add(tgt, idx, src, axis=0):
    return tgt.at[idx].add(src)

def _segment_sum(src, seg, n):
    return jax.ops.segment_sum(src, seg, n)
kernel_name = 'mk_gnn_preln_d2_gnn_r8_9b3e1d'

def setup_inputs(seed: int=0):
    np.random.seed(seed)
    _w = jnp.asarray

    def _rec_inputs():
        import jax
        import jax.numpy as jnp
        _gk = jax.random.key(seed)
        x = -0.0005121 + 1.001 * jax.random.normal(jax.random.fold_in(_gk, 1), (6250, 64), jnp.float32)
        _s = jax.random.randint(jax.random.fold_in(_gk, 2), (100000,), 0, 6250, jnp.int32)
        _d = jax.random.randint(jax.random.fold_in(_gk, 3), (100000,), 0, 6250, jnp.int32)
        _loop = jnp.arange(6250, dtype=jnp.int32)
        src = jnp.concatenate([_s, _d, _loop])
        dst = jnp.concatenate([_d, _s, _loop])
        _o = jnp.argsort(dst, stable=True)
        src = src[_o]
        dst = dst[_o]
        edge_attr_64 = -2.25437e-05 + 0.999858 * jax.random.normal(jax.random.fold_in(_gk, 12), (206250, 64), jnp.float32)
        edge_weight = jax.random.uniform(jax.random.fold_in(_gk, 14), (206250,), jnp.float32, 0.0, 0.999998)
        node_vec = jax.random.uniform(jax.random.fold_in(_gk, 15), (6250,), jnp.float32, 0.0, 0.999957)
        node_vec1 = jax.random.uniform(jax.random.fold_in(_gk, 16), (6250, 1), jnp.float32, 0.0, 0.999993)
        node_vec1_n2 = jax.random.uniform(jax.random.fold_in(_gk, 17), (6250, 1), jnp.float32, 0.0, 0.999993)
        return (x, src, dst, edge_attr_64, edge_weight, node_vec, node_vec1, node_vec1_n2)
    x, src, dst, edge_attr_64, edge_weight, node_vec, node_vec1, node_vec1_n2 = _rec_inputs()

    def _L0_gnn_setup():
        import jax, jax.numpy as jnp
        import numpy as np
        N_NODES = 6250
        N_EDGES = 50000
        D_IN = 64
        D_OUT = 64
        G_HID = 128
        F_HID = 64
        HEADS = 4
        NEG_SLOPE = 0.2

        def _lrelu(v):
            return jnp.where(v >= 0, v, NEG_SLOPE * v)
        key = jax.random.key(seed)
        ks = jax.random.split(key, 8)
        x = jax.random.normal(ks[0], (N_NODES, D_IN), dtype=jnp.float32)
        edge_index = jax.random.randint(ks[1], (2, N_EDGES), 0, N_NODES, dtype=jnp.int64)
        pos = jax.random.uniform(ks[2], (N_NODES,), dtype=jnp.float32)
        s = 0.05
        gate_w1 = jax.random.normal(ks[3], (HEADS, F_HID, 2 * D_IN), dtype=jnp.float32) * s
        gate_w2 = jax.random.normal(ks[4], (HEADS, 1, F_HID), dtype=jnp.float32) * s
        msg_w1 = jax.random.normal(ks[5], (HEADS, G_HID, 2 * D_IN), dtype=jnp.float32) * s
        msg_w2 = jax.random.normal(ks[6], (HEADS, D_OUT, G_HID), dtype=jnp.float32) * s
        return {'x': x, 'edge_index': edge_index, 'pos': pos, 'gate_w1': gate_w1, 'gate_w2': gate_w2, 'msg_w1': msg_w1, 'msg_w2': msg_w2}
    _L0_gnn_all = _L0_gnn_setup()
    _L0_gnn_in = {k: v for k, v in _L0_gnn_all.items() if k in ('gate_w1', 'gate_w2', 'msg_w1', 'msg_w2')}
    del _L0_gnn_all

    def _L1_gnn_setup():
        import jax, jax.numpy as jnp
        import numpy as np
        N_SRC = 12500
        N_DST = 12500
        E = 125000
        D = 64
        key = jax.random.key(seed)
        ks = jax.random.split(key, 10)
        return {'weight': jax.random.normal(ks[0], (N_SRC, D), jnp.float32) * 0.02, 'review_feat': jax.random.normal(ks[1], (E, D), jnp.float32), 'attn': jax.random.uniform(ks[2], (E,), jnp.float32), 'cj': jax.random.uniform(ks[3], (N_SRC, 1), jnp.float32), 'ci': jax.random.uniform(ks[4], (N_DST, 1), jnp.float32), 'prob_w': jax.random.normal(ks[5], (1, D), jnp.float32) * 0.1, 'review_score_w': jax.random.normal(ks[6], (1, D), jnp.float32) * 0.1, 'review_w': jax.random.normal(ks[7], (D, D), jnp.float32) * 0.1, 'src_idx': jax.random.randint(ks[8], (E,), 0, N_SRC, jnp.int32), 'dst_idx': jax.random.randint(ks[9], (E,), 0, N_DST, jnp.int32)}
    _L1_gnn_all = _L1_gnn_setup()
    _L1_gnn_in = {k: v for k, v in _L1_gnn_all.items() if k in ('prob_w', 'review_score_w', 'review_w')}
    del _L1_gnn_all
    return {'x': x, 'src': src, 'dst': dst, 'edge_attr_64': edge_attr_64, 'edge_weight': edge_weight, 'node_vec': node_vec, 'node_vec1': node_vec1, 'node_vec1_n2': node_vec1_n2, 'L0_gnn_gate_w1': _L0_gnn_in['gate_w1'], 'L0_gnn_gate_w2': _L0_gnn_in['gate_w2'], 'L0_gnn_msg_w1': _L0_gnn_in['msg_w1'], 'L0_gnn_msg_w2': _L0_gnn_in['msg_w2'], 'L1_gnn_prob_w': _L1_gnn_in['prob_w'], 'L1_gnn_review_score_w': _L1_gnn_in['review_score_w'], 'L1_gnn_review_w': _L1_gnn_in['review_w']}

def reference(x, src, dst, edge_attr_64, edge_weight, node_vec, node_vec1, node_vec1_n2, L0_gnn_gate_w1, L0_gnn_gate_w2, L0_gnn_msg_w1, L0_gnn_msg_w2, L1_gnn_prob_w, L1_gnn_review_score_w, L1_gnn_review_w):
    import jax
    import jax.numpy as jnp

    def _L0_gnn_ref(x, edge_index, pos, gate_w1, gate_w2, msg_w1, msg_w2):
        import jax, jax.numpy as jnp
        import numpy as np
        N_NODES = 6250
        N_EDGES = 50000
        D_IN = 64
        D_OUT = 64
        G_HID = 128
        F_HID = 64
        HEADS = 4
        NEG_SLOPE = 0.2

        def _lrelu(v):
            return jnp.where(v >= 0, v, NEG_SLOPE * v)
        row, col = (edge_index[0], edge_index[1])
        e = jnp.concatenate([x[row], x[col]], axis=-1)
        g1 = _lrelu(jnp.einsum('ef,hgf->heg', e, gate_w1))
        alpha = _lrelu(jnp.einsum('heg,hog->heo', g1, gate_w2))
        w_edge = pos[col][None, :, None]
        a = w_edge * jnp.exp(alpha)
        seg = lambda t: jax.ops.segment_sum(t, row, num_segments=N_NODES)
        rowsum = jax.vmap(seg)(a)
        inv = 1.0 / rowsum + 1e-16
        alpha_n = a * inv[:, row]
        m1 = _lrelu(jnp.einsum('ef,hgf->heg', e, msg_w1))
        beta = _lrelu(jnp.einsum('heg,hog->heo', m1, msg_w2))
        out_h = jax.vmap(seg)(alpha_n * beta)
        return jnp.mean(out_h, axis=0)

    def _L1_gnn_ref(weight, review_feat, attn, cj, ci, prob_w, review_score_w, review_w, src_idx, dst_idx):
        import jax, jax.numpy as jnp
        import numpy as np
        N_SRC = 12500
        N_DST = 12500
        E = 125000
        D = 64
        pa = jax.nn.sigmoid(review_feat @ prob_w.T)
        ra = jax.nn.sigmoid(review_feat @ review_score_w.T)
        rf = review_feat @ review_w.T
        h_src = weight[src_idx]
        cj_e = cj[src_idx]
        a = attn[:, None]
        m = (h_src * pa + rf * (ra * a)) * cj_e
        h = jax.ops.segment_sum(m, dst_idx, num_segments=ci.shape[0])
        return h * ci
    edge_index = jnp.stack([src, dst])
    h = jnp.maximum(_layernorm(x, axis=-1), 0.0)
    x = x + _L0_gnn_ref(h, edge_index, node_vec, L0_gnn_gate_w1, L0_gnn_gate_w2, L0_gnn_msg_w1, L0_gnn_msg_w2)
    h = jnp.maximum(_layernorm(x, axis=-1), 0.0)
    x = x + _L1_gnn_ref(h, edge_attr_64, edge_weight, node_vec1, node_vec1_n2, L1_gnn_prob_w, L1_gnn_review_score_w, L1_gnn_review_w, src, dst)
    return x

_drawn_inputs = setup_inputs


def setup_inputs(seed=0):
    import zlib

    import numpy as np

    out = dict(_drawn_inputs(seed))
    spreads = {}
    factors = {}
    for name, (base, spread) in spreads.items():
        noise = np.random.default_rng([zlib.crc32(name.encode()), seed]).standard_normal(out[name].shape)
        drawn = base * np.exp(spread * noise) if base else spread * noise
        out[name] = jnp.asarray(drawn.astype(out[name].dtype))
    for name, factor in factors.items():
        out[name] = (out[name] * factor).astype(out[name].dtype)
    return out
```

```python
import concourse.bass as bass
import numpy as np
from concourse import mybir
from contextlib import ExitStack

F32, I32 = mybir.dt.float32, mybir.dt.int32
ALU = mybir.AluOpType
ACT = mybir.ActivationFunctionType
AX = mybir.AxisListType

P = 128
N = 6250
D = 64
E = 206250
H = 4
NT = -(-N // P)
NP = NT * P
ROWS = NP + P
T = 4
B = T * P
NB = 2 * -(-E // (2 * B))
EP = NB * B
W0 = H * D + H + 1
W1 = 2 * D
NK = 6
NL = 3
CH = 7
NCH = NT // CH
SLOPE = 0.2
EPS = 1e-5
ZW = ROWS * W0 // P // 5
assert NT % CH == 0 and NB % 2 == 0 and NB >= 6 and ROWS * W0 % (P * 5) == 0


def gnn(nc, x, src, dst, src_rows, dst_rows, edge_attr, edge_weight, node_vec, node_vec1, node_vec1_n2,
        w1, gate_w2, msg_w2, prob_w, score_w, review_w, out):
    ctx = ExitStack()
    with ctx:
        def sb(name, shape, dt=F32):
            return ctx.enter_context(nc.sbuf_tensor(name, shape, dt))

        def pb(name, shape):
            return ctx.enter_context(nc.psum_tensor(name, shape, F32))

        def sem(name):
            return ctx.enter_context(nc.semaphore(name))

        def dram(name, shape):
            return nc.dram_tensor(name, shape, F32, kind="Internal").ap()

        row_table = dram("row_table", [NP, D])
        col_table = dram("col_table", [NP, D + 1])
        src_table = dram("src_table", [NP, D + 1])
        sums0 = [dram(f"sums0_{t}", [ROWS, W0]) for t in range(T)]
        sums1 = [dram(f"sums1_{t}", [ROWS, W1]) for t in range(T)]

        x_sb = sb("x_sb", [P, NT, D])
        centered = sb("centered", [P, NT, D])
        squares = sb("squares", [P, NT, D])
        table_sb = sb("table_sb", [P, NT, D + 1])
        stat = sb("stat", [P, 4, NT])
        pos_sb = sb("pos_sb", [P, NT])
        cj_sb = sb("cj_sb", [P, NT])
        ci_sb = sb("ci_sb", [P, NT])
        zeros = sb("zeros", [P, ZW])
        ident = sb("ident", [P, P])
        spare = sb("spare", [P, 1])
        before = sb("before", [P, P])
        w1_sb = sb("w1_sb", [P, NK * P])
        gate_w2_sb = sb("gate_w2_sb", [P, 2, 2])
        msg_w2_sb = sb("msg_w2_sb", [P, H, D])
        dots_w = sb("dots_w", [P, 2, D])
        review_w_sb = sb("review_w_sb", [D, D])
        src_sb = [sb(f"src_sb{j}", [P, T], I32) for j in range(2)]
        dst_sb = [sb(f"dst_sb{j}", [P, T], I32) for j in range(2)]
        key_rows = [sb(f"key_rows{j}", [P, T, P], I32) for j in range(2)]
        equal = [sb(f"equal{j}", [P, T, P]) for j in range(2)]
        earlier = sb("earlier", [P, T, P])
        earlier_max = sb("earlier_max", [P, T])
        target = [sb(f"target{j}", [P, T], I32) for j in range(2)]
        ends = [sb(f"ends{j}", [P, T, W1 + 1]) for j in range(2)]
        ends_T = [sb(f"ends_T{j}", [P, B]) for j in range(2)]
        scaled = [sb(f"scaled{j}", [P, B]) for j in range(NL)]
        hidden = [sb(f"hidden{k}", [P, B]) for k in range(NK)]
        alpha_scaled = sb("alpha_scaled", [P, T * H])
        alpha = sb("alpha", [P, T * H])
        alpha_exp = sb("alpha_exp", [P, T, H])
        beta_scaled = sb("beta_scaled", [P, T * H * D])
        beta = sb("beta", [P, T, H, D])
        terms0 = [sb(f"terms0_{j}", [P, T, W0]) for j in range(2)]
        summed0 = [sb(f"summed0_{t}", [P, W0]) for t in range(T)]
        feat = [sb(f"feat{j}", [P, T, D]) for j in range(2)]
        attn = [sb(f"attn{j}", [P, T]) for j in range(2)]
        ends1 = [sb(f"ends1_{j}", [P, T, D + 1]) for j in range(2)]
        products = sb("products", [P, 2, T, D])
        dots = sb("dots", [P, 2, T])
        gates = sb("gates", [P, 2, T])
        feat_gate = sb("feat_gate", [P, T])
        terms1 = [sb(f"terms1_{j}", [P, T, W1]) for j in range(2)]
        summed1 = [sb(f"summed1_{j}", [P, T, W1]) for j in range(2)]
        parts = [sb(f"parts{j}", [P, T, CH, W0]) for j in range(2)]
        inverse = sb("inverse", [P, CH, H])
        empty = sb("empty", [P, CH])
        mean = sb("mean", [P, CH, D])
        feat_T = sb("feat_T", [D, CH, P])

        ps_T = pb("ps_T", [P, B])
        ps_hidden = [pb(f"ps_hidden{j}", [P, B]) for j in range(NL)]
        ps_beta = [pb(f"ps_beta{j}", [P, B]) for j in range(2)]
        ps_alpha = pb("ps_alpha", [P, B])
        ps_sum = pb("ps_sum", [P, B])

        loaded = sem("loaded")
        made = sem("made")
        zeroed = sem("zeroed")
        zeros_set = sem("zeros_set")
        weights_set = sem("weights_set")
        step = sem("step")
        sqrt_in = sem("sqrt_in")
        sqrt_out = sem("sqrt_out")
        tables = sem("tables")
        edge_in = [sem(f"edge_in{j}") for j in range(2)]
        gathered = [sem(f"gathered{j}") for j in range(2)]
        transposed = sem("transposed")
        ends_ready = sem("ends_ready")
        hidden_done = sem("hidden_done")
        scaled_ready = sem("scaled_ready")
        hidden_ready = sem("hidden_ready")
        second_done = sem("second_done")
        alpha_scaled_ready = sem("alpha_scaled_ready")
        alpha_ready = sem("alpha_ready")
        exp_ready = sem("exp_ready")
        weight_ready = sem("weight_ready")
        beta_scaled_ready = sem("beta_scaled_ready")
        beta_ready = sem("beta_ready")
        terms_ready = sem("terms_ready")
        dup_step = sem("dup_step")
        summed = sem("summed")
        summed_ready = sem("summed_ready")
        scattered = [sem(f"scattered{t}") for t in range(T)]
        part_in = [sem(f"part_in{j}") for j in range(2)]
        part_sum = sem("part_sum")
        part_free = sem("part_free")
        edge_in1 = [sem(f"edge_in1_{j}") for j in range(2)]
        gathered1 = [sem(f"gathered1_{j}") for j in range(2)]
        dot_step = sem("dot_step")
        gates_ready = sem("gates_ready")
        terms1_step = sem("terms1_step")
        dup_step1 = sem("dup_step1")
        summed1_done = sem("summed1_done")
        summed1_ready = sem("summed1_ready")
        scattered1 = [sem(f"scattered1_{t}") for t in range(T)]
        part_in1 = [sem(f"part_in1_{j}") for j in range(2)]
        part_sum1 = sem("part_sum1")
        feat_T_done = sem("feat_T_done")
        feat_T_ready = sem("feat_T_ready")
        review_done = sem("review_done")
        chunk_out = sem("chunk_out")
        stored = sem("stored")
        settled = sem("settled")

        def wait(eng, s, value):
            if not (isinstance(value, int) and value <= 0):
                eng.wait_ge(s, value)

        def blocks(eng, body):
            body(0, 0, 0)
            body(1, 0, 1)
            with eng.Fori(1, NB // 2 - 1) as i:
                body(2 * i, i, 0)
                body(2 * i + 1, i, 1)
            body(NB - 2, NB // 2 - 1, 0)
            body(NB - 1, NB // 2 - 1, 1)

        def is_last(b):
            return isinstance(b, int) and b == NB - 1

        def is_last_two(b):
            return isinstance(b, int) and b >= NB - 2

        def settle(eng):
            eng.sem_inc(settled, 1)

        def nodes(dram_ap):
            return dram_ap.rearrange("(p t) w -> p t w", p=P)

        LAYER0_STEPS = [0]

        block = ctx.enter_context(nc.Block())

        @block.sync
        def _(sp):
            sp.dma_start(x_sb[:, :, :], nodes(x)).then_inc(loaded, 16)
            sp.dma_start(pos_sb[:, :], node_vec).then_inc(loaded, 16)
            sp.dma_start(cj_sb[:, :], node_vec1).then_inc(loaded, 16)
            sp.dma_start(ci_sb[:, :], node_vec1_n2).then_inc(loaded, 16)
            sp.dma_start(w1_sb[:, :], w1).then_inc(loaded, 16)
            sp.dma_start(msg_w2_sb[:, :, :], msg_w2).then_inc(loaded, 16)
            sp.dma_start(dots_w[:, 0, :], prob_w.broadcast_to([P, D])).then_inc(loaded, 16)
            sp.dma_start(dots_w[:, 1, :], score_w.broadcast_to([P, D])).then_inc(loaded, 16)
            sp.dma_start(review_w_sb[:, :], review_w).then_inc(loaded, 16)
            sp.wait_ge(weights_set, 1)
            for h in range(H):
                sp.dma_start(gate_w2_sb[(h % 2) * D:(h % 2 + 1) * D, h // 2, h % 2:h % 2 + 1],
                             gate_w2[h]).then_inc(loaded, 16)

            def load0(b, half, j):
                if not (isinstance(b, int) and b < 2):
                    sp.wait_ge(dup_step, 4 * (b - 1))
                    settle(sp)
                    sp.wait_ge(gathered[j], 128 * half)
                    settle(sp)
                sp.dma_start(src_sb[j][:, :], src[bass.ds(b, 1)]).then_inc(edge_in[j], 16)
                sp.dma_start(dst_sb[j][:, :], dst[bass.ds(b, 1)]).then_inc(edge_in[j], 16)
                sp.dma_start(key_rows[j][:, :, :],
                             src_rows[bass.ds(b, 1)].broadcast_to([P, T, P])).then_inc(edge_in[j], 16)

            blocks(sp, load0)

            for c in range(NCH):
                if c == 0:
                    for t in range(T):
                        sp.wait_ge(scattered[t], 16 * NB)
                if c >= 2:
                    sp.wait_ge(part_free, c - 1)
                for t in range(T):
                    sp.dma_start(parts[c % 2][:, t, :, :],
                                 nodes(sums0[t][0:NP, :])[:, c * CH:(c + 1) * CH, :]).then_inc(part_in[c % 2], 16)

            def load1(b, half, j):
                if isinstance(b, int) and b < 2:
                    sp.wait_ge(dup_step, 4 * NB)
                    sp.wait_ge(gathered[j], 128 * (NB // 2))
                else:
                    sp.wait_ge(dup_step1, 4 * (b - 1))
                    settle(sp)
                    sp.wait_ge(gathered1[j], 64 * half)
                    settle(sp)
                    sp.wait_ge(terms1_step, 4 * (b - 1))
                    settle(sp)
                sp.dma_start(src_sb[j][:, :], src[bass.ds(b, 1)]).then_inc(edge_in1[j], 16)
                sp.dma_start(dst_sb[j][:, :], dst[bass.ds(b, 1)]).then_inc(edge_in1[j], 16)
                sp.dma_start(key_rows[j][:, :, :],
                             dst_rows[bass.ds(b, 1)].broadcast_to([P, T, P])).then_inc(edge_in1[j], 16)
                sp.dma_start(feat[j][:, :, :], edge_attr[bass.ds(b, 1)]).then_inc(edge_in1[j], 16)
                sp.dma_start(attn[j][:, :], edge_weight[bass.ds(b, 1)]).then_inc(edge_in1[j], 16)

            blocks(sp, load1)

            for c in range(NCH):
                if c == 0:
                    for t in range(T):
                        sp.wait_ge(scattered1[t], 16 * NB)
                if c < 2:
                    sp.wait_ge(part_free, NCH)
                else:
                    sp.wait_ge(part_free, NCH + c - 1)
                for t in range(T):
                    sp.dma_start(parts[c % 2][:, t, :, 0:W1],
                                 nodes(sums1[t][0:NP, :])[:, c * CH:(c + 1) * CH, :]).then_inc(part_in1[c % 2], 16)
            sp.wait_ge(chunk_out, NCH)
            sp.dma_start(nodes(out), x_sb[:, :, :]).then_inc(stored, 16)
            sp.wait_ge(stored, 16)

        @block.gpsimd
        def _(pool):
            nc.gpsimd.memset(ident[:, :], 0.0).then_inc(made, 1)
            nc.gpsimd.iota(spare[:, :], pattern=[[0, 1]], base=NP, channel_multiplier=1,
                           allow_small_or_imprecise_dtypes=True).then_inc(made, 1)
            pool.wait_ge(made, 2)
            nc.gpsimd.affine_select(out=ident[:, :], in_=ident[:, :], compare_op=ALU.not_equal, fill=1.0,
                                    base=0, pattern=[[-1, P]], channel_multiplier=1).then_inc(made, 1)
            nc.gpsimd.tensor_copy(before[:, :], spare[:, 0:1].broadcast_to([P, P])).then_inc(made, 1)
            pool.wait_ge(made, 4)
            nc.gpsimd.affine_select(out=before[:, :], in_=before[:, :], compare_op=ALU.is_gt, fill=0.0,
                                    base=0, pattern=[[-1, P]], channel_multiplier=1).then_inc(made, 1)

            def gather0(b, half, j):
                pool.wait_ge(edge_in[j], 48 * (half + 1))
                if not (isinstance(b, int) and b < 2):
                    pool.wait_ge(transposed, b - 1)
                    pool.wait_ge(weight_ready, b - 1)
                settle(pool)
                for t in range(T):
                    pool.indirect_dma_start(
                        out=ends[j][:, t, 0:D], out_offset=None, in_=row_table,
                        in_offset=bass.IndirectOffsetOnAxis(ap=src_sb[j][:, t:t + 1], axis=0)).then_inc(gathered[j], 16)
                    pool.indirect_dma_start(
                        out=ends[j][:, t, D:2 * D + 1], out_offset=None, in_=col_table,
                        in_offset=bass.IndirectOffsetOnAxis(ap=dst_sb[j][:, t:t + 1], axis=0)).then_inc(gathered[j], 16)

            def scatter0(b, half, j):
                pool.wait_ge(dup_step, 4 * b + 4)
                for t in range(T):
                    pool.wait_ge(summed_ready, 4 * b + t + 1)
                    wait(pool, scattered[t], 16 * b)
                    settle(pool)
                    pool.indirect_dma_start(
                        out=sums0[t], out_offset=bass.IndirectOffsetOnAxis(ap=target[j][:, t:t + 1], axis=0),
                        in_=summed0[t][:, :], in_offset=None, compute_op=ALU.add).then_inc(scattered[t], 16)

            def edges0(b, half, j):
                if not is_last_two(b):
                    gather0(b + 2, half + 1, j)
                scatter0(b, half, j)

            pool.wait_ge(tables, 32)
            gather0(0, 0, 0)
            gather0(1, 0, 1)
            pool.wait_ge(zeroed, 16 * (5 * T + T))
            blocks(pool, edges0)

            for c in range(NCH):
                pool.wait_ge(part_in[c % 2], 64 * (c // 2 + 1))
                nc.gpsimd.tensor_tensor(parts[c % 2][:, 2, :, :], parts[c % 2][:, 2, :, :],
                                        parts[c % 2][:, 3, :, :], ALU.add).then_inc(part_sum, 1)

            def gather1(b, half, j):
                pool.wait_ge(edge_in1[j], 80 * (half + 1))
                if not (isinstance(b, int) and b < 2):
                    pool.wait_ge(terms1_step, 4 * (b - 1))
                settle(pool)
                for t in range(T):
                    pool.indirect_dma_start(
                        out=ends1[j][:, t, :], out_offset=None, in_=src_table,
                        in_offset=bass.IndirectOffsetOnAxis(ap=src_sb[j][:, t:t + 1], axis=0)).then_inc(gathered1[j], 16)

            def scatter1(b, half, j):
                pool.wait_ge(dup_step1, 4 * b + 4)
                pool.wait_ge(summed1_ready, b + 1)
                for t in range(T):
                    wait(pool, scattered1[t], 16 * b)
                    settle(pool)
                    pool.indirect_dma_start(
                        out=sums1[t], out_offset=bass.IndirectOffsetOnAxis(ap=target[j][:, t:t + 1], axis=0),
                        in_=summed1[j][:, t, :], in_offset=None, compute_op=ALU.add).then_inc(scattered1[t], 16)

            def edges1(b, half, j):
                if not is_last_two(b):
                    gather1(b + 2, half + 1, j)
                scatter1(b, half, j)

            pool.wait_ge(tables, 48)
            gather1(0, 0, 0)
            gather1(1, 0, 1)
            blocks(pool, edges1)

            for c in range(NCH):
                pool.wait_ge(part_in1[c % 2], 64 * (c // 2 + 1))
                nc.gpsimd.tensor_tensor(parts[c % 2][:, 2, :, 0:W1], parts[c % 2][:, 2, :, 0:W1],
                                        parts[c % 2][:, 3, :, 0:W1], ALU.add).then_inc(part_sum1, 1)

        @block.scalar
        def _(act):
            act.wait_ge(zeros_set, 1)
            for t in range(T):
                flat = sums0[t].rearrange("(p a) w -> p (a w)", p=P)
                for k in range(5):
                    act.dma_start(flat[:, k * ZW:(k + 1) * ZW], zeros[:, :]).then_inc(zeroed, 16)
                act.dma_start(sums1[t].rearrange("(p a) w -> p a w", p=P),
                              zeros[:, 0:W1].unsqueeze(1).broadcast_to([P, ROWS // P, W1])).then_inc(zeroed, 16)
            act.wait_ge(sqrt_in, 1)
            nc.scalar.activation(stat[:, 2, :], stat[:, 1, :], ACT.Sqrt).then_inc(sqrt_out, 1)
            act.wait_ge(step, STEPS_TABLE0)
            act.dma_start(nodes(row_table), table_sb[:, :, 0:D]).then_inc(tables, 16)
            act.dma_start(nodes(col_table), table_sb[:, :, :]).then_inc(tables, 16)

            def scale_chunk(b, k):
                act.wait_ge(hidden_done, NK * b + k + 1)
                wait(act, hidden_ready, NK * b + k + 1 - NL)
                nc.scalar.activation(scaled[k % NL][:, :], ps_hidden[k % NL][:, :], ACT.Copy,
                                     scale=SLOPE).then_inc(scaled_ready, 1)

            def scale_beta(b, half):
                act.wait_ge(second_done, NK * b + NK)
                wait(act, beta_ready, 2 * (b - 1) + half + 1)
                nc.scalar.activation(beta_scaled[:, half * B:(half + 1) * B], ps_beta[half][:, :], ACT.Copy,
                                     scale=SLOPE).then_inc(beta_scaled_ready, 1)

            def copy_sum(b, t):
                act.wait_ge(summed, 4 * b + t + 1)
                wait(act, scattered[t], 16 * b)
                nc.scalar.activation(summed0[t][:, :], ps_sum[:, 0:W0], ACT.Copy).then_inc(summed_ready, 1)

            def edges0(b, half, j):
                begun = not (isinstance(b, int) and b == 0)
                if begun:
                    scale_beta(b - 1, 0)
                scale_chunk(b, 0)
                if begun:
                    scale_beta(b - 1, 1)
                scale_chunk(b, 1)
                scale_chunk(b, 2)
                scale_chunk(b, 3)
                act.wait_ge(second_done, NK * b + 2)
                wait(act, alpha_ready, b)
                nc.scalar.activation(alpha_scaled[:, :], ps_alpha[:, 0:T * H], ACT.Copy,
                                     scale=SLOPE).then_inc(alpha_scaled_ready, 1)
                if begun:
                    copy_sum(b - 1, 0)
                act.wait_ge(alpha_ready, b + 1)
                wait(act, weight_ready, b)
                nc.scalar.activation(alpha_exp[:, :, :].rearrange("p t h -> p (t h)"), alpha[:, :],
                                     ACT.Exp).then_inc(exp_ready, 1)
                scale_chunk(b, 4)
                if begun:
                    copy_sum(b - 1, 1)
                scale_chunk(b, 5)
                if begun:
                    copy_sum(b - 1, 2)
                    copy_sum(b - 1, 3)

            blocks(act, edges0)
            scale_beta(NB - 1, 0)
            scale_beta(NB - 1, 1)
            for t in range(T):
                copy_sum(NB - 1, t)

            act.wait_ge(sqrt_in, 2)
            nc.scalar.activation(stat[:, 2, :], stat[:, 1, :], ACT.Sqrt).then_inc(sqrt_out, 1)
            act.wait_ge(step, STEPS_TABLE1)
            act.dma_start(nodes(src_table), table_sb[:, :, :]).then_inc(tables, 16)

            def copy_sum1(b, j):
                act.wait_ge(summed1_done, b + 1)
                if not (isinstance(b, int) and b < 2):
                    for t in range(T):
                        act.wait_ge(scattered1[t], 16 * (b - 1))
                nc.scalar.activation(summed1[j][:, :, :].rearrange("p t w -> p (t w)"), ps_beta[j][:, :],
                                     ACT.Copy).then_inc(summed1_ready, 1)

            def edges1(b, half, j):
                act.wait_ge(dot_step, 4 * b + 4)
                wait(act, terms1_step, 4 * b)
                nc.scalar.activation(gates[:, :, :].rearrange("p a t -> p (a t)"),
                                     dots[:, :, :].rearrange("p a t -> p (a t)"), ACT.Sigmoid).then_inc(gates_ready, 1)
                if not (isinstance(b, int) and b == 0):
                    copy_sum1(b - 1, 1 - j)

            blocks(act, edges1)
            copy_sum1(NB - 1, 1)

            for c in range(NCH):
                act.wait_ge(feat_T_done, c + 1)
                wait(act, review_done, c)
                nc.scalar.activation(feat_T[:, 0:4, :].rearrange("d t p -> d (t p)"), ps_hidden[0][0:D, :],
                                     ACT.Copy).then_inc(feat_T_ready, 1)
                nc.scalar.activation(feat_T[:, 4:CH, :].rearrange("d t p -> d (t p)"), ps_hidden[1][0:D, 0:(CH - 4) * P],
                                     ACT.Copy).then_inc(feat_T_ready, 1)

        @block.vector
        def _(dve):
            def link(ins):
                LAYER0_STEPS[0] += 1
                ins.then_inc(step, 1)
                dve.wait_ge(step, LAYER0_STEPS[0])

            nc.vector.memset(zeros[:, :], 0.0).then_inc(zeros_set, 1)
            nc.vector.memset(gate_w2_sb[:, :, :], 0.0).then_inc(weights_set, 1)
            for j in range(2):
                link(nc.vector.memset(terms0[j][:, :, W0 - 1:W0], 1.0))

            def norm(n):
                def wide(k):
                    return stat[:, k, :].unsqueeze(2).broadcast_to([P, NT, D])
                link(nc.vector.tensor_reduce(out=stat[:, 0, :], in_=x_sb[:, :, :], axis=AX.X, op=ALU.add))
                link(nc.vector.tensor_scalar(stat[:, 0, :], stat[:, 0, :], 1.0 / D, None, ALU.mult))
                link(nc.vector.tensor_tensor(centered[:, :, :], x_sb[:, :, :], wide(0), ALU.subtract))
                link(nc.vector.tensor_tensor(squares[:, :, :], centered[:, :, :], centered[:, :, :], ALU.mult))
                link(nc.vector.tensor_reduce(out=stat[:, 1, :], in_=squares[:, :, :], axis=AX.X, op=ALU.add))
                nc.vector.tensor_scalar(stat[:, 1, :], stat[:, 1, :], 1.0 / D, EPS, ALU.mult, ALU.add).then_inc(sqrt_in, 1)
                dve.wait_ge(sqrt_out, n)
                link(nc.vector.reciprocal(stat[:, 3, :], stat[:, 2, :]))
                link(nc.vector.tensor_tensor(centered[:, :, :], centered[:, :, :], wide(3), ALU.mult))
                link(nc.vector.tensor_scalar(centered[:, :, :], centered[:, :, :], 0.0, None, ALU.max))

            dve.wait_ge(loaded, 16 * 13)
            norm(1)
            link(nc.vector.tensor_copy(table_sb[:, :, 0:D], centered[:, :, :]))
            link(nc.vector.tensor_copy(table_sb[:, :, D:D + 1], pos_sb[:, :].unsqueeze(2)))
            assert LAYER0_STEPS[0] == STEPS_TABLE0
            dve.wait_ge(made, 5)

            def find_targets(b, j, keys, here, before_equal, before_target):
                before_equal()
                nc.vector.tensor_tensor(equal[j][:, :, :], key_rows[j][:, :, :],
                                        keys[j][:, :].unsqueeze(2).broadcast_to([P, T, P]),
                                        ALU.is_equal).then_inc(here, 1)
                dve.wait_ge(here, 4 * b + 1)
                nc.vector.tensor_tensor(earlier[:, :, :], equal[j][:, :, :],
                                        before[:, :].unsqueeze(1).broadcast_to([P, T, P]), ALU.mult).then_inc(here, 1)
                dve.wait_ge(here, 4 * b + 2)
                nc.vector.tensor_reduce(out=earlier_max[:, :], in_=earlier[:, :, :], axis=AX.X,
                                        op=ALU.max).then_inc(here, 1)
                dve.wait_ge(here, 4 * b + 3)
                before_target()
                nc.vector.tensor_tensor(target[j][:, :], earlier_max[:, :], keys[j][:, :], ALU.max).then_inc(here, 1)

            def turn_ends(b, j):
                dve.wait_ge(transposed, b + 1)
                wait(dve, hidden_done, NK * (b - 1))
                nc.vector.tensor_copy(ends_T[j][:, :], ps_T[:, :]).then_inc(ends_ready, 1)

            def rectify_chunk(b, k):
                dve.wait_ge(scaled_ready, NK * b + k + 1)
                if not (isinstance(b, int) and b == 0):
                    dve.wait_ge(second_done, NK * (b - 1) + k + 1)
                nc.vector.tensor_tensor(hidden[k][:, :], scaled[k % NL][:, :], ps_hidden[k % NL][:, :],
                                        ALU.max).then_inc(hidden_ready, 1)

            def rectify_beta(b, half):
                dve.wait_ge(beta_scaled_ready, 2 * b + half + 1)
                wait(dve, terms_ready, b)
                nc.vector.tensor_tensor(beta[:, :, :, :].rearrange("p t h d -> p (t h d)")[:, half * B:(half + 1) * B],
                                        beta_scaled[:, half * B:(half + 1) * B], ps_beta[half][:, :],
                                        ALU.max).then_inc(beta_ready, 1)

            def weigh_beta(b, j):
                dve.wait_ge(beta_ready, 2 * b + 2)
                dve.wait_ge(weight_ready, b + 1)
                for t in range(T):
                    last = nc.vector.tensor_tensor(
                        terms0[j][:, t, 0:H * D].rearrange("p (h d) -> p h d", h=H), beta[:, t, :, :],
                        terms0[j][:, t, H * D:H * D + H].unsqueeze(2).broadcast_to([P, H, D]), ALU.mult)
                    if t == T - 1:
                        last.then_inc(terms_ready, 1)

            def targets0(b, j):
                def before_equal():
                    wait_in(b, j)
                    if not (isinstance(b, int) and b < 2):
                        dve.wait_ge(summed, 4 * (b - 1))
                def before_target():
                    if not (isinstance(b, int) and b < 2):
                        for t in range(T):
                            dve.wait_ge(scattered[t], 16 * (b - 1))
                find_targets(b, j, src_sb, dup_step, before_equal, before_target)

            halves = {}

            def wait_in(b, j):
                dve.wait_ge(edge_in[j], 48 * (halves["half"] + 1))

            def edges0(b, half, j):
                halves["half"] = half
                begun = not (isinstance(b, int) and b == 0)
                if begun:
                    rectify_beta(b - 1, 0)
                rectify_chunk(b, 0)
                if begun:
                    rectify_beta(b - 1, 1)
                rectify_chunk(b, 1)
                if begun:
                    weigh_beta(b - 1, 1 - j)
                rectify_chunk(b, 2)
                rectify_chunk(b, 3)
                dve.wait_ge(alpha_scaled_ready, b + 1)
                wait(dve, exp_ready, b)
                nc.vector.tensor_tensor(alpha[:, :], alpha_scaled[:, :], ps_alpha[:, 0:T * H],
                                        ALU.max).then_inc(alpha_ready, 1)
                targets0(b, j)
                rectify_chunk(b, 4)
                dve.wait_ge(exp_ready, b + 1)
                if not (isinstance(b, int) and b < 2):
                    dve.wait_ge(summed, 4 * (b - 1))
                nc.vector.tensor_tensor(terms0[j][:, :, H * D:H * D + H], alpha_exp[:, :, :],
                                        ends[j][:, :, 2 * D:2 * D + 1].broadcast_to([P, T, H]),
                                        ALU.mult).then_inc(weight_ready, 1)
                rectify_chunk(b, 5)
                if not is_last(b):
                    turn_ends(b + 1, 1 - j)

            turn_ends(0, 0)
            blocks(dve, edges0)
            rectify_beta(NB - 1, 0)
            rectify_beta(NB - 1, 1)
            weigh_beta(NB - 1, 1)

            for c in range(NCH):
                q = parts[c % 2]
                dve.wait_ge(part_in[c % 2], 64 * (c // 2 + 1))
                link(nc.vector.tensor_tensor(q[:, 0, :, :], q[:, 0, :, :], q[:, 1, :, :], ALU.add))
                dve.wait_ge(part_sum, c + 1)
                link(nc.vector.tensor_tensor(q[:, 0, :, :], q[:, 0, :, :], q[:, 2, :, :], ALU.add))
                link(nc.vector.tensor_scalar(empty[:, :].unsqueeze(2), q[:, 0, :, W0 - 1:W0], 0.0, None, ALU.is_equal))
                link(nc.vector.tensor_tensor(inverse[:, :, :], q[:, 0, :, H * D:H * D + H],
                                             empty[:, :].unsqueeze(2).broadcast_to([P, CH, H]), ALU.add))
                link(nc.vector.reciprocal(inverse[:, :, :], inverse[:, :, :]))
                link(nc.vector.tensor_scalar(inverse[:, :, :], inverse[:, :, :], 1e-16, 1.0 / H, ALU.add, ALU.mult))
                for t in range(CH):
                    last = nc.vector.tensor_tensor(q[:, 1, t, 0:H * D].rearrange("p (h d) -> p h d", h=H),
                                                   q[:, 0, t, 0:H * D].rearrange("p (h d) -> p h d", h=H),
                                                   inverse[:, t, :].unsqueeze(2).broadcast_to([P, H, D]), ALU.mult)
                link(last)
                for t in range(CH):
                    last = nc.vector.tensor_reduce(out=mean[:, t, :], in_=q[:, 1, t, 0:H * D].rearrange("p (h d) -> p d h", h=H),
                                                   axis=AX.X, op=ALU.add)
                last.then_inc(part_free, 1)
                dve.wait_ge(part_free, c + 1)
                link(nc.vector.tensor_tensor(x_sb[:, c * CH:(c + 1) * CH, :], x_sb[:, c * CH:(c + 1) * CH, :],
                                             mean[:, :, :], ALU.add))
            norm(2)
            link(nc.vector.tensor_tensor(table_sb[:, :, 0:D], centered[:, :, :],
                                         cj_sb[:, :].unsqueeze(2).broadcast_to([P, NT, D]), ALU.mult))
            link(nc.vector.tensor_copy(table_sb[:, :, D:D + 1], cj_sb[:, :].unsqueeze(2)))
            assert LAYER0_STEPS[0] == STEPS_TABLE1

            def edges1(b, half, j):
                def before_equal():
                    dve.wait_ge(edge_in1[j], 80 * (half + 1))
                    if not (isinstance(b, int) and b < 2):
                        dve.wait_ge(summed1_done, b - 1)
                    elif b < 2:
                        dve.wait_ge(summed, 4 * NB)
                def before_target():
                    for t in range(T):
                        if isinstance(b, int) and b < 2:
                            dve.wait_ge(scattered[t], 16 * NB)
                        else:
                            dve.wait_ge(scattered1[t], 16 * (b - 1))
                dve.wait_ge(edge_in1[j], 80 * (half + 1))
                wait(dve, dot_step, 4 * b)
                for a in range(2):
                    nc.vector.tensor_tensor(products[:, a, :, :], feat[j][:, :, :],
                                            dots_w[:, a, :].unsqueeze(1).broadcast_to([P, T, D]),
                                            ALU.mult).then_inc(dot_step, 1)
                wait(dve, gates_ready, b)
                for a in range(2):
                    dve.wait_ge(dot_step, 4 * b + 1 + a)
                    nc.vector.tensor_reduce(out=dots[:, a, :], in_=products[:, a, :, :], axis=AX.X,
                                            op=ALU.add).then_inc(dot_step, 1)
                find_targets(b, j, dst_sb, dup_step1, before_equal, before_target)
                dve.wait_ge(gates_ready, b + 1)
                nc.vector.tensor_tensor(feat_gate[:, :], gates[:, 1, :], attn[j][:, :], ALU.mult).then_inc(terms1_step, 1)
                dve.wait_ge(gathered1[j], 64 * (half + 1))
                if not (isinstance(b, int) and b < 2):
                    dve.wait_ge(summed1_done, b - 1)
                nc.vector.tensor_tensor(terms1[j][:, :, 0:D], ends1[j][:, :, 0:D],
                                        gates[:, 0, :].unsqueeze(2).broadcast_to([P, T, D]), ALU.mult).then_inc(terms1_step, 1)
                dve.wait_ge(terms1_step, 4 * b + 2)
                nc.vector.tensor_tensor(feat_gate[:, :].unsqueeze(2), feat_gate[:, :].unsqueeze(2),
                                        ends1[j][:, :, D:D + 1], ALU.mult).then_inc(terms1_step, 1)
                dve.wait_ge(terms1_step, 4 * b + 3)
                nc.vector.tensor_tensor(terms1[j][:, :, D:W1], feat[j][:, :, :],
                                        feat_gate[:, :].unsqueeze(2).broadcast_to([P, T, D]), ALU.mult).then_inc(terms1_step, 1)

            blocks(dve, edges1)

            for c in range(NCH):
                q = parts[c % 2]
                dve.wait_ge(part_in1[c % 2], 64 * (c // 2 + 1))
                link(nc.vector.tensor_tensor(q[:, 0, :, 0:W1], q[:, 0, :, 0:W1], q[:, 1, :, 0:W1], ALU.add))
                dve.wait_ge(part_sum1, c + 1)
                link(nc.vector.tensor_tensor(q[:, 0, :, 0:W1], q[:, 0, :, 0:W1], q[:, 2, :, 0:W1], ALU.add))
                dve.wait_ge(review_done, c + 1)
                link(nc.vector.tensor_tensor(mean[:, :, :], q[:, 0, :, 0:D],
                                             ps_sum[:, 0:CH * D].rearrange("p (t d) -> p t d", t=CH), ALU.add))
                nc.vector.tensor_tensor(mean[:, :, :], mean[:, :, :],
                                        ci_sb[:, c * CH:(c + 1) * CH].unsqueeze(2).broadcast_to([P, CH, D]),
                                        ALU.mult).then_inc(part_free, 1)
                dve.wait_ge(part_free, NCH + c + 1)
                nc.vector.tensor_tensor(x_sb[:, c * CH:(c + 1) * CH, :], x_sb[:, c * CH:(c + 1) * CH, :],
                                        mean[:, :, :], ALU.add).then_inc(chunk_out, 1)

        @block.tensor
        def _(pe):
            def transpose_ends(b, half, j):
                pe.wait_ge(gathered[j], 128 * (half + 1))
                wait(pe, ends_ready, b)
                for t in range(T):
                    last = nc.tensor.transpose(ps_T[:, t * P:(t + 1) * P], ends[j][:, t, 0:2 * D], ident[:, :])
                last.then_inc(transposed, 1)

            def first_product(b, k, j):
                if k == 0:
                    pe.wait_ge(ends_ready, b + 1)
                wait(pe, hidden_ready, NK * b + k + 1 - NL)
                nc.tensor.matmul(ps_hidden[k % NL][:, :], w1_sb[:, k * P:(k + 1) * P], ends_T[j][:, :],
                                 start=True, stop=True).then_inc(hidden_done, 1)

            def second_product(b, k):
                pe.wait_ge(hidden_ready, NK * b + k + 1)
                if k == 0:
                    wait(pe, alpha_ready, b)
                if k == 2:
                    wait(pe, beta_ready, 2 * b)
                for t in range(T):
                    if k < 2:
                        o, w = ps_alpha[:, t * H + 2 * k:t * H + 2 * k + 2], gate_w2_sb[:, k, :]
                    else:
                        at = (t % 2) * H * D + (k - 2) * D
                        o, w = ps_beta[t // 2][:, at:at + D], msg_w2_sb[:, k - 2, :]
                    last = nc.tensor.matmul(o, hidden[k][:, t * P:(t + 1) * P], w, start=True, stop=True)
                last.then_inc(second_done, 1)

            def sum_tile(b, t, j):
                if t == 0:
                    pe.wait_ge(terms_ready, b + 1)
                    pe.wait_ge(dup_step, 4 * b + 1)
                wait(pe, summed_ready, 4 * b + t)
                nc.tensor.matmul(ps_sum[:, 0:W0], equal[j][:, t, :], terms0[j][:, t, :],
                                 start=True, stop=True).then_inc(summed, 1)

            def edges0(b, half, j):
                begun = not (isinstance(b, int) and b == 0)
                first_product(b, 0, j)
                first_product(b, 1, j)
                first_product(b, 2, j)
                second_product(b, 0)
                first_product(b, 3, j)
                second_product(b, 1)
                if begun:
                    sum_tile(b - 1, 0, 1 - j)
                first_product(b, 4, j)
                second_product(b, 2)
                if begun:
                    sum_tile(b - 1, 1, 1 - j)
                first_product(b, 5, j)
                second_product(b, 3)
                if begun:
                    sum_tile(b - 1, 2, 1 - j)
                if not is_last(b):
                    transpose_ends(b + 1, half + j, 1 - j)
                second_product(b, 4)
                if begun:
                    sum_tile(b - 1, 3, 1 - j)
                second_product(b, 5)

            pe.wait_ge(made, 5)
            pe.wait_ge(loaded, 16 * 13)
            transpose_ends(0, 0, 0)
            blocks(pe, edges0)
            for t in range(T):
                sum_tile(NB - 1, t, 1)

            def edges1(b, half, j):
                pe.wait_ge(terms1_step, 4 * b + 4)
                pe.wait_ge(dup_step1, 4 * b + 1)
                if isinstance(b, int) and b < 2:
                    pe.wait_ge(beta_ready, 2 * NB)
                else:
                    pe.wait_ge(summed1_ready, b - 1)
                for t in range(T):
                    last = nc.tensor.matmul(ps_beta[j][:, t * W1:(t + 1) * W1], equal[j][:, t, :], terms1[j][:, t, :],
                                            start=True, stop=True)
                last.then_inc(summed1_done, 1)

            blocks(pe, edges1)

            for c in range(NCH):
                pe.wait_ge(step, STEPS_SUMS1 + 3 * c)
                wait(pe, feat_T_ready, 2 * c)
                for t in range(CH):
                    last = nc.tensor.transpose(ps_hidden[t // 4][0:D, (t % 4) * P:(t % 4 + 1) * P],
                                               parts[c % 2][:, 0, t, D:W1], ident[:, :])
                last.then_inc(feat_T_done, 1)
                pe.wait_ge(feat_T_ready, 2 * c + 2)
                wait(pe, step, STEPS_SUMS1 + 3 * c - 2 if c else 0)
                for t in range(CH):
                    last = nc.tensor.matmul(ps_sum[:, t * D:(t + 1) * D], feat_T[:, t, :], review_w_sb[:, :],
                                            start=True, stop=True)
                last.then_inc(review_done, 1)


NORM_STEPS = 8
STEPS_TABLE0 = 2 + NORM_STEPS + 2
STEPS_TABLE1 = STEPS_TABLE0 + 8 * NCH + NORM_STEPS + 2
STEPS_SUMS1 = STEPS_TABLE1 + 2


def kernel(x, src, dst, edge_attr_64, edge_weight, node_vec, node_vec1, node_vec1_n2, L0_gnn_gate_w1,
           L0_gnn_gate_w2, L0_gnn_msg_w1, L0_gnn_msg_w2, L1_gnn_prob_w, L1_gnn_review_score_w, L1_gnn_review_w):
    import concourse.bacc as bacc
    from concourse.bass_utils import run_bass_kernel_spmd

    def padded(a, n, value=0):
        a = np.asarray(a)
        return np.concatenate([a, np.full((n - a.shape[0],) + a.shape[1:], value, a.dtype)])

    src, dst = padded(src, EP, N), padded(dst, EP, N)
    first = np.concatenate([np.asarray(L0_gnn_gate_w1).reshape(2 * P, P), np.asarray(L0_gnn_msg_w1).reshape(4 * P, P)])
    arrays = {
        "x": padded(x, NP),
        "src": src.reshape(NB, P, T), "dst": dst.reshape(NB, P, T),
        "src_rows": src.reshape(NB, P, T).transpose(0, 2, 1), "dst_rows": dst.reshape(NB, P, T).transpose(0, 2, 1),
        "edge_attr": padded(edge_attr_64, EP).reshape(NB, P, T, D),
        "edge_weight": padded(edge_weight, EP).reshape(NB, P, T),
        "node_vec": padded(node_vec, NP, 1).reshape(P, NT),
        "node_vec1": padded(node_vec1, NP).reshape(P, NT),
        "node_vec1_n2": padded(node_vec1_n2, NP).reshape(P, NT),
        "w1": first.T,
        "gate_w2": np.asarray(L0_gnn_gate_w2).reshape(H, D, 1),
        "msg_w2": np.asarray(L0_gnn_msg_w2).transpose(2, 0, 1),
        "prob_w": np.asarray(L1_gnn_prob_w), "score_w": np.asarray(L1_gnn_review_score_w),
        "review_w": np.asarray(L1_gnn_review_w).T,
    }
    arrays = {f"in_{k}": np.ascontiguousarray(a) for k, a in arrays.items()}
    nc = bacc.Bacc("TRN2", target_bir_lowering=False, num_devices=1)
    args = [nc.dram_tensor(k, a.shape, mybir.dt.from_np(a.dtype), kind="ExternalInput").ap() for k, a in arrays.items()]
    out = nc.dram_tensor("out", (NP, D), F32, kind="ExternalOutput").ap()
    gnn(nc, *args, out)
    r = run_bass_kernel_spmd(nc, [arrays], core_ids=[0])
    return r.results[0]["out"][:N]
```

```python
import concourse.bass as bass
import numpy as np
from concourse import mybir
from contextlib import ExitStack

F32, F32R, I32 = mybir.dt.float32, mybir.dt.float32r, mybir.dt.int32
ALU = mybir.AluOpType
ACT = mybir.ActivationFunctionType
AX = mybir.AxisListType

P = 128
N = 6250
D = 64
E = 206250
H = 4
NT = -(-N // P)
NP = NT * P
ROWS = NP + P
T = 4
B = T * P
NB = 4 * -(-E // (4 * B))
WIN0 = 32
WIN = 128
EP = NB * B
W0 = H * D + H + 1
W1 = 2 * D
NK = 6
NL = 3
CH = 7
NCH = NT // CH
SLOPE = 0.2
EPS = 1e-5
ZW = ROWS * W0 // P // 5
HID = NK * P
WT = HID + 4
assert NT % CH == 0 and NB >= 12 and ROWS * W0 % (P * 5) == 0


def gnn(nc, x, src, dst, src_rows, dst_rows, dst_all, edge_attr, edge_weight, node_vec, node_vec1, node_vec1_n2,
        w1, gate_w2, msg_w2, prob_w, score_w, review_w, out):
    ctx = ExitStack()
    with ctx:
        def sb(name, shape, dt=F32):
            return ctx.enter_context(nc.sbuf_tensor(name, shape, dt))

        def pb(name, shape):
            return ctx.enter_context(nc.psum_tensor(name, shape, F32))

        def sem(name):
            return ctx.enter_context(nc.semaphore(name))

        def dram(name, shape):
            return nc.dram_tensor(name, shape, F32, kind="Internal").ap()

        row_table = dram("row_table", [NP, D])
        twice_table = dram("twice_table", [NP, 2 * D])
        col_table = dram("col_table", [NP, D + 1])
        src_table = dram("src_table", [NP, D + 1])
        window_table = dram("window_table", [ROWS, 2, WT])
        sums0 = [dram(f"sums0_{t}", [ROWS, W0]) for t in range(T)]
        sums1 = [dram(f"sums1_{t}", [ROWS, W1]) for t in range(T)]

        parts = [sb(f"parts{j}", [P, T, CH, W0]) for j in range(2)]
        squares = parts[0][:, :, :, :].rearrange("p a t w -> p (a t w)")[:, 0:NT * D].rearrange("p (t d) -> p t d", d=D)
        zeros = parts[1][:, :, :, :].rearrange("p a t w -> p (a t w)")[:, 0:ZW]
        x_sb = sb("x_sb", [P, NT, D])
        centered = sb("centered", [P, NT, D])
        table_sb = sb("table_sb", [P, NT, D + 1])
        stat = sb("stat", [P, 4, NT])
        pos_sb = sb("pos_sb", [P, NT])
        cj_sb = sb("cj_sb", [P, NT])
        ci_sb = sb("ci_sb", [P, NT])
        node_sb = sb("node_sb", [P, NT])
        ident = sb("ident", [P, P])
        spare = sb("spare", [P, 1])
        before = sb("before", [P, P])
        w1_sb = sb("w1_sb", [P, NK * P])
        gate_w2_sb = sb("gate_w2_sb", [P, 2, 2])
        msg_w2_sb = sb("msg_w2_sb", [P, H, D])
        dots_w = sb("dots_w", [P, 2, D])
        review_w_sb = sb("review_w_sb", [D, D])
        dst_all_sb = parts[1][:, :, :, :].rearrange("p a t w -> p (a t w)")[:, ZW:ZW + NB * T].bitcast(I32)
        offset0 = parts[1][:, :, :, :].rearrange("p a t w -> p (a t w)")[:, ZW + NB * T:ZW + 2 * NB * T]
        first_node = sb("first_node", [1, NB], I32)
        first_dst = sb("first_dst", [1, NB])
        offset = sb("offset", [P, NB * T])
        reach = sb("reach", [P, 8])
        fits_sb = sb("fits_sb", [1, 1], I32)
        ones = sb("ones", [1, P])
        w1_dst = sb("w1_dst", [D, HID])
        columns = sb("columns", [P, WIN])
        h_T = [sb(f"h_T{j}", [D, P]) for j in range(2)]
        table_row = [parts[0][:, :, :, :].rearrange("p a t w -> p (a t w)")[:, 2 * j * WT:2 * (j + 1) * WT]
                     .rearrange("p (a w) -> p a w", a=2).bitcast(F32R) for j in range(2)]
        tails = sb("tails", [P, NT, 2, 4])
        pos_high = sb("pos_high", [P, NT], F32R)
        w1_src = sb("w1_src", [P, HID])
        w1_split = sb("w1_split", [P, HID], F32R)
        window = [sb(f"window{j}", [P, WT], F32R) for j in range(2)]
        src_sb = [sb(f"src_sb{j}", [P, T], I32) for j in range(2)]
        gather_sb = [sb(f"gather_sb{j}", [P, T], I32) for j in range(2)]
        dst_sb = [sb(f"dst_sb{j}", [P, T], I32) for j in range(2)]
        key_rows = [sb(f"key_rows{j}", [P, T, P], I32) for j in range(2)]
        equal = [sb(f"equal{j}", [P, T, P]) for j in range(2)]
        earlier = sb("earlier", [P, T, P])
        earlier_max = sb("earlier_max", [P, T])
        target = [sb(f"target{j}", [P, T], I32) for j in range(2)]
        ends = [sb(f"ends{j}", [P, T, W1 + 1]) for j in range(2)]
        ends_T = [sb(f"ends_T{j}", [P, B]) for j in range(2)]
        ends_high = [sb(f"ends_high{j}", [P, B], F32R) for j in range(2)]
        ends_low = [sb(f"ends_low{j}", [P, B], F32R) for j in range(2)]
        dst_rows_sb = [sb(f"dst_rows_sb{j}", [P, T, P], I32) for j in range(2)]
        scaled = [sb(f"scaled{j}", [P, B]) for j in range(NL)]
        hidden = [sb(f"hidden{k}", [P, B]) for k in range(NK)]
        alpha_scaled = sb("alpha_scaled", [P, T * H])
        alpha = sb("alpha", [P, T * H])
        alpha_exp = sb("alpha_exp", [P, T, H])
        beta_scaled = sb("beta_scaled", [P, T * H * D])
        beta = sb("beta", [P, T, H, D])
        terms0 = [sb(f"terms0_{j}", [P, T, W0]) for j in range(2)]
        summed0 = [sb(f"summed0_{t}", [P, W0]) for t in range(T)]
        feat = [sb(f"feat{j}", [P, T, D]) for j in range(2)]
        attn = [sb(f"attn{j}", [P, T]) for j in range(2)]
        ends1 = [sb(f"ends1_{j}", [P, T, D + 1]) for j in range(2)]
        products = hidden[4][:, :].rearrange("p (a t d) -> p a t d", a=2, d=D)
        dots = sb("dots", [P, 2, T])
        gates = sb("gates", [P, 2, T])
        feat_gate = sb("feat_gate", [P, T])
        terms1 = [hidden[j][:, :].rearrange("p (t w) -> p t w", w=W1) for j in range(2)]
        summed1 = [hidden[2 + j][:, :].rearrange("p (t w) -> p t w", w=W1) for j in range(2)]
        ends1_windows = ends1 + [ends[j][:, :, 0:D + 1] for j in range(2)]
        feat_windows = feat + [ends_T[j][:, 0:T * D].rearrange("p (t d) -> p t d", d=D) for j in range(2)]
        terms1_windows = [hidden[m][:, :].rearrange("p (t w) -> p t w", w=W1) for m in range(4)]
        attn_windows = attn + [sb(f"attn{j}", [P, T]) for j in range(2, 4)]
        src_windows = src_sb + gather_sb
        hot = equal
        window_sum = sb("window_sum", [WIN, W1])
        inverse = sb("inverse", [P, CH, H])
        empty = sb("empty", [P, CH])
        mean = beta_scaled[:, 0:CH * D].rearrange("p (t d) -> p t d", d=D)
        feat_T = beta[0:D, :, :, :].rearrange("p t h d -> p (t h d)")[:, 0:CH * P].rearrange("d (t p) -> d t p", p=P)

        ps_T = pb("ps_T", [P, B])
        ps_hidden = [pb(f"ps_hidden{j}", [P, B]) for j in range(NL)]
        ps_beta = [pb(f"ps_beta{j}", [P, B]) for j in range(2)]
        ps_alpha = pb("ps_alpha", [P, B])
        ps_sum = pb("ps_sum", [P, B])

        loaded = sem("loaded")
        made = sem("made")
        zeroed = sem("zeroed")
        zeros_set = sem("zeros_set")
        weights_set = sem("weights_set")
        step = sem("step")
        sqrt_in = sem("sqrt_in")
        sqrt_out = sem("sqrt_out")
        tables = sem("tables")
        edge_in = [sem(f"edge_in{j}") for j in range(2)]
        gather_in = [sem(f"gather_in{j}") for j in range(2)]
        gathered = [sem(f"gathered{j}") for j in range(2)]
        transposed = sem("transposed")
        ends_ready = sem("ends_ready")
        hidden_done = sem("hidden_done")
        scaled_ready = sem("scaled_ready")
        hidden_ready = sem("hidden_ready")
        second_done = sem("second_done")
        alpha_scaled_ready = sem("alpha_scaled_ready")
        alpha_ready = sem("alpha_ready")
        exp_ready = sem("exp_ready")
        weight_ready = sem("weight_ready")
        beta_scaled_ready = sem("beta_scaled_ready")
        beta_ready = sem("beta_ready")
        terms_ready = sem("terms_ready")
        dup_step = sem("dup_step")
        summed = sem("summed")
        summed_ready = sem("summed_ready")
        scattered = [sem(f"scattered{t}") for t in range(T)]
        part_in = [sem(f"part_in{j}") for j in range(2)]
        part_sum = sem("part_sum")
        part_free = sem("part_free")
        edge_in1 = [sem(f"edge_in1_{j}") for j in range(2)]
        gathered1 = [sem(f"gathered1_{j}") for j in range(2)]
        dot_step = sem("dot_step")
        gates_ready = sem("gates_ready")
        terms1_step = sem("terms1_step")
        dup_step1 = sem("dup_step1")
        summed1_done = sem("summed1_done")
        summed1_ready = sem("summed1_ready")
        scattered1 = [sem(f"scattered1_{t}") for t in range(T)]
        part_in1 = [sem(f"part_in1_{j}") for j in range(2)]
        part_sum1 = sem("part_sum1")
        copies_added = sem("copies_added")
        mean_step = sem("mean_step")
        feat_T_done = sem("feat_T_done")
        feat_T_ready = sem("feat_T_ready")
        review_done = sem("review_done")
        chunk_out = sem("chunk_out")
        stored = sem("stored")
        fits_step = sem("fits_step")
        firsts_ready = sem("firsts_ready")
        firsts_spread = sem("firsts_spread")
        reach_ready = sem("reach_ready")
        reach_turned = sem("reach_turned")
        fits_ready = sem("fits_ready")
        w_high_ready = sem("w_high_ready")
        w_low_ready = sem("w_low_ready")
        tail_step = sem("tail_step")
        h_turned = sem("h_turned")
        h_T_ready = sem("h_T_ready")
        projected = sem("projected")
        high_ready = sem("high_ready")
        low_ready = sem("low_ready")
        tail_ready = sem("tail_ready")
        row_out = [sem(f"row_out{j}") for j in range(2)]
        pads_out = sem("pads_out")
        window_in = [sem(f"window_in{j}") for j in range(2)]
        ends_high_ready = sem("ends_high_ready")
        ends_low_ready = sem("ends_low_ready")
        hot_T_ready = sem("hot_T_ready")
        hot_ready = sem("hot_ready")
        window_copied = sem("window_copied")
        edge_in1w = [sem(f"edge_in1w{m}") for m in range(4)]
        gathered1w = [sem(f"gathered1w{m}") for m in range(4)]
        window_added = sem("window_added")
        sums1_landed = sem("sums1_landed")
        settled = sem("settled")

        def wait(eng, s, value):
            if not (isinstance(value, int) and value <= 0):
                eng.wait_ge(s, value)

        def blocks(eng, body, tail=2):
            body(0, 0, 0)
            body(1, 0, 1)
            with eng.Fori(1, (NB - tail) // 2) as i:
                body(2 * i, i, 0)
                body(2 * i + 1, i, 1)
            for b in range(NB - tail, NB):
                body(b, b // 2, b % 2)

        def fours(eng, body):
            for m in range(4):
                body(m, 0, m)
            with eng.Fori(1, NB // 4 - 1) as i:
                for m in range(4):
                    body(4 * i + m, i, m)
            for m in range(4):
                body(NB - 4 + m, NB // 4 - 1, m)

        def early(b):
            return isinstance(b, int) and b < 2

        def first_four(b):
            return isinstance(b, int) and b < 4

        def is_last(b):
            return isinstance(b, int) and b == NB - 1

        def is_last_two(b):
            return isinstance(b, int) and b >= NB - 2

        def settle(eng):
            eng.sem_inc(settled, 1)

        def nodes(dram_ap):
            return dram_ap.rearrange("(p t) w -> p t w", p=P)

        def project_bank(t, k):
            return (ps_hidden if t % 2 == 0 else ps_beta)[k]

        def column_bank(t):
            return (ps_T, ps_alpha)[t % 2]

        LAYER0_STEPS = [0]
        LOADS = 13 + H

        def fits(eng):
            eng.wait_ge(fits_ready, 1)
            return eng.value_load(fits_sb[0:1, 0:1], min_val=0, max_val=1)

        def window_start(eng, b):
            return eng.value_load(first_node[0:1, bass.ds(b, 1)], min_val=0, max_val=N)

        block = ctx.enter_context(nc.Block())

        @block.sync
        def _(sp):
            sp.dma_start(x_sb[:, :, :], nodes(x)).then_inc(loaded, 16)
            sp.dma_start(pos_sb[:, :], node_vec).then_inc(loaded, 16)
            sp.dma_start(cj_sb[:, :], node_vec1).then_inc(loaded, 16)
            sp.dma_start(ci_sb[:, :], node_vec1_n2).then_inc(loaded, 16)
            sp.dma_start(w1_sb[:, :], w1).then_inc(loaded, 16)
            sp.dma_start(msg_w2_sb[:, :, :], msg_w2).then_inc(loaded, 16)
            sp.dma_start(dots_w[:, 0, :], prob_w.broadcast_to([P, D])).then_inc(loaded, 16)
            sp.dma_start(dots_w[:, 1, :], score_w.broadcast_to([P, D])).then_inc(loaded, 16)
            sp.dma_start(review_w_sb[:, :], review_w).then_inc(loaded, 16)
            sp.dma_start(w1_dst[:, :], w1[D:P, :]).then_inc(loaded, 16)
            sp.dma_start(dst_all_sb, dst_all).then_inc(loaded, 16)
            for a in range(2):
                sp.dma_start(w1_src[a * D:(a + 1) * D, :], w1[0:D, :]).then_inc(loaded, 16)
            sp.wait_ge(weights_set, 1)
            for h in range(H):
                sp.dma_start(gate_w2_sb[(h % 2) * D:(h % 2 + 1) * D, h // 2, h % 2:h % 2 + 1],
                             gate_w2[h]).then_inc(loaded, 16)

            def load0(b, half, j):
                if not (isinstance(b, int) and b < 2):
                    sp.wait_ge(dup_step, 4 * (b - 1))
                    settle(sp)
                    sp.wait_ge(gathered[j], 128 * half)
                    settle(sp)
                sp.dma_start(src_sb[j][:, :], src[bass.ds(b, 1)]).then_inc(edge_in[j], 16)
                sp.dma_start(dst_sb[j][:, :], dst[bass.ds(b, 1)]).then_inc(edge_in[j], 16)
                sp.dma_start(key_rows[j][:, :, :],
                             src_rows[bass.ds(b, 1)].broadcast_to([P, T, P])).then_inc(edge_in[j], 16)

            def load0_windows(b, half, j):
                if not early(b):
                    sp.wait_ge(dup_step, 4 * (b - 1))
                    settle(sp)
                    sp.wait_ge(hot_T_ready, b - 1)
                    settle(sp)
                sp.dma_start(src_sb[j][:, :], src[bass.ds(b, 1)]).then_inc(edge_in[j], 16)
                sp.dma_start(key_rows[j][:, :, :],
                             src_rows[bass.ds(b, 1)].broadcast_to([P, T, P])).then_inc(edge_in[j], 16)
                sp.dma_start(dst_rows_sb[j][D:P, :, :],
                             dst_rows[bass.ds(b, 1)].broadcast_to([P - D, T, P])).then_inc(edge_in[j], 16)
                if not early(b):
                    sp.wait_ge(hidden_done, NK * (b - 1))
                    settle(sp)
                first = window_start(sp, b)
                for a in range(2):
                    at = D + a * WIN0
                    sp.dma_start(window[j][at:at + WIN0, :].bitcast(F32),
                                 window_table[bass.ds(first, WIN0), a, :]).then_inc(window_in[j], 16)
                if not is_last_two(b):
                    sp.wait_ge(gathered[j], 64 * (half + 1))
                    settle(sp)
                    sp.dma_start(gather_sb[j][:, :], src[bass.ds(b + 2, 1)]).then_inc(gather_in[j], 16)

            fit = fits(sp)
            with sp.If(fit):
                for b in range(2):
                    sp.dma_start(gather_sb[b][:, :], src[b:b + 1]).then_inc(gather_in[b], 16)
                sp.wait_ge(zeros_set, 1)
                sp.dma_start(window_table[NP:NP + P].rearrange("n a w -> n (a w)"), zeros[:, 0:2 * WT]).then_inc(pads_out, 16)
                for t in range(NT):
                    j = t % 2
                    sp.wait_ge(high_ready, 2 * t + 2)
                    sp.wait_ge(low_ready, 2 * t + 2)
                    sp.wait_ge(tail_ready, t + 1)
                    sp.dma_start(window_table[0:NP].rearrange("(p t) a w -> p t a w", p=P)[:, t, :, :],
                                 table_row[j].bitcast(F32)).then_inc(row_out[j], 16)
                sp.wait_ge(pads_out, 16)
                sp.wait_ge(row_out[0], 16 * ((NT + 1) // 2))
                sp.wait_ge(row_out[1], 16 * (NT // 2))
                blocks(sp, load0_windows)
            with sp.Else():
                blocks(sp, load0)

            for c in range(NCH):
                if c == 0:
                    for t in range(T):
                        sp.wait_ge(scattered[t], 16 * NB)
                if c >= 2:
                    sp.wait_ge(part_free, c - 1)
                for t in range(T):
                    sp.dma_start(parts[c % 2][:, t, :, :],
                                 nodes(sums0[t][0:NP, :])[:, c * CH:(c + 1) * CH, :]).then_inc(part_in[c % 2], 16)

            def load1(b, half, j):
                if isinstance(b, int) and b < 2:
                    sp.wait_ge(dup_step, 4 * NB)
                    sp.wait_ge(gathered[j], 128 * (NB // 2))
                else:
                    sp.wait_ge(dup_step1, 4 * (b - 1))
                    settle(sp)
                    sp.wait_ge(gathered1[j], 64 * half)
                    settle(sp)
                    sp.wait_ge(terms1_step, 4 * (b - 1))
                    settle(sp)
                sp.dma_start(src_sb[j][:, :], src[bass.ds(b, 1)]).then_inc(edge_in1[j], 16)
                sp.dma_start(dst_sb[j][:, :], dst[bass.ds(b, 1)]).then_inc(edge_in1[j], 16)
                sp.dma_start(key_rows[j][:, :, :],
                             dst_rows[bass.ds(b, 1)].broadcast_to([P, T, P])).then_inc(edge_in1[j], 16)
                sp.dma_start(feat[j][:, :, :], edge_attr[bass.ds(b, 1)]).then_inc(edge_in1[j], 16)
                sp.dma_start(attn[j][:, :], edge_weight[bass.ds(b, 1)]).then_inc(edge_in1[j], 16)

            def load1_windows(b, quad, m):
                if first_four(b):
                    sp.wait_ge(gathered[0], 64 * (NB // 2))
                    sp.wait_ge(gathered[1], 64 * (NB // 2))
                    sp.wait_ge(dup_step, 4 * NB)
                else:
                    sp.wait_ge(gathered1w[m], 64 * quad)
                    settle(sp)
                    sp.wait_ge(terms1_step, 4 * (b - 3))
                    settle(sp)
                sp.dma_start(src_windows[m][:, :], src[bass.ds(b, 1)]).then_inc(edge_in1w[m], 16)
                sp.dma_start(feat_windows[m][:, :, :], edge_attr[bass.ds(b, 1)]).then_inc(edge_in1w[m], 16)
                sp.dma_start(attn_windows[m][:, :], edge_weight[bass.ds(b, 1)]).then_inc(edge_in1w[m], 16)

            with sp.If(fit):
                fours(sp, load1_windows)
            with sp.Else():
                blocks(sp, load1)

            def read_sums1(copies):
                for c in range(NCH):
                    if c == 0:
                        sp.wait_ge(sums1_landed, 1)
                    if c < 2:
                        sp.wait_ge(part_free, NCH)
                    else:
                        sp.wait_ge(part_free, NCH + c - 1)
                    for t in range(copies):
                        sp.dma_start(parts[c % 2][:, t, :, 0:W1],
                                     nodes(sums1[t][0:NP, :])[:, c * CH:(c + 1) * CH, :]).then_inc(part_in1[c % 2], 16)

            with sp.If(fit):
                read_sums1(1)
            with sp.Else():
                read_sums1(T)
            sp.wait_ge(chunk_out, NCH)
            sp.dma_start(nodes(out), x_sb[:, :, :]).then_inc(stored, 16)
            sp.wait_ge(stored, 16)

        @block.gpsimd
        def _(pool):
            nc.gpsimd.memset(ident[:, :], 0.0).then_inc(made, 1)
            nc.gpsimd.iota(spare[:, :], pattern=[[0, 1]], base=NP, channel_multiplier=1,
                           allow_small_or_imprecise_dtypes=True).then_inc(made, 1)
            pool.wait_ge(made, 2)
            nc.gpsimd.affine_select(out=ident[:, :], in_=ident[:, :], compare_op=ALU.not_equal, fill=1.0,
                                    base=0, pattern=[[-1, P]], channel_multiplier=1).then_inc(made, 1)
            nc.gpsimd.tensor_copy(before[:, :], spare[:, 0:1].broadcast_to([P, P])).then_inc(made, 1)
            pool.wait_ge(made, 4)
            nc.gpsimd.affine_select(out=before[:, :], in_=before[:, :], compare_op=ALU.is_gt, fill=0.0,
                                    base=0, pattern=[[-1, P]], channel_multiplier=1).then_inc(made, 1)

            nc.gpsimd.iota(node_sb[:, :], pattern=[[1, NT]], base=0, channel_multiplier=NT,
                           allow_small_or_imprecise_dtypes=True).then_inc(made, 1)
            nc.gpsimd.iota(columns[:, :], pattern=[[1, WIN]], base=0, channel_multiplier=0,
                           allow_small_or_imprecise_dtypes=True).then_inc(made, 1)

            def gather0(b, half, j):
                pool.wait_ge(edge_in[j], 48 * (half + 1))
                if not (isinstance(b, int) and b < 2):
                    pool.wait_ge(transposed, b - 1)
                    pool.wait_ge(weight_ready, b - 1)
                settle(pool)
                for t in range(T):
                    pool.indirect_dma_start(
                        out=ends[j][:, t, 0:D], out_offset=None, in_=row_table,
                        in_offset=bass.IndirectOffsetOnAxis(ap=src_sb[j][:, t:t + 1], axis=0)).then_inc(gathered[j], 16)
                    pool.indirect_dma_start(
                        out=ends[j][:, t, D:2 * D + 1], out_offset=None, in_=col_table,
                        in_offset=bass.IndirectOffsetOnAxis(ap=dst_sb[j][:, t:t + 1], axis=0)).then_inc(gathered[j], 16)

            def scatter_tile(b, j, t):
                pool.wait_ge(dup_step, 4 * b + 4)
                pool.wait_ge(summed_ready, 4 * b + t + 1)
                wait(pool, scattered[t], 16 * b)
                settle(pool)
                pool.indirect_dma_start(
                    out=sums0[t], out_offset=bass.IndirectOffsetOnAxis(ap=target[j][:, t:t + 1], axis=0),
                    in_=summed0[t][:, :], in_offset=None, compute_op=ALU.add).then_inc(scattered[t], 16)

            def scatter0(b, half, j):
                for t in range(T):
                    scatter_tile(b, j, t)

            def edges0(b, half, j):
                if not is_last_two(b):
                    gather0(b + 2, half + 1, j)
                scatter0(b, half, j)

            def gather_tile(b, half, j, t):
                if t == 0:
                    pool.wait_ge(gather_in[j], 16 * (half + 1))
                    if not early(b):
                        pool.wait_ge(transposed, b - 1)
                    settle(pool)
                pool.indirect_dma_start(
                    out=ends[j][:, t, 0:2 * D], out_offset=None, in_=twice_table,
                    in_offset=bass.IndirectOffsetOnAxis(ap=gather_sb[j][:, t:t + 1], axis=0)).then_inc(gathered[j], 16)

            def edges0_windows(b, half, j):
                for t in range(T):
                    if t < 2:
                        if not (isinstance(b, int) and b >= NB - 3):
                            gather_tile(b + 3, half + 1 + j, 1 - j, t + 2)
                    elif not (isinstance(b, int) and b >= NB - 4):
                        gather_tile(b + 4, half + 2, j, t - 2)
                    scatter_tile(b, j, t)

            fit = fits(pool)
            with pool.If(fit):
                pool.wait_ge(tail_step, 5)
                for t in range(NT):
                    if t >= 2:
                        pool.wait_ge(row_out[t % 2], 16 * (t // 2))
                    nc.gpsimd.tensor_copy(table_row[t % 2][:, :, HID:WT].bitcast(F32), tails[:, t, :, :]).then_inc(tail_ready, 1)
                pool.wait_ge(tables, 64)
                for b in range(3):
                    for t in range(T):
                        gather_tile(b, b // 2, b % 2, t)
                for t in range(2):
                    gather_tile(3, 1, 1, t)
                pool.wait_ge(zeroed, 16 * (5 * T + T))
                blocks(pool, edges0_windows, tail=4)
            with pool.Else():
                pool.wait_ge(tables, 64)
                gather0(0, 0, 0)
                gather0(1, 0, 1)
                pool.wait_ge(zeroed, 16 * (5 * T + T))
                blocks(pool, edges0)

            for c in range(NCH):
                pool.wait_ge(part_in[c % 2], 64 * (c // 2 + 1))
                nc.gpsimd.tensor_tensor(parts[c % 2][:, 2, :, :], parts[c % 2][:, 2, :, :],
                                        parts[c % 2][:, 3, :, :], ALU.add).then_inc(part_sum, 1)

            def gather1(b, half, j):
                pool.wait_ge(edge_in1[j], 80 * (half + 1))
                if not (isinstance(b, int) and b < 2):
                    pool.wait_ge(terms1_step, 4 * (b - 1))
                settle(pool)
                for t in range(T):
                    pool.indirect_dma_start(
                        out=ends1[j][:, t, :], out_offset=None, in_=src_table,
                        in_offset=bass.IndirectOffsetOnAxis(ap=src_sb[j][:, t:t + 1], axis=0)).then_inc(gathered1[j], 16)

            def scatter1(b, half, j):
                pool.wait_ge(dup_step1, 4 * b + 4)
                pool.wait_ge(summed1_ready, b + 1)
                for t in range(T):
                    wait(pool, scattered1[t], 16 * b)
                    settle(pool)
                    pool.indirect_dma_start(
                        out=sums1[t], out_offset=bass.IndirectOffsetOnAxis(ap=target[j][:, t:t + 1], axis=0),
                        in_=summed1[j][:, t, :], in_offset=None, compute_op=ALU.add).then_inc(scattered1[t], 16)

            def edges1(b, half, j):
                if not is_last_two(b):
                    gather1(b + 2, half + 1, j)
                scatter1(b, half, j)

            def gather1_windows(b, quad, m):
                pool.wait_ge(edge_in1w[m], 48 * (quad + 1))
                if not first_four(b):
                    pool.wait_ge(terms1_step, 4 * (b - 3))
                settle(pool)
                for t in range(T):
                    pool.indirect_dma_start(
                        out=ends1_windows[m][:, t, :], out_offset=None, in_=src_table,
                        in_offset=bass.IndirectOffsetOnAxis(ap=src_windows[m][:, t:t + 1], axis=0)).then_inc(gathered1w[m], 16)

            def add_window(quad):
                first = window_start(pool, 4 * quad)
                pool.wait_ge(window_copied, quad + 1)
                settle(pool)
                if not (isinstance(quad, int) and quad == 0):
                    pool.wait_ge(window_added, 16 * quad)
                    settle(pool)
                pool.dma_start(sums1[0][bass.ds(first, WIN), :], window_sum[:, :],
                               accum_op=ALU.add).then_inc(window_added, 16)

            def edges1_windows(b, quad, m):
                gather1_windows(b, quad, m)
                if m == 2 and not first_four(b):
                    add_window(quad - 1)

            pool.wait_ge(tables, 80)
            with pool.If(fit):
                fours(pool, edges1_windows)
                add_window(NB // 4 - 1)
                pool.wait_ge(window_added, 16 * (NB // 4))
                pool.sem_inc(sums1_landed, 1)
            with pool.Else():
                gather1(0, 0, 0)
                gather1(1, 0, 1)
                blocks(pool, edges1)
                for t in range(T):
                    pool.wait_ge(scattered1[t], 16 * NB)
                pool.sem_inc(sums1_landed, 1)
                for c in range(NCH):
                    pool.wait_ge(part_in1[c % 2], 64 * (c // 2 + 1))
                    nc.gpsimd.tensor_tensor(parts[c % 2][:, 2, :, 0:W1], parts[c % 2][:, 2, :, 0:W1],
                                            parts[c % 2][:, 3, :, 0:W1], ALU.add).then_inc(part_sum1, 1)

        @block.scalar
        def _(act):
            act.wait_ge(zeros_set, 1)
            for t in range(T):
                flat = sums0[t].rearrange("(p a) w -> p (a w)", p=P)
                for k in range(5):
                    act.dma_start(flat[:, k * ZW:(k + 1) * ZW], zeros).then_inc(zeroed, 16)
                act.dma_start(sums1[t].rearrange("(p a) w -> p a w", p=P),
                              zeros[:, 0:W1].unsqueeze(1).broadcast_to([P, ROWS // P, W1])).then_inc(zeroed, 16)
            act.wait_ge(sqrt_in, 1)
            nc.scalar.activation(stat[:, 2, :], stat[:, 1, :], ACT.Sqrt).then_inc(sqrt_out, 1)
            act.wait_ge(step, STEPS_TABLE0)
            act.dma_start(nodes(row_table), table_sb[:, :, 0:D]).then_inc(tables, 16)
            act.dma_start(nodes(col_table), table_sb[:, :, :]).then_inc(tables, 16)
            for a in range(2):
                act.dma_start(nodes(twice_table)[:, :, a * D:(a + 1) * D], table_sb[:, :, 0:D]).then_inc(tables, 16)

            def scale_chunk(b, k):
                act.wait_ge(hidden_done, NK * b + k + 1)
                wait(act, hidden_ready, NK * b + k + 1 - NL)
                nc.scalar.activation(scaled[k % NL][:, :], ps_hidden[k % NL][:, :], ACT.Copy,
                                     scale=SLOPE).then_inc(scaled_ready, 1)

            def scale_beta(b, half):
                act.wait_ge(second_done, NK * b + NK)
                wait(act, beta_ready, 2 * (b - 1) + half + 1)
                nc.scalar.activation(beta_scaled[:, half * B:(half + 1) * B], ps_beta[half][:, :], ACT.Copy,
                                     scale=SLOPE).then_inc(beta_scaled_ready, 1)

            def copy_sum(b, t):
                act.wait_ge(summed, 4 * b + t + 1)
                wait(act, scattered[t], 16 * b)
                nc.scalar.activation(summed0[t][:, :], ps_sum[:, 0:W0], ACT.Copy).then_inc(summed_ready, 1)

            def edges0(b, half, j):
                begun = not (isinstance(b, int) and b == 0)
                if begun:
                    scale_beta(b - 1, 0)
                scale_chunk(b, 0)
                if begun:
                    scale_beta(b - 1, 1)
                scale_chunk(b, 1)
                scale_chunk(b, 2)
                scale_chunk(b, 3)
                act.wait_ge(second_done, NK * b + 2)
                wait(act, alpha_ready, b)
                nc.scalar.activation(alpha_scaled[:, :], ps_alpha[:, 0:T * H], ACT.Copy,
                                     scale=SLOPE).then_inc(alpha_scaled_ready, 1)
                if begun:
                    copy_sum(b - 1, 0)
                act.wait_ge(alpha_ready, b + 1)
                wait(act, weight_ready, b)
                nc.scalar.activation(alpha_exp[:, :, :].rearrange("p t h -> p (t h)"), alpha[:, :],
                                     ACT.Exp).then_inc(exp_ready, 1)
                scale_chunk(b, 4)
                if begun:
                    copy_sum(b - 1, 1)
                scale_chunk(b, 5)
                if begun:
                    copy_sum(b - 1, 2)
                    copy_sum(b - 1, 3)

            def round_ends(b, j):
                act.wait_ge(transposed, b + 1)
                wait(act, hidden_done, NK * (b - 1))
                nc.scalar.activation(ends_high[j][:, :], ps_T[:, :], ACT.Copy).then_inc(ends_high_ready, 1)

            def scale_alpha(b):
                act.wait_ge(second_done, NK * b + 2)
                wait(act, alpha_ready, b)
                nc.scalar.activation(alpha_scaled[:, :], ps_alpha[:, 0:T * H], ACT.Copy,
                                     scale=SLOPE).then_inc(alpha_scaled_ready, 1)

            def exp_alpha(b):
                act.wait_ge(alpha_ready, b + 1)
                wait(act, weight_ready, b)
                nc.scalar.activation(alpha_exp[:, :, :].rearrange("p t h -> p (t h)"), alpha[:, :],
                                     ACT.Exp).then_inc(exp_ready, 1)

            def edges0_windows(b, half, j):
                begun = not (isinstance(b, int) and b == 0)
                if begun:
                    scale_beta(b - 1, 0)
                    scale_beta(b - 1, 1)
                scale_chunk(b, 2)
                scale_chunk(b, 3)
                scale_alpha(b)
                if not is_last(b):
                    round_ends(b + 1, 1 - j)
                scale_chunk(b, 4)
                if begun:
                    copy_sum(b - 1, 0)
                exp_alpha(b)
                if begun:
                    copy_sum(b - 1, 1)
                scale_chunk(b, 5)
                if begun:
                    copy_sum(b - 1, 2)
                    copy_sum(b - 1, 3)
                if not is_last(b):
                    scale_chunk(b + 1, 0)
                    scale_chunk(b + 1, 1)

            fit = fits(act)
            with act.If(fit):
                act.wait_ge(loaded, 16 * LOADS)
                nc.scalar.activation(w1_split[:, :], w1_src[:, :], ACT.Copy).then_inc(w_high_ready, 1)
                for j in range(2):
                    nc.scalar.activation(window[j][0:D, 0:HID], w1_src[0:D, :], ACT.Copy).then_inc(w_high_ready, 1)
                def copy_column(t):
                    act.wait_ge(h_turned, t + 1)
                    if t >= 2:
                        act.wait_ge(projected, 2 * (t - 1))
                    nc.scalar.activation(h_T[t % 2][:, :], column_bank(t)[0:D, 0:P], ACT.Copy).then_inc(h_T_ready, 1)

                copy_column(0)
                copy_column(1)
                for t in range(NT):
                    j = t % 2
                    for k, n in enumerate((B, HID - B)):
                        act.wait_ge(projected, 2 * t + k + 1)
                        if t >= 2:
                            act.wait_ge(row_out[j], 16 * (t // 2))
                        nc.scalar.activation(table_row[j][:, 0, k * B:k * B + n], project_bank(t, k)[:, 0:n],
                                             ACT.Copy).then_inc(high_ready, 1)
                    if t + 2 < NT:
                        copy_column(t + 2)
                round_ends(0, 0)
                scale_chunk(0, 0)
                scale_chunk(0, 1)
                blocks(act, edges0_windows)
                scale_beta(NB - 1, 0)
                scale_beta(NB - 1, 1)
                for t in range(T):
                    copy_sum(NB - 1, t)
            with act.Else():
                blocks(act, edges0)
                scale_beta(NB - 1, 0)
                scale_beta(NB - 1, 1)
                for t in range(T):
                    copy_sum(NB - 1, t)

            act.wait_ge(sqrt_in, 2)
            nc.scalar.activation(stat[:, 2, :], stat[:, 1, :], ACT.Sqrt).then_inc(sqrt_out, 1)
            act.wait_ge(step, STEPS_TABLE1)
            act.dma_start(nodes(src_table), table_sb[:, :, :]).then_inc(tables, 16)

            def copy_sum1(b, j):
                act.wait_ge(summed1_done, b + 1)
                if not (isinstance(b, int) and b < 2):
                    for t in range(T):
                        act.wait_ge(scattered1[t], 16 * (b - 1))
                nc.scalar.activation(summed1[j][:, :, :].rearrange("p t w -> p (t w)"), ps_beta[j][:, :],
                                     ACT.Copy).then_inc(summed1_ready, 1)

            def edges1(b, half, j):
                act.wait_ge(dot_step, 4 * b + 4)
                wait(act, terms1_step, 4 * b)
                nc.scalar.activation(gates[:, :, :].rearrange("p a t -> p (a t)"),
                                     dots[:, :, :].rearrange("p a t -> p (a t)"), ACT.Sigmoid).then_inc(gates_ready, 1)
                if not (isinstance(b, int) and b == 0):
                    copy_sum1(b - 1, 1 - j)

            def edges1_windows(b, quad, m):
                act.wait_ge(dot_step, 4 * b + 4)
                wait(act, terms1_step, 4 * b)
                nc.scalar.activation(gates[:, :, :].rearrange("p a t -> p (a t)"),
                                     dots[:, :, :].rearrange("p a t -> p (a t)"), ACT.Sigmoid).then_inc(gates_ready, 1)
                if m == 0 and not first_four(b):
                    copy_window(quad - 1)

            def copy_window(quad):
                act.wait_ge(summed1_done, 4 * quad + 4)
                wait(act, window_added, 16 * quad)
                nc.scalar.activation(window_sum[:, :], ps_beta[0][0:WIN, 0:W1], ACT.Copy).then_inc(window_copied, 1)

            with act.If(fit):
                fours(act, edges1_windows)
                copy_window(NB // 4 - 1)
            with act.Else():
                blocks(act, edges1)
                copy_sum1(NB - 1, 1)

            for c in range(NCH):
                act.wait_ge(feat_T_done, c + 1)
                wait(act, review_done, c)
                nc.scalar.activation(feat_T[:, 0:4, :].rearrange("d t p -> d (t p)"), ps_hidden[0][0:D, :],
                                     ACT.Copy).then_inc(feat_T_ready, 1)
                nc.scalar.activation(feat_T[:, 4:CH, :].rearrange("d t p -> d (t p)"), ps_hidden[1][0:D, 0:(CH - 4) * P],
                                     ACT.Copy).then_inc(feat_T_ready, 1)

        @block.vector
        def _(dve):
            def link(ins):
                LAYER0_STEPS[0] += 1
                ins.then_inc(step, 1)
                dve.wait_ge(step, LAYER0_STEPS[0])

            nc.vector.memset(zeros, 0.0).then_inc(zeros_set, 1)
            nc.vector.memset(gate_w2_sb[:, :, :], 0.0).then_inc(weights_set, 1)
            for j in range(2):
                link(nc.vector.memset(terms0[j][:, :, W0 - 1:W0], 1.0))

            def norm(n):
                def wide(k):
                    return stat[:, k, :].unsqueeze(2).broadcast_to([P, NT, D])
                link(nc.vector.tensor_reduce(out=stat[:, 0, :], in_=x_sb[:, :, :], axis=AX.X, op=ALU.add))
                link(nc.vector.tensor_scalar(stat[:, 0, :], stat[:, 0, :], 1.0 / D, None, ALU.mult))
                link(nc.vector.tensor_tensor(centered[:, :, :], x_sb[:, :, :], wide(0), ALU.subtract))
                link(nc.vector.tensor_tensor(squares, centered[:, :, :], centered[:, :, :], ALU.mult))
                link(nc.vector.tensor_reduce(out=stat[:, 1, :], in_=squares, axis=AX.X, op=ALU.add))
                nc.vector.tensor_scalar(stat[:, 1, :], stat[:, 1, :], 1.0 / D, EPS, ALU.mult, ALU.add).then_inc(sqrt_in, 1)
                dve.wait_ge(sqrt_out, n)
                link(nc.vector.reciprocal(stat[:, 3, :], stat[:, 2, :]))
                link(nc.vector.tensor_tensor(centered[:, :, :], centered[:, :, :], wide(3), ALU.mult))
                link(nc.vector.tensor_scalar(centered[:, :, :], centered[:, :, :], 0.0, None, ALU.max))

            dve.wait_ge(loaded, 16 * LOADS)
            norm(1)
            link(nc.vector.tensor_copy(table_sb[:, :, 0:D], centered[:, :, :]))
            link(nc.vector.tensor_copy(table_sb[:, :, D:D + 1], pos_sb[:, :].unsqueeze(2)))
            assert LAYER0_STEPS[0] == STEPS_TABLE0
            dve.wait_ge(made, 7)

            def find_targets(b, j, keys, here, before_equal, before_target):
                before_equal()
                nc.vector.tensor_tensor(equal[j][:, :, :], key_rows[j][:, :, :],
                                        keys[j][:, :].unsqueeze(2).broadcast_to([P, T, P]),
                                        ALU.is_equal).then_inc(here, 1)
                dve.wait_ge(here, 4 * b + 1)
                nc.vector.tensor_tensor(earlier[:, :, :], equal[j][:, :, :],
                                        before[:, :].unsqueeze(1).broadcast_to([P, T, P]), ALU.mult).then_inc(here, 1)
                dve.wait_ge(here, 4 * b + 2)
                nc.vector.tensor_reduce(out=earlier_max[:, :], in_=earlier[:, :, :], axis=AX.X,
                                        op=ALU.max).then_inc(here, 1)
                dve.wait_ge(here, 4 * b + 3)
                before_target()
                nc.vector.tensor_tensor(target[j][:, :], earlier_max[:, :], keys[j][:, :], ALU.max).then_inc(here, 1)

            def turn_ends(b, j):
                dve.wait_ge(transposed, b + 1)
                wait(dve, hidden_done, NK * (b - 1))
                nc.vector.tensor_copy(ends_T[j][:, :], ps_T[:, :]).then_inc(ends_ready, 1)

            def rectify_chunk(b, k):
                dve.wait_ge(scaled_ready, NK * b + k + 1)
                if not (isinstance(b, int) and b == 0):
                    dve.wait_ge(second_done, NK * (b - 1) + k + 1)
                nc.vector.tensor_tensor(hidden[k][:, :], scaled[k % NL][:, :], ps_hidden[k % NL][:, :],
                                        ALU.max).then_inc(hidden_ready, 1)

            def rectify_beta(b, half):
                dve.wait_ge(beta_scaled_ready, 2 * b + half + 1)
                wait(dve, terms_ready, b)
                nc.vector.tensor_tensor(beta[:, :, :, :].rearrange("p t h d -> p (t h d)")[:, half * B:(half + 1) * B],
                                        beta_scaled[:, half * B:(half + 1) * B], ps_beta[half][:, :],
                                        ALU.max).then_inc(beta_ready, 1)

            def weigh_beta(b, j):
                dve.wait_ge(beta_ready, 2 * b + 2)
                dve.wait_ge(weight_ready, b + 1)
                nc.vector.tensor_tensor(
                    terms0[j][:, :, 0:H * D].rearrange("p t (h d) -> p t h d", h=H), beta[:, :, :, :],
                    terms0[j][:, :, H * D:H * D + H].unsqueeze(3).broadcast_to([P, T, H, D]),
                    ALU.mult).then_inc(terms_ready, 1)

            def targets0(b, j):
                def before_equal():
                    wait_in(b, j)
                    if not (isinstance(b, int) and b < 2):
                        dve.wait_ge(summed, 4 * (b - 1))
                def before_target():
                    if not (isinstance(b, int) and b < 2):
                        for t in range(T):
                            dve.wait_ge(scattered[t], 16 * (b - 1))
                find_targets(b, j, src_sb, dup_step, before_equal, before_target)

            halves = {}

            def wait_in(b, j):
                dve.wait_ge(edge_in[j], 48 * (halves["half"] + 1))

            def edges0(b, half, j):
                halves["half"] = half
                begun = not (isinstance(b, int) and b == 0)
                if begun:
                    rectify_beta(b - 1, 0)
                rectify_chunk(b, 0)
                if begun:
                    rectify_beta(b - 1, 1)
                rectify_chunk(b, 1)
                if begun:
                    weigh_beta(b - 1, 1 - j)
                rectify_chunk(b, 2)
                rectify_chunk(b, 3)
                dve.wait_ge(alpha_scaled_ready, b + 1)
                wait(dve, exp_ready, b)
                nc.vector.tensor_tensor(alpha[:, :], alpha_scaled[:, :], ps_alpha[:, 0:T * H],
                                        ALU.max).then_inc(alpha_ready, 1)
                targets0(b, j)
                rectify_chunk(b, 4)
                dve.wait_ge(exp_ready, b + 1)
                if not (isinstance(b, int) and b < 2):
                    dve.wait_ge(summed, 4 * (b - 1))
                nc.vector.tensor_tensor(terms0[j][:, :, H * D:H * D + H], alpha_exp[:, :, :],
                                        ends[j][:, :, 2 * D:2 * D + 1].broadcast_to([P, T, H]),
                                        ALU.mult).then_inc(weight_ready, 1)
                rectify_chunk(b, 5)
                if not is_last(b):
                    turn_ends(b + 1, 1 - j)

            def split_ends(b, half, j):
                dve.wait_ge(edge_in[j], 48 * (half + 1))
                dve.wait_ge(window_in[j], 32 * (half + 1))
                wait(dve, hidden_done, NK * (b - 1))
                nc.vector.tensor_scalar(ends_low[j][D:P, :], dst_rows_sb[j][D:P, :, :].rearrange("p t e -> p (t e)"),
                                        window[j][D:P, HID:HID + 1].bitcast(F32), None,
                                        ALU.is_equal).then_inc(hot_T_ready, 1)
                dve.wait_ge(ends_high_ready, b + 1)
                nc.vector.tensor_tensor(ends_low[j][0:D, :], ps_T[0:D, :], ends_high[j][0:D, :].bitcast(F32),
                                        ALU.subtract).then_inc(ends_low_ready, 1)

            def edges0_windows(b, half, j):
                begun = not (isinstance(b, int) and b == 0)
                if begun:
                    rectify_beta(b - 1, 0)
                    rectify_beta(b - 1, 1)
                    weigh_beta(b - 1, 1 - j)
                rectify_chunk(b, 2)
                rectify_chunk(b, 3)
                dve.wait_ge(alpha_scaled_ready, b + 1)
                wait(dve, exp_ready, b)
                nc.vector.tensor_tensor(alpha[:, :], alpha_scaled[:, :], ps_alpha[:, 0:T * H],
                                        ALU.max).then_inc(alpha_ready, 1)
                if not is_last(b):
                    split_ends(b + 1, half + j, 1 - j)
                rectify_chunk(b, 4)
                dve.wait_ge(edge_in[j], 48 * (half + 1))
                if not early(b):
                    dve.wait_ge(summed, 4 * (b - 1))
                nc.vector.tensor_tensor(equal[j][:, :, :], key_rows[j][:, :, :],
                                        src_sb[j][:, :].unsqueeze(2).broadcast_to([P, T, P]),
                                        ALU.is_equal).then_inc(dup_step, 1)
                dve.wait_ge(exp_ready, b + 1)
                nc.vector.tensor_tensor(terms0[j][:, :, H * D:H * D + H], alpha_exp[:, :, :],
                                        ps_alpha[:, T * H:T * H + 2 * T].rearrange("p (t a) -> p t a", a=2)[:, :, 0:1]
                                        .broadcast_to([P, T, H]), ALU.mult).then_inc(weight_ready, 1)
                rectify_chunk(b, 5)
                dve.wait_ge(dup_step, 4 * b + 1)
                nc.vector.tensor_tensor(earlier[:, :, :], equal[j][:, :, :],
                                        before[:, :].unsqueeze(1).broadcast_to([P, T, P]), ALU.mult).then_inc(dup_step, 1)
                dve.wait_ge(dup_step, 4 * b + 2)
                nc.vector.tensor_reduce(out=earlier_max[:, :], in_=earlier[:, :, :], axis=AX.X,
                                        op=ALU.max).then_inc(dup_step, 1)
                dve.wait_ge(dup_step, 4 * b + 3)
                if not early(b):
                    for t in range(T):
                        dve.wait_ge(scattered[t], 16 * (b - 1))
                nc.vector.tensor_tensor(target[j][:, :], earlier_max[:, :], src_sb[j][:, :], ALU.max).then_inc(dup_step, 1)
                if not is_last(b):
                    rectify_chunk(b + 1, 0)
                    rectify_chunk(b + 1, 1)

            dst_blocks = dst_all_sb.rearrange("p (w e) -> p w e", e=T)
            dst_fours = dst_all_sb.rearrange("p (w e) -> p w e", e=4 * T)
            nc.vector.memset(ones[:, :], 1.0).then_inc(fits_step, 1)
            nc.vector.tensor_copy(first_dst[:, :], dst_blocks[0:1, :, 0]).then_inc(firsts_ready, 1)
            nc.vector.tensor_copy(first_node[:, :], dst_blocks[0:1, :, 0]).then_inc(fits_step, 1)
            dve.wait_ge(firsts_spread, 1)
            nc.vector.tensor_tensor(offset0.rearrange("p (w e) -> p w e", e=T), dst_blocks,
                                    ps_sum[:, 0:NB].unsqueeze(2).broadcast_to([P, NB, T]),
                                    ALU.subtract).then_inc(fits_step, 1)
            nc.vector.tensor_tensor(offset[:, :].rearrange("p (w e) -> p w e", e=4 * T), dst_fours,
                                    ps_sum[:, 0:NB].rearrange("p (w a) -> p w a", a=4)[:, :, 0:1]
                                    .broadcast_to([P, NB // 4, 4 * T]), ALU.subtract).then_inc(fits_step, 1)
            dve.wait_ge(fits_step, 4)
            for k, o in enumerate((offset0, offset[:, :])):
                nc.vector.tensor_reduce(out=reach[:, k:k + 1], in_=o, axis=AX.X, op=ALU.max).then_inc(fits_step, 1)
                nc.vector.tensor_reduce(out=reach[:, 2 + k:3 + k], in_=o, axis=AX.X, op=ALU.min).then_inc(fits_step, 1)
            dve.wait_ge(fits_step, 8)
            nc.vector.tensor_scalar(reach[:, 4:5], reach[:, 0:1], float(WIN - WIN0), None, ALU.add).then_inc(fits_step, 1)
            nc.vector.tensor_scalar(reach[:, 5:7], reach[:, 2:4], -1.0, float(WIN - 1), ALU.mult, ALU.add).then_inc(fits_step, 1)
            nc.vector.tensor_copy(reach[:, 7:8], reach[:, 1:2]).then_inc(fits_step, 1)
            dve.wait_ge(fits_step, 11)
            nc.vector.tensor_reduce(out=reach[:, 0:1], in_=reach[:, 4:8], axis=AX.X, op=ALU.max).then_inc(reach_ready, 1)
            dve.wait_ge(reach_turned, 1)
            nc.vector.tensor_reduce(out=first_dst[0:1, 0:1], in_=ps_sum[0:1, 0:P], axis=AX.X,
                                    op=ALU.max).then_inc(fits_step, 1)
            dve.wait_ge(fits_step, 12)
            nc.vector.tensor_scalar(fits_sb[:, :], first_dst[0:1, 0:1], float(WIN - 1), None,
                                    ALU.is_le).then_inc(fits_ready, 1)

            fit = fits(dve)
            with dve.If(fit):
                nc.vector.memset(tails[:, :, :, :], 0.0).then_inc(tail_step, 1)
                nc.vector.tensor_copy(pos_high[:, :], pos_sb[:, :]).then_inc(tail_step, 1)
                dve.wait_ge(tail_step, 2)
                nc.vector.tensor_copy(tails[:, :, :, 0], node_sb[:, :].unsqueeze(2).broadcast_to([P, NT, 2])).then_inc(tail_step, 1)
                nc.vector.tensor_copy(tails[:, :, 0, 2], pos_high[:, :].bitcast(F32)).then_inc(tail_step, 1)
                nc.vector.tensor_tensor(tails[:, :, 1, 2], pos_sb[:, :], pos_high[:, :].bitcast(F32),
                                        ALU.subtract).then_inc(tail_step, 1)
                dve.wait_ge(w_high_ready, 3)
                nc.vector.tensor_tensor(w1_split[D:P, :], w1_src[D:P, :], w1_split[D:P, :].bitcast(F32),
                                        ALU.subtract).then_inc(w_low_ready, 1)
                for t in range(NT):
                    j = t % 2
                    for k, n in enumerate((B, HID - B)):
                        dve.wait_ge(high_ready, 2 * t + k + 1)
                        nc.vector.tensor_tensor(table_row[j][:, 1, k * B:k * B + n], project_bank(t, k)[:, 0:n],
                                                table_row[j][:, 0, k * B:k * B + n].bitcast(F32),
                                                ALU.subtract).then_inc(low_ready, 1)
                split_ends(0, 0, 0)
                rectify_chunk(0, 0)
                rectify_chunk(0, 1)
                blocks(dve, edges0_windows)
                rectify_beta(NB - 1, 0)
                rectify_beta(NB - 1, 1)
                weigh_beta(NB - 1, 1)
            with dve.Else():
                turn_ends(0, 0)
                blocks(dve, edges0)
                rectify_beta(NB - 1, 0)
                rectify_beta(NB - 1, 1)
                weigh_beta(NB - 1, 1)

            for c in range(NCH):
                q = parts[c % 2]
                dve.wait_ge(part_in[c % 2], 64 * (c // 2 + 1))
                link(nc.vector.tensor_tensor(q[:, 0, :, :], q[:, 0, :, :], q[:, 1, :, :], ALU.add))
                dve.wait_ge(part_sum, c + 1)
                link(nc.vector.tensor_tensor(q[:, 0, :, :], q[:, 0, :, :], q[:, 2, :, :], ALU.add))
                link(nc.vector.tensor_scalar(empty[:, :].unsqueeze(2), q[:, 0, :, W0 - 1:W0], 0.0, None, ALU.is_equal))
                link(nc.vector.tensor_tensor(inverse[:, :, :], q[:, 0, :, H * D:H * D + H],
                                             empty[:, :].unsqueeze(2).broadcast_to([P, CH, H]), ALU.add))
                link(nc.vector.reciprocal(inverse[:, :, :], inverse[:, :, :]))
                link(nc.vector.tensor_scalar(inverse[:, :, :], inverse[:, :, :], 1e-16, 1.0 / H, ALU.add, ALU.mult))
                for t in range(CH):
                    last = nc.vector.tensor_tensor(q[:, 1, t, 0:H * D].rearrange("p (h d) -> p h d", h=H),
                                                   q[:, 0, t, 0:H * D].rearrange("p (h d) -> p h d", h=H),
                                                   inverse[:, t, :].unsqueeze(2).broadcast_to([P, H, D]), ALU.mult)
                link(last)
                for t in range(CH):
                    last = nc.vector.tensor_reduce(out=mean[:, t, :], in_=q[:, 1, t, 0:H * D].rearrange("p (h d) -> p d h", h=H),
                                                   axis=AX.X, op=ALU.add)
                last.then_inc(part_free, 1)
                dve.wait_ge(part_free, c + 1)
                link(nc.vector.tensor_tensor(x_sb[:, c * CH:(c + 1) * CH, :], x_sb[:, c * CH:(c + 1) * CH, :],
                                             mean[:, :, :], ALU.add))
            norm(2)
            link(nc.vector.tensor_tensor(table_sb[:, :, 0:D], centered[:, :, :],
                                         cj_sb[:, :].unsqueeze(2).broadcast_to([P, NT, D]), ALU.mult))
            link(nc.vector.tensor_copy(table_sb[:, :, D:D + 1], cj_sb[:, :].unsqueeze(2)))
            assert LAYER0_STEPS[0] == STEPS_TABLE1

            def edges1(b, half, j):
                def before_equal():
                    dve.wait_ge(edge_in1[j], 80 * (half + 1))
                    if not (isinstance(b, int) and b < 2):
                        dve.wait_ge(summed1_done, b - 1)
                    elif b < 2:
                        dve.wait_ge(summed, 4 * NB)
                def before_target():
                    for t in range(T):
                        if isinstance(b, int) and b < 2:
                            dve.wait_ge(scattered[t], 16 * NB)
                        else:
                            dve.wait_ge(scattered1[t], 16 * (b - 1))
                dve.wait_ge(edge_in1[j], 80 * (half + 1))
                wait(dve, dot_step, 4 * b)
                for a in range(2):
                    nc.vector.tensor_tensor(products[:, a, :, :], feat[j][:, :, :],
                                            dots_w[:, a, :].unsqueeze(1).broadcast_to([P, T, D]),
                                            ALU.mult).then_inc(dot_step, 1)
                wait(dve, gates_ready, b)
                for a in range(2):
                    dve.wait_ge(dot_step, 4 * b + 1 + a)
                    nc.vector.tensor_reduce(out=dots[:, a, :], in_=products[:, a, :, :], axis=AX.X,
                                            op=ALU.add).then_inc(dot_step, 1)
                find_targets(b, j, dst_sb, dup_step1, before_equal, before_target)
                dve.wait_ge(gates_ready, b + 1)
                nc.vector.tensor_tensor(feat_gate[:, :], gates[:, 1, :], attn[j][:, :], ALU.mult).then_inc(terms1_step, 1)
                dve.wait_ge(gathered1[j], 64 * (half + 1))
                if not (isinstance(b, int) and b < 2):
                    dve.wait_ge(summed1_done, b - 1)
                nc.vector.tensor_tensor(terms1[j][:, :, 0:D], ends1[j][:, :, 0:D],
                                        gates[:, 0, :].unsqueeze(2).broadcast_to([P, T, D]), ALU.mult).then_inc(terms1_step, 1)
                dve.wait_ge(terms1_step, 4 * b + 2)
                nc.vector.tensor_tensor(feat_gate[:, :].unsqueeze(2), feat_gate[:, :].unsqueeze(2),
                                        ends1[j][:, :, D:D + 1], ALU.mult).then_inc(terms1_step, 1)
                dve.wait_ge(terms1_step, 4 * b + 3)
                nc.vector.tensor_tensor(terms1[j][:, :, D:W1], feat[j][:, :, :],
                                        feat_gate[:, :].unsqueeze(2).broadcast_to([P, T, D]), ALU.mult).then_inc(terms1_step, 1)

            def edge_gates(b, quad, m):
                dve.wait_ge(edge_in1w[m], 48 * (quad + 1))
                wait(dve, dot_step, 4 * b)
                for a in range(2):
                    nc.vector.tensor_tensor(products[:, a, :, :], feat_windows[m][:, :, :],
                                            dots_w[:, a, :].unsqueeze(1).broadcast_to([P, T, D]),
                                            ALU.mult).then_inc(dot_step, 1)
                wait(dve, gates_ready, b)
                for a in range(2):
                    dve.wait_ge(dot_step, 4 * b + 1 + a)
                    nc.vector.tensor_reduce(out=dots[:, a, :], in_=products[:, a, :, :], axis=AX.X,
                                            op=ALU.add).then_inc(dot_step, 1)

            def edges1_windows(b, quad, m):
                edge_gates(b, quad, m)
                if not early(b):
                    dve.wait_ge(summed1_done, b - 1)
                nc.vector.tensor_tensor(hot[m % 2][:, :, :], columns[:, :].unsqueeze(1).broadcast_to([P, T, WIN]),
                                        offset[:, bass.ds(b * T, T)].unsqueeze(2).broadcast_to([P, T, WIN]),
                                        ALU.is_equal).then_inc(hot_ready, 1)
                dve.wait_ge(gates_ready, b + 1)
                nc.vector.tensor_tensor(feat_gate[:, :], gates[:, 1, :], attn_windows[m][:, :], ALU.mult).then_inc(terms1_step, 1)
                dve.wait_ge(gathered1w[m], 64 * (quad + 1))
                nc.vector.tensor_tensor(terms1_windows[m][:, :, 0:D], ends1_windows[m][:, :, 0:D],
                                        gates[:, 0, :].unsqueeze(2).broadcast_to([P, T, D]), ALU.mult).then_inc(terms1_step, 1)
                dve.wait_ge(terms1_step, 4 * b + 2)
                nc.vector.tensor_tensor(feat_gate[:, :].unsqueeze(2), feat_gate[:, :].unsqueeze(2),
                                        ends1_windows[m][:, :, D:D + 1], ALU.mult).then_inc(terms1_step, 1)
                dve.wait_ge(terms1_step, 4 * b + 3)
                nc.vector.tensor_tensor(terms1_windows[m][:, :, D:W1], feat_windows[m][:, :, :],
                                        feat_gate[:, :].unsqueeze(2).broadcast_to([P, T, D]), ALU.mult).then_inc(terms1_step, 1)

            with dve.If(fit):
                fours(dve, edges1_windows)
            with dve.Else():
                blocks(dve, edges1)

            def add_copies(c):
                q = parts[c % 2]
                dve.wait_ge(part_in1[c % 2], 64 * (c // 2 + 1))
                nc.vector.tensor_tensor(q[:, 0, :, 0:W1], q[:, 0, :, 0:W1], q[:, 1, :, 0:W1], ALU.add).then_inc(copies_added, 1)
                dve.wait_ge(part_sum1, c + 1)
                dve.wait_ge(copies_added, 2 * c + 1)
                nc.vector.tensor_tensor(q[:, 0, :, 0:W1], q[:, 0, :, 0:W1], q[:, 2, :, 0:W1], ALU.add).then_inc(copies_added, 1)
                dve.wait_ge(copies_added, 2 * c + 2)

            def finish_chunk(c, add):
                q = parts[c % 2]
                if add:
                    add_copies(c)
                else:
                    dve.wait_ge(part_in1[c % 2], 16 * (c // 2 + 1))
                dve.wait_ge(review_done, c + 1)
                nc.vector.tensor_tensor(mean[:, :, :], q[:, 0, :, 0:D],
                                        ps_sum[:, 0:CH * D].rearrange("p (t d) -> p t d", t=CH), ALU.add).then_inc(mean_step, 1)
                dve.wait_ge(mean_step, c + 1)
                nc.vector.tensor_tensor(mean[:, :, :], mean[:, :, :],
                                        ci_sb[:, c * CH:(c + 1) * CH].unsqueeze(2).broadcast_to([P, CH, D]),
                                        ALU.mult).then_inc(part_free, 1)
                dve.wait_ge(part_free, NCH + c + 1)
                nc.vector.tensor_tensor(x_sb[:, c * CH:(c + 1) * CH, :], x_sb[:, c * CH:(c + 1) * CH, :],
                                        mean[:, :, :], ALU.add).then_inc(chunk_out, 1)
                dve.wait_ge(chunk_out, c + 1)

            with dve.If(fit):
                for c in range(NCH):
                    finish_chunk(c, False)
            with dve.Else():
                for c in range(NCH):
                    finish_chunk(c, True)

        @block.tensor
        def _(pe):
            def transpose_ends(b, half, j):
                pe.wait_ge(gathered[j], 128 * (half + 1))
                wait(pe, ends_ready, b)
                for t in range(T):
                    last = nc.tensor.transpose(ps_T[:, t * P:(t + 1) * P], ends[j][:, t, 0:2 * D], ident[:, :])
                last.then_inc(transposed, 1)

            def first_product(b, k, j):
                if k == 0:
                    pe.wait_ge(ends_ready, b + 1)
                wait(pe, hidden_ready, NK * b + k + 1 - NL)
                nc.tensor.matmul(ps_hidden[k % NL][:, :], w1_sb[:, k * P:(k + 1) * P], ends_T[j][:, :],
                                 start=True, stop=True).then_inc(hidden_done, 1)

            def turn_src(b, half, j):
                pe.wait_ge(gathered[j], 64 * (half + 1))
                wait(pe, ends_low_ready, b)
                settle(pe)
                for t in range(T):
                    last = nc.tensor.transpose(ps_T[:, t * P:(t + 1) * P],
                                               ends[j][:, t, 0:2 * D], ident[:, :])
                last.then_inc(transposed, 1)

            def first_product_windows(b, k, half, j):
                if k == 0:
                    pe.wait_ge(ends_low_ready, b + 1)
                    pe.wait_ge(hot_T_ready, b + 1)
                    pe.wait_ge(window_in[j], 32 * (half + 1))
                wait(pe, hidden_ready, NK * b + k + 1 - NL)
                o = ps_hidden[k % NL][:, :]
                nc.tensor.matmul(o, w1_split[:, k * P:(k + 1) * P], ends_high[j][:, :], start=True, stop=False)
                nc.tensor.matmul(o, window[j][:, k * P:(k + 1) * P], ends_low[j][:, :],
                                 start=False, stop=True).then_inc(hidden_done, 1)

            def dst_vec(b, j):
                wait(pe, weight_ready, b)
                for t in range(T):
                    nc.tensor.matmul(ps_alpha[:, T * H + 2 * t:T * H + 2 * t + 2],
                                     ends_low[j][D:P, t * P:(t + 1) * P], window[j][D:P, HID + 2:WT], start=True, stop=True)

            def second_product(b, k):
                pe.wait_ge(hidden_ready, NK * b + k + 1)
                if k == 0:
                    wait(pe, alpha_ready, b)
                if k == 2:
                    wait(pe, beta_ready, 2 * b)
                for t in range(T):
                    if k < 2:
                        o, w = ps_alpha[:, t * H + 2 * k:t * H + 2 * k + 2], gate_w2_sb[:, k, :]
                    else:
                        at = (t % 2) * H * D + (k - 2) * D
                        o, w = ps_beta[t // 2][:, at:at + D], msg_w2_sb[:, k - 2, :]
                    last = nc.tensor.matmul(o, hidden[k][:, t * P:(t + 1) * P], w, start=True, stop=True)
                last.then_inc(second_done, 1)

            def sum_tile(b, t, j):
                if t == 0:
                    pe.wait_ge(terms_ready, b + 1)
                    pe.wait_ge(dup_step, 4 * b + 1)
                wait(pe, summed_ready, 4 * b + t)
                nc.tensor.matmul(ps_sum[:, 0:W0], equal[j][:, t, :], terms0[j][:, t, :],
                                 start=True, stop=True).then_inc(summed, 1)

            def edges0_windows(b, half, j):
                begun = not (isinstance(b, int) and b == 0)
                first_product_windows(b, 2, half, j)
                dst_vec(b, j)
                second_product(b, 0)
                first_product_windows(b, 3, half, j)
                second_product(b, 1)
                if not is_last(b):
                    turn_src(b + 1, half + j, 1 - j)
                first_product_windows(b, 4, half, j)
                if begun:
                    sum_tile(b - 1, 0, 1 - j)
                second_product(b, 2)
                if begun:
                    sum_tile(b - 1, 1, 1 - j)
                first_product_windows(b, 5, half, j)
                second_product(b, 3)
                if begun:
                    sum_tile(b - 1, 2, 1 - j)
                second_product(b, 4)
                if begun:
                    sum_tile(b - 1, 3, 1 - j)
                if not is_last(b):
                    first_product_windows(b + 1, 0, half + j, 1 - j)
                    first_product_windows(b + 1, 1, half + j, 1 - j)
                second_product(b, 5)

            def edges0(b, half, j):
                begun = not (isinstance(b, int) and b == 0)
                first_product(b, 0, j)
                first_product(b, 1, j)
                first_product(b, 2, j)
                second_product(b, 0)
                first_product(b, 3, j)
                second_product(b, 1)
                if begun:
                    sum_tile(b - 1, 0, 1 - j)
                first_product(b, 4, j)
                second_product(b, 2)
                if begun:
                    sum_tile(b - 1, 1, 1 - j)
                first_product(b, 5, j)
                second_product(b, 3)
                if begun:
                    sum_tile(b - 1, 2, 1 - j)
                if not is_last(b):
                    transpose_ends(b + 1, half + j, 1 - j)
                second_product(b, 4)
                if begun:
                    sum_tile(b - 1, 3, 1 - j)
                second_product(b, 5)

            pe.wait_ge(made, 7)
            pe.wait_ge(loaded, 16 * LOADS)
            pe.wait_ge(fits_step, 1)
            pe.wait_ge(firsts_ready, 1)
            nc.tensor.matmul(ps_sum[:, 0:NB], ones[:, :], first_dst[:, :], start=True,
                             stop=True).then_inc(firsts_spread, 1)
            pe.wait_ge(reach_ready, 1)
            nc.tensor.transpose(ps_sum[0:1, 0:P], reach[:, 0:1], ident[:, :]).then_inc(reach_turned, 1)

            def turn_column(t):
                wait(pe, h_T_ready, t - 1)
                nc.tensor.transpose(column_bank(t)[0:D, 0:P], centered[:, t, :], ident[:, :]).then_inc(h_turned, 1)

            fit = fits(pe)
            with pe.If(fit):
                pe.wait_ge(step, STEPS_TABLE0 - 2)
                pe.wait_ge(w_low_ready, 1)
                for t in range(NT):
                    if t == 0:
                        turn_column(0)
                    if t < NT - 1:
                        turn_column(t + 1)
                    pe.wait_ge(h_T_ready, t + 1)
                    for k, n in enumerate((B, HID - B)):
                        wait(pe, low_ready, 2 * (t - 2) + k + 1)
                        nc.tensor.matmul(project_bank(t, k)[:, 0:n], h_T[t % 2][:, :], w1_dst[:, k * B:k * B + n],
                                         start=True, stop=True).then_inc(projected, 1)
                turn_src(0, 0, 0)
                first_product_windows(0, 0, 0, 0)
                first_product_windows(0, 1, 0, 0)
                blocks(pe, edges0_windows)
                for t in range(T):
                    sum_tile(NB - 1, t, 1)
            with pe.Else():
                transpose_ends(0, 0, 0)
                blocks(pe, edges0)
                for t in range(T):
                    sum_tile(NB - 1, t, 1)

            def edges1(b, half, j):
                pe.wait_ge(terms1_step, 4 * b + 4)
                pe.wait_ge(dup_step1, 4 * b + 1)
                if isinstance(b, int) and b < 2:
                    pe.wait_ge(beta_ready, 2 * NB)
                else:
                    pe.wait_ge(summed1_ready, b - 1)
                for t in range(T):
                    last = nc.tensor.matmul(ps_beta[j][:, t * W1:(t + 1) * W1], equal[j][:, t, :], terms1[j][:, t, :],
                                            start=True, stop=True)
                last.then_inc(summed1_done, 1)

            def edges1_windows(b, quad, m):
                pe.wait_ge(terms1_step, 4 * b + 4)
                pe.wait_ge(hot_ready, b + 1)
                if m == 0:
                    if first_four(b):
                        pe.wait_ge(beta_ready, 2 * NB)
                    else:
                        pe.wait_ge(window_copied, quad)
                for t in range(T):
                    last = nc.tensor.matmul(ps_beta[0][0:WIN, 0:W1], hot[m % 2][:, t, :], terms1_windows[m][:, t, :],
                                            start=(m == 0 and t == 0), stop=(m == 3 and t == T - 1))
                last.then_inc(summed1_done, 1)

            with pe.If(fit):
                fours(pe, edges1_windows)
            with pe.Else():
                blocks(pe, edges1)

            def project_sums(c, added):
                if added:
                    pe.wait_ge(copies_added, 2 * c + 2)
                else:
                    pe.wait_ge(part_in1[c % 2], 16 * (c // 2 + 1))
                wait(pe, feat_T_ready, 2 * c)
                for t in range(CH):
                    last = nc.tensor.transpose(ps_hidden[t // 4][0:D, (t % 4) * P:(t % 4 + 1) * P],
                                               parts[c % 2][:, 0, t, D:W1], ident[:, :])
                last.then_inc(feat_T_done, 1)
                pe.wait_ge(feat_T_ready, 2 * c + 2)
                wait(pe, mean_step, c)
                for t in range(CH):
                    last = nc.tensor.matmul(ps_sum[:, t * D:(t + 1) * D], feat_T[:, t, :], review_w_sb[:, :],
                                            start=True, stop=True)
                last.then_inc(review_done, 1)

            with pe.If(fit):
                for c in range(NCH):
                    project_sums(c, False)
            with pe.Else():
                for c in range(NCH):
                    project_sums(c, True)


NORM_STEPS = 8
STEPS_TABLE0 = 2 + NORM_STEPS + 2
STEPS_TABLE1 = STEPS_TABLE0 + 8 * NCH + NORM_STEPS + 2


def kernel(x, src, dst, edge_attr_64, edge_weight, node_vec, node_vec1, node_vec1_n2, L0_gnn_gate_w1,
           L0_gnn_gate_w2, L0_gnn_msg_w1, L0_gnn_msg_w2, L1_gnn_prob_w, L1_gnn_review_score_w, L1_gnn_review_w):
    import concourse.bacc as bacc
    from concourse.bass_utils import run_bass_kernel_spmd

    def padded(a, n, value=0):
        a = np.asarray(a)
        return np.concatenate([a, np.full((n - a.shape[0],) + a.shape[1:], value, a.dtype)])

    src, dst = padded(src, EP, N), padded(dst, EP, N)
    first = np.concatenate([np.asarray(L0_gnn_gate_w1).reshape(2 * P, P), np.asarray(L0_gnn_msg_w1).reshape(4 * P, P)])
    arrays = {
        "x": padded(x, NP),
        "src": src.reshape(NB, P, T), "dst": dst.reshape(NB, P, T),
        "src_rows": src.reshape(NB, P, T).transpose(0, 2, 1), "dst_rows": dst.reshape(NB, P, T).transpose(0, 2, 1),
        "dst_all": dst.reshape(NB, P, T).transpose(1, 0, 2).reshape(P, NB * T),
        "edge_attr": padded(edge_attr_64, EP).reshape(NB, P, T, D),
        "edge_weight": padded(edge_weight, EP).reshape(NB, P, T),
        "node_vec": padded(node_vec, NP, 1).reshape(P, NT),
        "node_vec1": padded(node_vec1, NP).reshape(P, NT),
        "node_vec1_n2": padded(node_vec1_n2, NP).reshape(P, NT),
        "w1": first.T,
        "gate_w2": np.asarray(L0_gnn_gate_w2).reshape(H, D, 1),
        "msg_w2": np.asarray(L0_gnn_msg_w2).transpose(2, 0, 1),
        "prob_w": np.asarray(L1_gnn_prob_w), "score_w": np.asarray(L1_gnn_review_score_w),
        "review_w": np.asarray(L1_gnn_review_w).T,
    }
    arrays = {f"in_{k}": np.ascontiguousarray(a) for k, a in arrays.items()}
    nc = bacc.Bacc("TRN2", target_bir_lowering=False, num_devices=1)
    args = [nc.dram_tensor(k, a.shape, mybir.dt.from_np(a.dtype), kind="ExternalInput").ap() for k, a in arrays.items()]
    out = nc.dram_tensor("out", (NP, D), F32, kind="ExternalOutput").ap()
    gnn(nc, *args, out)
    r = run_bass_kernel_spmd(nc, [arrays], core_ids=[0])
    return r.results[0]["out"][:N]
```

```python
import concourse.bass as bass
import numpy as np
from concourse import mybir
from contextlib import ExitStack

F32, F32R, I32 = mybir.dt.float32, mybir.dt.float32r, mybir.dt.int32
ALU = mybir.AluOpType
ACT = mybir.ActivationFunctionType
AX = mybir.AxisListType

P = 128
N = 6250
D = 64
E = 206250
H = 4
NT = -(-N // P)
NP = NT * P
ROWS = NP + P
T = 4
COPIES = 2
B = T * P
NB = 4 * -(-E // (4 * B))
WIN0 = 32
WIN = 128
EP = NB * B
W0 = H * D + H + 1
W1 = 2 * D
NK = 6
NL = 3
CH = 7
NCH = NT // CH
SLOPE = 0.2
EPS = 1e-5
ZW = ROWS * W0 // P // 5
HID = NK * P
WT = HID + 4
assert COPIES == 2 and NT % CH == 0 and NB >= 12 and ROWS * W0 % (P * 5) == 0


def gnn(nc, x, src, dst, src_rows, dst_rows, dst_all, edge_attr, edge_weight, node_vec, node_vec1, node_vec1_n2,
        w1, gate_w2, msg_w2, prob_w, score_w, review_w, out):
    ctx = ExitStack()
    with ctx:
        def sb(name, shape, dt=F32):
            return ctx.enter_context(nc.sbuf_tensor(name, shape, dt))

        def pb(name, shape):
            return ctx.enter_context(nc.psum_tensor(name, shape, F32))

        def sem(name):
            return ctx.enter_context(nc.semaphore(name))

        def dram(name, shape):
            return nc.dram_tensor(name, shape, F32, kind="Internal").ap()

        row_table = dram("row_table", [NP, D])
        split_table = dram("split_table", [NP, 2 * D])
        col_table = dram("col_table", [NP, D + 1])
        src_table = dram("src_table", [NP, D + 1])
        window_table = dram("window_table", [ROWS, 2, WT])
        sums0 = [dram(f"sums0_{c}", [ROWS, W0]) for c in range(COPIES)]
        sums1 = [dram(f"sums1_{t}", [ROWS, W1]) for t in range(T)]

        parts = [sb(f"parts{j}", [P, T, CH, W0]) for j in range(2)]
        squares = parts[0][:, :, :, :].rearrange("p a t w -> p (a t w)")[:, 0:NT * D].rearrange("p (t d) -> p t d", d=D)
        zeros = parts[1][:, :, :, :].rearrange("p a t w -> p (a t w)")[:, 0:ZW]
        x_sb = sb("x_sb", [P, NT, D])
        centered = sb("centered", [P, NT, D])
        table_sb = sb("table_sb", [P, NT, D + 1])
        stat = sb("stat", [P, 4, NT])
        pos_sb = sb("pos_sb", [P, NT])
        cj_sb = sb("cj_sb", [P, NT])
        ci_sb = sb("ci_sb", [P, NT])
        node_sb = sb("node_sb", [P, NT])
        ident = sb("ident", [P, P])
        spare = sb("spare", [P, 1])
        before = sb("before", [P, P])
        w1_sb = sb("w1_sb", [P, NK * P])
        gate_w2_sb = sb("gate_w2_sb", [P, 2, 2])
        msg_w2_sb = sb("msg_w2_sb", [P, H, D])
        dots_w = sb("dots_w", [P, 2, D])
        review_w_sb = sb("review_w_sb", [D, D])
        dst_all_sb = parts[1][:, :, :, :].rearrange("p a t w -> p (a t w)")[:, ZW:ZW + NB * T].bitcast(I32)
        offset0 = parts[1][:, :, :, :].rearrange("p a t w -> p (a t w)")[:, ZW + NB * T:ZW + 2 * NB * T]
        first_node = sb("first_node", [1, NB], I32)
        first_dst = sb("first_dst", [1, NB])
        offset = sb("offset", [P, NB * T])
        reach = sb("reach", [P, 8])
        fits_sb = sb("fits_sb", [1, 1], I32)
        ones = sb("ones", [1, P])
        w1_dst = sb("w1_dst", [D, HID])
        columns = sb("columns", [P, WIN])
        h_T = [sb(f"h_T{j}", [D, P]) for j in range(2)]
        h_parts = [parts[0][:, :, :, :].rearrange("p a t w -> p (a t w)")[:, 4 * WT:4 * WT + NT * D]
                   .rearrange("p (t d) -> p t d", d=D),
                   parts[1][:, :, :, :].rearrange("p a t w -> p (a t w)")[:, ZW:ZW + NT * D].rearrange("p (t d) -> p t d", d=D)]
        table_row = [parts[0][:, :, :, :].rearrange("p a t w -> p (a t w)")[:, 2 * j * WT:2 * (j + 1) * WT]
                     .rearrange("p (a w) -> p a w", a=2).bitcast(F32R) for j in range(2)]
        tails = sb("tails", [P, NT, 2, 4])
        pos_high = sb("pos_high", [P, NT], F32R)
        w1_src = sb("w1_src", [P, HID])
        w1_high = sb("w1_high", [P, HID], F32R)
        window = [sb(f"window{j}", [P, WT], F32R) for j in range(2)]
        src_sb = [sb(f"src_sb{j}", [P, T], I32) for j in range(2)]
        gather_sb = [sb(f"gather_sb{j}", [P, T], I32) for j in range(2)]
        dst_sb = [sb(f"dst_sb{j}", [P, T], I32) for j in range(2)]
        key_rows = [sb(f"key_rows{j}", [P, T, P], I32) for j in range(2)]
        equal = [sb(f"equal{j}", [P, T, P], F32R) for j in range(2)]
        earlier = sb("earlier", [P, T, P])
        earlier_max = sb("earlier_max", [P, T])
        target = [sb(f"target{j}", [P, T], I32) for j in range(2)]
        ends = [sb(f"ends{j}", [P, T, W1 + 1]) for j in range(2)]
        ends_T = [sb(f"ends_T{j}", [P, B]) for j in range(2)]
        ends_parts = [sb(f"ends_parts{j}", [P, B], F32R) for j in range(2)]
        ends_hot = [sb(f"ends_hot{j}", [P, B], F32R) for j in range(2)]
        dst_rows_sb = [sb(f"dst_rows_sb{j}", [P, T, P], I32) for j in range(2)]
        scaled = [sb(f"scaled{j}", [P, B]) for j in range(NL)]
        hidden = [sb(f"hidden{k}", [P, B]) for k in range(NK)]
        alpha_scaled = sb("alpha_scaled", [P, T * H])
        alpha = sb("alpha", [P, T * H])
        alpha_exp = sb("alpha_exp", [P, T, H])
        beta_scaled = sb("beta_scaled", [P, T * H * D])
        beta = sb("beta", [P, T, H, D])
        terms0 = [sb(f"terms0_{j}", [P, T, W0]) for j in range(2)]
        terms_parts = [sb(f"terms_parts{a}", [P, T, W0 + 1], F32R) for a in range(2)]
        summed0 = [sb(f"summed0_{t}", [P, W0]) for t in range(T)]
        feat = [ends_T[j][:, 0:T * D].rearrange("p (t d) -> p t d", d=D) for j in range(2)]
        attn = [sb(f"attn{j}", [P, T]) for j in range(2)]
        ends1 = [scaled[j][:, 0:T * (D + 1)].rearrange("p (t d) -> p t d", d=D + 1) for j in range(2)]
        products = hidden[4][:, :].rearrange("p (a t d) -> p a t d", a=2, d=D)
        dots = sb("dots", [P, 2, T])
        gates = sb("gates", [P, 2, T])
        feat_gate = sb("feat_gate", [P, T])
        terms1 = [hidden[j][:, :].rearrange("p (t w) -> p t w", w=W1) for j in range(2)]
        summed1 = [hidden[2 + j][:, :].rearrange("p (t w) -> p t w", w=W1) for j in range(2)]
        ends1_windows = ends1 + [ends[j][:, :, 0:D + 1] for j in range(2)]
        feat_windows = feat + [key_rows[j][:, 0:2, :].rearrange("p t e -> p (t e)").bitcast(F32)
                               .rearrange("p (t d) -> p t d", d=D) for j in range(2)]
        terms1_windows = [hidden[m][:, :].rearrange("p (t w) -> p t w", w=W1) for m in range(4)]
        attn_windows = attn + [sb(f"attn{j}", [P, T]) for j in range(2, 4)]
        src_windows = src_sb + gather_sb
        hot = equal
        window_sum = sb("window_sum", [WIN, W1])
        inverse = sb("inverse", [P, CH, H])
        empty = sb("empty", [P, CH])
        mean = beta_scaled[:, 0:CH * D].rearrange("p (t d) -> p t d", d=D)
        feat_T = beta[0:D, :, :, :].rearrange("p t h d -> p (t h d)")[:, 0:CH * P].rearrange("d (t p) -> d t p", p=P)

        ps_T = pb("ps_T", [P, B])
        ps_hidden = [pb(f"ps_hidden{j}", [P, B]) for j in range(NL)]
        ps_beta = [pb(f"ps_beta{j}", [P, B]) for j in range(2)]
        ps_alpha = pb("ps_alpha", [P, B])
        ps_sum = pb("ps_sum", [P, B])

        loaded = sem("loaded")
        made = sem("made")
        zeroed = sem("zeroed")
        zeroed1 = sem("zeroed1")
        zeros_set = sem("zeros_set")
        weights_set = sem("weights_set")
        step = sem("step")
        sqrt_in = sem("sqrt_in")
        sqrt_out = sem("sqrt_out")
        tables = sem("tables")
        tables_split = sem("tables_split")
        edge_in = [sem(f"edge_in{j}") for j in range(2)]
        gather_in = [sem(f"gather_in{j}") for j in range(2)]
        gathered = [sem(f"gathered{j}") for j in range(2)]
        transposed = sem("transposed")
        ends_ready = sem("ends_ready")
        hidden_done = sem("hidden_done")
        scaled_ready = sem("scaled_ready")
        hidden_ready = sem("hidden_ready")
        second_done = sem("second_done")
        alpha_scaled_ready = sem("alpha_scaled_ready")
        alpha_ready = sem("alpha_ready")
        exp_ready = sem("exp_ready")
        weight_ready = sem("weight_ready")
        beta_scaled_ready = sem("beta_scaled_ready")
        beta_ready = sem("beta_ready")
        terms_ready = sem("terms_ready")
        dup_step = sem("dup_step")
        earlier_ready = sem("earlier_ready")
        summed = sem("summed")
        summed_ready = sem("summed_ready")
        scattered = [sem(f"scattered{c}") for c in range(COPIES)]
        part_sum = sem("part_sum")
        part_in = [sem(f"part_in{j}") for j in range(2)]
        part_free = sem("part_free")
        edge_in1 = [sem(f"edge_in1_{j}") for j in range(2)]
        gathered1 = [sem(f"gathered1_{j}") for j in range(2)]
        dot_step = sem("dot_step")
        gates_ready = sem("gates_ready")
        terms1_step = sem("terms1_step")
        dup_step1 = sem("dup_step1")
        summed1_done = sem("summed1_done")
        summed1_ready = sem("summed1_ready")
        scattered1 = [sem(f"scattered1_{t}") for t in range(T)]
        part_in1 = [sem(f"part_in1_{j}") for j in range(2)]
        part_sum1 = sem("part_sum1")
        copies_added = sem("copies_added")
        mean_step = sem("mean_step")
        feat_T_done = sem("feat_T_done")
        feat_T_ready = sem("feat_T_ready")
        review_done = sem("review_done")
        chunk_out = sem("chunk_out")
        stored = sem("stored")
        fits_step = sem("fits_step")
        firsts_ready = sem("firsts_ready")
        firsts_spread = sem("firsts_spread")
        reach_ready = sem("reach_ready")
        reach_turned = sem("reach_turned")
        fits_ready = sem("fits_ready")
        w_high_ready = sem("w_high_ready")
        w_low_ready = sem("w_low_ready")
        tail_step = sem("tail_step")
        h_turned = sem("h_turned")
        h_T_ready = sem("h_T_ready")
        projected = sem("projected")
        parts_split = sem("parts_split")
        pad_set = sem("pad_set")
        terms_high_ready = sem("terms_high_ready")
        terms_low_ready = sem("terms_low_ready")
        high_ready = sem("high_ready")
        low_ready = sem("low_ready")
        tail_ready = sem("tail_ready")
        row_out = [sem(f"row_out{j}") for j in range(2)]
        pads_out = sem("pads_out")
        window_in = [sem(f"window_in{j}") for j in range(2)]
        ends_parts_ready = sem("ends_parts_ready")
        ends_hot_ready = sem("ends_hot_ready")
        hot_T_ready = sem("hot_T_ready")
        hot_ready = sem("hot_ready")
        window_copied = sem("window_copied")
        edge_in1w = [sem(f"edge_in1w{m}") for m in range(4)]
        gathered1w = [sem(f"gathered1w{m}") for m in range(4)]
        window_added = sem("window_added")
        sums1_landed = sem("sums1_landed")
        settled = sem("settled")

        def wait(eng, s, value):
            if not (isinstance(value, int) and value <= 0):
                eng.wait_ge(s, value)

        def blocks(eng, body, tail=2):
            body(0, 0, 0)
            body(1, 0, 1)
            with eng.Fori(1, (NB - tail) // 2) as i:
                body(2 * i, i, 0)
                body(2 * i + 1, i, 1)
            for b in range(NB - tail, NB):
                body(b, b // 2, b % 2)

        def fours(eng, body):
            for m in range(4):
                body(m, 0, m)
            with eng.Fori(1, NB // 4 - 1) as i:
                for m in range(4):
                    body(4 * i + m, i, m)
            for m in range(4):
                body(NB - 4 + m, NB // 4 - 1, m)

        def early(b):
            return isinstance(b, int) and b < 2

        def first_four(b):
            return isinstance(b, int) and b < 4

        def is_last(b):
            return isinstance(b, int) and b == NB - 1

        def is_last_two(b):
            return isinstance(b, int) and b >= NB - 2

        def added(b):
            return 16 * (T // COPIES) * b

        def settle(eng):
            eng.sem_inc(settled, 1)

        def nodes(dram_ap):
            return dram_ap.rearrange("(p t) w -> p t w", p=P)

        def project_bank(t, k):
            return (ps_hidden if t % 2 == 0 else ps_beta)[k]

        def column_bank(t):
            return (ps_T, ps_alpha)[t % 2]

        LAYER0_STEPS = [0]
        LOADS = 13 + H

        def fits(eng):
            eng.wait_ge(fits_ready, 1)
            return eng.value_load(fits_sb[0:1, 0:1], min_val=0, max_val=1)

        def window_start(eng, b):
            return eng.value_load(first_node[0:1, bass.ds(b, 1)], min_val=0, max_val=N)

        block = ctx.enter_context(nc.Block())

        @block.sync
        def _(sp):
            sp.dma_start(x_sb[:, :, :], nodes(x)).then_inc(loaded, 16)
            sp.dma_start(pos_sb[:, :], node_vec).then_inc(loaded, 16)
            sp.dma_start(cj_sb[:, :], node_vec1).then_inc(loaded, 16)
            sp.dma_start(ci_sb[:, :], node_vec1_n2).then_inc(loaded, 16)
            sp.dma_start(w1_sb[:, :], w1).then_inc(loaded, 16)
            sp.dma_start(msg_w2_sb[:, :, :], msg_w2).then_inc(loaded, 16)
            sp.dma_start(dots_w[:, 0, :], prob_w.broadcast_to([P, D])).then_inc(loaded, 16)
            sp.dma_start(dots_w[:, 1, :], score_w.broadcast_to([P, D])).then_inc(loaded, 16)
            sp.dma_start(review_w_sb[:, :], review_w).then_inc(loaded, 16)
            sp.dma_start(w1_dst[:, :], w1[D:P, :]).then_inc(loaded, 16)
            sp.dma_start(dst_all_sb, dst_all).then_inc(loaded, 16)
            for a in range(2):
                sp.dma_start(w1_src[a * D:(a + 1) * D, :], w1[0:D, :]).then_inc(loaded, 16)
            sp.wait_ge(weights_set, 1)
            for h in range(H):
                sp.dma_start(gate_w2_sb[(h % 2) * D:(h % 2 + 1) * D, h // 2, h % 2:h % 2 + 1],
                             gate_w2[h]).then_inc(loaded, 16)

            def load0(b, half, j):
                if not (isinstance(b, int) and b < 2):
                    sp.wait_ge(dup_step, 4 * (b - 1))
                    settle(sp)
                    sp.wait_ge(gathered[j], 128 * half)
                    settle(sp)
                sp.dma_start(src_sb[j][:, :], src[bass.ds(b, 1)]).then_inc(edge_in[j], 16)
                sp.dma_start(dst_sb[j][:, :], dst[bass.ds(b, 1)]).then_inc(edge_in[j], 16)
                sp.dma_start(key_rows[j][:, :, :],
                             src_rows[bass.ds(b, 1)].broadcast_to([P, T, P])).then_inc(edge_in[j], 16)

            def load0_windows(b, half, j):
                if not early(b):
                    sp.wait_ge(hidden_done, NK * (b - 1))
                    settle(sp)
                first = window_start(sp, b)
                for a in range(2):
                    at = D + a * WIN0
                    sp.dma_start(window[j][at:at + WIN0, :].bitcast(F32),
                                 window_table[bass.ds(first, WIN0), a, :]).then_inc(window_in[j], 16)
                if not early(b):
                    sp.wait_ge(hot_T_ready, b - 1)
                    settle(sp)
                sp.dma_start(dst_rows_sb[j][D:P, :, :],
                             dst_rows[bass.ds(b, 1)].broadcast_to([P - D, T, P])).then_inc(window_in[j], 16)
                if not is_last_two(b):
                    sp.wait_ge(gathered[j], 64 * (half + 1))
                    settle(sp)
                    sp.dma_start(gather_sb[j][:, :], src[bass.ds(b + 2, 1)]).then_inc(gather_in[j], 16)
                if not early(b):
                    sp.wait_ge(dup_step, 4 * (b - 1))
                    settle(sp)
                sp.dma_start(src_sb[j][:, :], src[bass.ds(b, 1)]).then_inc(edge_in[j], 16)
                sp.dma_start(key_rows[j][:, :, :],
                             src_rows[bass.ds(b, 1)].broadcast_to([P, T, P])).then_inc(edge_in[j], 16)

            fit = fits(sp)
            with sp.If(fit):
                for b in range(2):
                    sp.dma_start(gather_sb[b][:, :], src[b:b + 1]).then_inc(gather_in[b], 16)
                sp.wait_ge(zeros_set, 1)
                sp.dma_start(window_table[NP:NP + P].rearrange("n a w -> n (a w)"), zeros[:, 0:2 * WT]).then_inc(pads_out, 16)
                for t in range(NT):
                    j = t % 2
                    sp.wait_ge(high_ready, 2 * t + 2)
                    sp.wait_ge(low_ready, 2 * t + 2)
                    sp.wait_ge(tail_ready, t + 1)
                    sp.dma_start(window_table[0:NP].rearrange("(p t) a w -> p t a w", p=P)[:, t, :, :],
                                 table_row[j].bitcast(F32)).then_inc(row_out[j], 16)
                sp.wait_ge(pads_out, 16)
                sp.wait_ge(row_out[0], 16 * ((NT + 1) // 2))
                sp.wait_ge(row_out[1], 16 * (NT // 2))
                blocks(sp, load0_windows)
                sp.wait_ge(zeroed1, 16)
            with sp.Else():
                blocks(sp, load0)
                sp.wait_ge(zeroed1, 16 * T)

            for c in range(NCH):
                if c == 0:
                    for k in range(COPIES):
                        sp.wait_ge(scattered[k], added(NB))
                if c >= 2:
                    sp.wait_ge(part_free, c - 1)
                for t in range(COPIES):
                    sp.dma_start(parts[c % 2][:, t, :, :],
                                 nodes(sums0[t][0:NP, :])[:, c * CH:(c + 1) * CH, :]).then_inc(part_in[c % 2], 16)

            def load1(b, half, j):
                if isinstance(b, int) and b < 2:
                    sp.wait_ge(dup_step, 4 * NB)
                    sp.wait_ge(gathered[j], 128 * (NB // 2))
                    sp.wait_ge(hidden_done, NK * NB)
                else:
                    sp.wait_ge(dup_step1, 4 * (b - 1))
                    settle(sp)
                    sp.wait_ge(gathered1[j], 64 * half)
                    settle(sp)
                    sp.wait_ge(terms1_step, 4 * (b - 1))
                    settle(sp)
                sp.dma_start(src_sb[j][:, :], src[bass.ds(b, 1)]).then_inc(edge_in1[j], 16)
                sp.dma_start(dst_sb[j][:, :], dst[bass.ds(b, 1)]).then_inc(edge_in1[j], 16)
                sp.dma_start(key_rows[j][:, :, :],
                             dst_rows[bass.ds(b, 1)].broadcast_to([P, T, P])).then_inc(edge_in1[j], 16)
                sp.dma_start(feat[j][:, :, :], edge_attr[bass.ds(b, 1)]).then_inc(edge_in1[j], 16)
                sp.dma_start(attn[j][:, :], edge_weight[bass.ds(b, 1)]).then_inc(edge_in1[j], 16)

            def load1_windows(b, quad, m):
                if first_four(b):
                    sp.wait_ge(gathered[0], 64 * (NB // 2))
                    sp.wait_ge(gathered[1], 64 * (NB // 2))
                    sp.wait_ge(dup_step, 4 * NB)
                else:
                    sp.wait_ge(gathered1w[m], 64 * quad)
                    settle(sp)
                    sp.wait_ge(terms1_step, 4 * (b - 3))
                    settle(sp)
                sp.dma_start(src_windows[m][:, :], src[bass.ds(b, 1)]).then_inc(edge_in1w[m], 16)
                sp.dma_start(feat_windows[m][:, :, :], edge_attr[bass.ds(b, 1)]).then_inc(edge_in1w[m], 16)
                sp.dma_start(attn_windows[m][:, :], edge_weight[bass.ds(b, 1)]).then_inc(edge_in1w[m], 16)

            with sp.If(fit):
                fours(sp, load1_windows)
            with sp.Else():
                blocks(sp, load1)

            def read_sums1(copies):
                for c in range(NCH):
                    if c == 0:
                        sp.wait_ge(sums1_landed, 1)
                    if c < 2:
                        sp.wait_ge(part_free, NCH)
                    else:
                        sp.wait_ge(part_free, NCH + c - 1)
                    for t in range(copies):
                        sp.dma_start(parts[c % 2][:, t, :, 0:W1],
                                     nodes(sums1[t][0:NP, :])[:, c * CH:(c + 1) * CH, :]).then_inc(part_in1[c % 2], 16)

            with sp.If(fit):
                read_sums1(1)
            with sp.Else():
                read_sums1(T)
            sp.wait_ge(chunk_out, NCH)
            sp.dma_start(nodes(out), x_sb[:, :, :]).then_inc(stored, 16)
            sp.wait_ge(stored, 16)

        @block.gpsimd
        def _(pool):
            nc.gpsimd.memset(ident[:, :], 0.0).then_inc(made, 1)
            nc.gpsimd.iota(spare[:, :], pattern=[[0, 1]], base=NP, channel_multiplier=1,
                           allow_small_or_imprecise_dtypes=True).then_inc(made, 1)
            pool.wait_ge(made, 2)
            nc.gpsimd.affine_select(out=ident[:, :], in_=ident[:, :], compare_op=ALU.not_equal, fill=1.0,
                                    base=0, pattern=[[-1, P]], channel_multiplier=1).then_inc(made, 1)
            nc.gpsimd.tensor_copy(before[:, :], spare[:, 0:1].broadcast_to([P, P])).then_inc(made, 1)
            pool.wait_ge(made, 4)
            nc.gpsimd.affine_select(out=before[:, :], in_=before[:, :], compare_op=ALU.is_gt, fill=0.0,
                                    base=0, pattern=[[-1, P]], channel_multiplier=1).then_inc(made, 1)

            nc.gpsimd.iota(node_sb[:, :], pattern=[[1, NT]], base=0, channel_multiplier=NT,
                           allow_small_or_imprecise_dtypes=True).then_inc(made, 1)
            nc.gpsimd.iota(columns[:, :], pattern=[[1, WIN]], base=0, channel_multiplier=0,
                           allow_small_or_imprecise_dtypes=True).then_inc(made, 1)

            def gather0(b, half, j):
                pool.wait_ge(edge_in[j], 48 * (half + 1))
                if not (isinstance(b, int) and b < 2):
                    pool.wait_ge(transposed, b - 1)
                    pool.wait_ge(weight_ready, b - 1)
                settle(pool)
                for t in range(T):
                    pool.indirect_dma_start(
                        out=ends[j][:, t, 0:D], out_offset=None, in_=row_table,
                        in_offset=bass.IndirectOffsetOnAxis(ap=src_sb[j][:, t:t + 1], axis=0)).then_inc(gathered[j], 16)
                    pool.indirect_dma_start(
                        out=ends[j][:, t, D:2 * D + 1], out_offset=None, in_=col_table,
                        in_offset=bass.IndirectOffsetOnAxis(ap=dst_sb[j][:, t:t + 1], axis=0)).then_inc(gathered[j], 16)

            def scatter_tile(b, j, t):
                pool.wait_ge(dup_step, 4 * b + 4)
                pool.wait_ge(summed_ready, 4 * b + t + 1)
                k = t % COPIES
                wait(pool, scattered[k], added(b) + 16 * (t // COPIES))
                settle(pool)
                pool.indirect_dma_start(
                    out=sums0[k], out_offset=bass.IndirectOffsetOnAxis(ap=target[j][:, t:t + 1], axis=0),
                    in_=summed0[t][:, :], in_offset=None, compute_op=ALU.add).then_inc(scattered[k], 16)

            def scatter0(b, half, j):
                for t in range(T):
                    scatter_tile(b, j, t)

            def edges0(b, half, j):
                if not is_last_two(b):
                    gather0(b + 2, half + 1, j)
                scatter0(b, half, j)

            def gather_tile(b, half, j, t):
                if t == 0:
                    pool.wait_ge(gather_in[j], 16 * (half + 1))
                    if not early(b):
                        pool.wait_ge(transposed, b - 1)
                    settle(pool)
                pool.indirect_dma_start(
                    out=ends[j][:, t, 0:2 * D], out_offset=None, in_=split_table,
                    in_offset=bass.IndirectOffsetOnAxis(ap=gather_sb[j][:, t:t + 1], axis=0)).then_inc(gathered[j], 16)

            def edges0_windows(b, half, j):
                for t in range(T):
                    if not (isinstance(b, int) and b >= NB - 4):
                        gather_tile(b + 4, half + 2, j, t)
                    scatter_tile(b, j, t)
                    if t == 1 and not is_last(b):
                        pairs_before(b + 1, 1 - j)

            def pairs_before(b, j):
                pool.wait_ge(dup_step, 4 * b + 1)
                settle(pool)
                nc.gpsimd.affine_select(out=earlier[:, :, :], in_=equal[j][:, :, :].bitcast(F32), compare_op=ALU.is_gt,
                                        fill=0.0, base=0, pattern=[[0, T], [-1, P]],
                                        channel_multiplier=1).then_inc(earlier_ready, 1)

            fit = fits(pool)
            with pool.If(fit):
                pool.wait_ge(tail_step, 5)
                for t in range(NT):
                    if t >= 2:
                        pool.wait_ge(row_out[t % 2], 16 * (t // 2))
                    nc.gpsimd.tensor_copy(table_row[t % 2][:, :, HID:WT].bitcast(F32), tails[:, t, :, :]).then_inc(tail_ready, 1)
                pool.wait_ge(tables_split, 32)
                for b in range(4):
                    for t in range(T):
                        gather_tile(b, b // 2, b % 2, t)
                pool.wait_ge(zeroed, 16 * 5 * COPIES)
                pairs_before(0, 0)
                blocks(pool, edges0_windows, tail=4)
            with pool.Else():
                pool.wait_ge(tables, 32)
                gather0(0, 0, 0)
                gather0(1, 0, 1)
                pool.wait_ge(zeroed, 16 * 5 * COPIES)
                blocks(pool, edges0)

            for c in range(NCH):
                pool.wait_ge(part_in[c % 2], 16 * COPIES * (c // 2 + 1))
                nc.gpsimd.tensor_tensor(parts[c % 2][:, 0, :, :], parts[c % 2][:, 0, :, :],
                                        parts[c % 2][:, 1, :, :], ALU.add).then_inc(part_sum, 1)

            def gather1(b, half, j):
                pool.wait_ge(edge_in1[j], 80 * (half + 1))
                if not (isinstance(b, int) and b < 2):
                    pool.wait_ge(terms1_step, 4 * (b - 1))
                settle(pool)
                for t in range(T):
                    pool.indirect_dma_start(
                        out=ends1[j][:, t, :], out_offset=None, in_=src_table,
                        in_offset=bass.IndirectOffsetOnAxis(ap=src_sb[j][:, t:t + 1], axis=0)).then_inc(gathered1[j], 16)

            def scatter1(b, half, j):
                pool.wait_ge(dup_step1, 4 * b + 4)
                pool.wait_ge(summed1_ready, b + 1)
                for t in range(T):
                    wait(pool, scattered1[t], 16 * b)
                    settle(pool)
                    pool.indirect_dma_start(
                        out=sums1[t], out_offset=bass.IndirectOffsetOnAxis(ap=target[j][:, t:t + 1], axis=0),
                        in_=summed1[j][:, t, :], in_offset=None, compute_op=ALU.add).then_inc(scattered1[t], 16)

            def edges1(b, half, j):
                if not is_last_two(b):
                    gather1(b + 2, half + 1, j)
                scatter1(b, half, j)

            def gather1_windows(b, quad, m):
                pool.wait_ge(edge_in1w[m], 48 * (quad + 1))
                if not first_four(b):
                    pool.wait_ge(terms1_step, 4 * (b - 3))
                settle(pool)
                for t in range(T):
                    pool.indirect_dma_start(
                        out=ends1_windows[m][:, t, :], out_offset=None, in_=src_table,
                        in_offset=bass.IndirectOffsetOnAxis(ap=src_windows[m][:, t:t + 1], axis=0)).then_inc(gathered1w[m], 16)

            def add_window(quad):
                first = window_start(pool, 4 * quad)
                pool.wait_ge(window_copied, quad + 1)
                settle(pool)
                if not (isinstance(quad, int) and quad == 0):
                    pool.wait_ge(window_added, 16 * quad)
                    settle(pool)
                pool.dma_start(sums1[0][bass.ds(first, WIN), :], window_sum[:, :],
                               accum_op=ALU.add).then_inc(window_added, 16)

            def edges1_windows(b, quad, m):
                gather1_windows(b, quad, m)
                if m == 2 and not first_four(b):
                    add_window(quad - 1)

            pool.wait_ge(tables, 48)
            with pool.If(fit):
                fours(pool, edges1_windows)
                add_window(NB // 4 - 1)
                pool.wait_ge(window_added, 16 * (NB // 4))
                pool.sem_inc(sums1_landed, 1)
            with pool.Else():
                gather1(0, 0, 0)
                gather1(1, 0, 1)
                blocks(pool, edges1)
                for t in range(T):
                    pool.wait_ge(scattered1[t], 16 * NB)
                pool.sem_inc(sums1_landed, 1)
                for c in range(NCH):
                    pool.wait_ge(part_in1[c % 2], 64 * (c // 2 + 1))
                    nc.gpsimd.tensor_tensor(parts[c % 2][:, 2, :, 0:W1], parts[c % 2][:, 2, :, 0:W1],
                                            parts[c % 2][:, 3, :, 0:W1], ALU.add).then_inc(part_sum1, 1)

        @block.scalar
        def _(act):
            def zero_sums1(copies):
                for t in range(copies):
                    act.dma_start(sums1[t].rearrange("(p a) w -> p a w", p=P),
                                  zeros[:, 0:W1].unsqueeze(1).broadcast_to([P, ROWS // P, W1])).then_inc(zeroed1, 16)

            act.wait_ge(zeros_set, 1)
            act.wait_ge(loaded, 16 * LOADS)
            for c in range(COPIES):
                flat = sums0[c].rearrange("(p a) w -> p (a w)", p=P)
                for k in range(5):
                    act.dma_start(flat[:, k * ZW:(k + 1) * ZW], zeros).then_inc(zeroed, 16)
            act.wait_ge(sqrt_in, 1)
            nc.scalar.activation(stat[:, 2, :], stat[:, 1, :], ACT.Sqrt).then_inc(sqrt_out, 1)
            act.wait_ge(step, STEPS_TABLE0)
            act.dma_start(nodes(row_table), table_sb[:, :, 0:D]).then_inc(tables, 16)
            act.dma_start(nodes(col_table), table_sb[:, :, :]).then_inc(tables, 16)

            def scale_chunk(b, k):
                act.wait_ge(hidden_done, NK * b + k + 1)
                wait(act, hidden_ready, NK * b + k + 1 - NL)
                nc.scalar.activation(scaled[k % NL][:, :], ps_hidden[k % NL][:, :], ACT.Copy,
                                     scale=SLOPE).then_inc(scaled_ready, 1)

            def scale_beta(b, half):
                act.wait_ge(second_done, NK * b + NK)
                wait(act, beta_ready, 2 * (b - 1) + half + 1)
                nc.scalar.activation(beta_scaled[:, half * B:(half + 1) * B], ps_beta[half][:, :], ACT.Copy,
                                     scale=SLOPE).then_inc(beta_scaled_ready, 1)

            def copy_sum(b, t):
                act.wait_ge(summed, 4 * b + t + 1)
                wait(act, scattered[t % COPIES], added(b - 1) + 16 * (t // COPIES + 1))
                nc.scalar.activation(summed0[t][:, :], ps_sum[:, 0:W0], ACT.Copy).then_inc(summed_ready, 1)

            def edges0(b, half, j):
                begun = not (isinstance(b, int) and b == 0)
                if begun:
                    scale_beta(b - 1, 0)
                scale_chunk(b, 0)
                if begun:
                    scale_beta(b - 1, 1)
                scale_chunk(b, 1)
                scale_chunk(b, 2)
                scale_chunk(b, 3)
                act.wait_ge(second_done, NK * b + 2)
                wait(act, alpha_ready, b)
                nc.scalar.activation(alpha_scaled[:, :], ps_alpha[:, 0:T * H], ACT.Copy,
                                     scale=SLOPE).then_inc(alpha_scaled_ready, 1)
                if begun:
                    copy_sum(b - 1, 0)
                act.wait_ge(alpha_ready, b + 1)
                wait(act, weight_ready, b)
                nc.scalar.activation(alpha_exp[:, :, :].rearrange("p t h -> p (t h)"), alpha[:, :],
                                     ACT.Exp).then_inc(exp_ready, 1)
                scale_chunk(b, 4)
                if begun:
                    copy_sum(b - 1, 1)
                scale_chunk(b, 5)
                if begun:
                    copy_sum(b - 1, 2)
                    copy_sum(b - 1, 3)

            def copy_ends(b, j):
                act.wait_ge(transposed, b + 1)
                wait(act, hidden_done, NK * (b - 1))
                nc.scalar.activation(ends_parts[j][:, :], ps_T[:, :], ACT.Copy).then_inc(ends_parts_ready, 1)
                nc.scalar.activation(ends_hot[j][0:D, :], ps_T[0:D, :], ACT.Copy).then_inc(ends_hot_ready, 1)

            def copy_sum_windows(b, t):
                act.wait_ge(summed, 4 * b + t + 1)
                wait(act, scattered[t % COPIES], added(b - 1) + 16 * (t // COPIES + 1))
                nc.scalar.activation(summed0[t][:, :], (ps_T, ps_sum)[t % 2][:, 0:W0], ACT.Copy).then_inc(summed_ready, 1)

            def round_terms(b, half):
                act.wait_ge(terms_ready, b + 1)
                wait(act, summed, 4 * b)
                nc.scalar.activation(terms_parts[0][:, 2 * half:2 * half + 2, 0:W0], terms0[0][:, 2 * half:2 * half + 2, :],
                                     ACT.Copy).then_inc(terms_high_ready, 1)

            def scale_alpha(b):
                act.wait_ge(second_done, NK * b + 2)
                wait(act, alpha_ready, b)
                nc.scalar.activation(alpha_scaled[:, :], ps_alpha[:, 0:T * H], ACT.Copy,
                                     scale=SLOPE).then_inc(alpha_scaled_ready, 1)

            def exp_alpha(b):
                act.wait_ge(alpha_ready, b + 1)
                wait(act, weight_ready, b)
                nc.scalar.activation(alpha_exp[:, :, :].rearrange("p t h -> p (t h)"), alpha[:, :],
                                     ACT.Exp).then_inc(exp_ready, 1)

            def edges0_windows(b, half, j):
                begun = not (isinstance(b, int) and b == 0)
                if begun:
                    scale_beta(b - 1, 0)
                    scale_beta(b - 1, 1)
                    if not (isinstance(b, int) and b == 1):
                        copy_sum_windows(b - 2, 3)
                scale_chunk(b, 2)
                if not is_last(b):
                    copy_ends(b + 1, 1 - j)
                scale_chunk(b, 3)
                scale_alpha(b)
                if begun:
                    round_terms(b - 1, 0)
                    round_terms(b - 1, 1)
                scale_chunk(b, 4)
                exp_alpha(b)
                scale_chunk(b, 5)
                if not is_last(b):
                    scale_chunk(b + 1, 0)
                if begun:
                    copy_sum_windows(b - 1, 0)
                    copy_sum_windows(b - 1, 1)
                if not is_last(b):
                    scale_chunk(b + 1, 1)
                if begun:
                    copy_sum_windows(b - 1, 2)

            fit = fits(act)
            with act.If(fit):
                act.wait_ge(parts_split, 2)
                for a in range(2):
                    act.dma_start(nodes(split_table)[:, :, a * D:(a + 1) * D], h_parts[a]).then_inc(tables_split, 16)
                act.wait_ge(loaded, 16 * LOADS)
                nc.scalar.activation(w1_high[:, :], w1_src[:, :], ACT.Copy).then_inc(w_high_ready, 1)
                def copy_column(t):
                    act.wait_ge(h_turned, t + 1)
                    if t >= 2:
                        act.wait_ge(projected, 2 * (t - 1))
                    nc.scalar.activation(h_T[t % 2][:, :], column_bank(t)[0:D, 0:P], ACT.Copy).then_inc(h_T_ready, 1)

                copy_column(0)
                copy_column(1)
                for t in range(NT):
                    j = t % 2
                    for k, n in enumerate((B, HID - B)):
                        act.wait_ge(projected, 2 * t + k + 1)
                        if t >= 2:
                            act.wait_ge(row_out[j], 16 * (t // 2))
                        nc.scalar.activation(table_row[j][:, 0, k * B:k * B + n], project_bank(t, k)[:, 0:n],
                                             ACT.Copy).then_inc(high_ready, 1)
                    if t + 2 < NT:
                        copy_column(t + 2)
                zero_sums1(1)
                copy_ends(0, 0)
                scale_chunk(0, 0)
                scale_chunk(0, 1)
                blocks(act, edges0_windows)
                scale_beta(NB - 1, 0)
                scale_beta(NB - 1, 1)
                copy_sum_windows(NB - 2, 3)
                round_terms(NB - 1, 0)
                round_terms(NB - 1, 1)
                for t in range(T):
                    copy_sum_windows(NB - 1, t)
            with act.Else():
                zero_sums1(T)
                blocks(act, edges0)
                scale_beta(NB - 1, 0)
                scale_beta(NB - 1, 1)
                for t in range(T):
                    copy_sum(NB - 1, t)

            act.wait_ge(sqrt_in, 2)
            nc.scalar.activation(stat[:, 2, :], stat[:, 1, :], ACT.Sqrt).then_inc(sqrt_out, 1)
            act.wait_ge(step, STEPS_TABLE1)
            act.dma_start(nodes(src_table), table_sb[:, :, :]).then_inc(tables, 16)

            def copy_sum1(b, j):
                act.wait_ge(summed1_done, b + 1)
                if not (isinstance(b, int) and b < 2):
                    for t in range(T):
                        act.wait_ge(scattered1[t], 16 * (b - 1))
                nc.scalar.activation(summed1[j][:, :, :].rearrange("p t w -> p (t w)"), ps_beta[j][:, :],
                                     ACT.Copy).then_inc(summed1_ready, 1)

            def edges1(b, half, j):
                act.wait_ge(dot_step, 4 * b + 4)
                wait(act, terms1_step, 4 * b)
                nc.scalar.activation(gates[:, :, :].rearrange("p a t -> p (a t)"),
                                     dots[:, :, :].rearrange("p a t -> p (a t)"), ACT.Sigmoid).then_inc(gates_ready, 1)
                if not (isinstance(b, int) and b == 0):
                    copy_sum1(b - 1, 1 - j)

            def edges1_windows(b, quad, m):
                act.wait_ge(dot_step, 4 * b + 4)
                wait(act, terms1_step, 4 * b)
                nc.scalar.activation(gates[:, :, :].rearrange("p a t -> p (a t)"),
                                     dots[:, :, :].rearrange("p a t -> p (a t)"), ACT.Sigmoid).then_inc(gates_ready, 1)
                if m == 0 and not first_four(b):
                    copy_window(quad - 1)

            def copy_window(quad):
                act.wait_ge(summed1_done, 4 * quad + 4)
                wait(act, window_added, 16 * quad)
                nc.scalar.activation(window_sum[:, :], ps_beta[0][0:WIN, 0:W1], ACT.Copy).then_inc(window_copied, 1)

            with act.If(fit):
                fours(act, edges1_windows)
                copy_window(NB // 4 - 1)
            with act.Else():
                blocks(act, edges1)
                copy_sum1(NB - 1, 1)

            for c in range(NCH):
                act.wait_ge(feat_T_done, c + 1)
                wait(act, review_done, c)
                nc.scalar.activation(feat_T[:, 0:4, :].rearrange("d t p -> d (t p)"), ps_hidden[0][0:D, :],
                                     ACT.Copy).then_inc(feat_T_ready, 1)
                nc.scalar.activation(feat_T[:, 4:CH, :].rearrange("d t p -> d (t p)"), ps_hidden[1][0:D, 0:(CH - 4) * P],
                                     ACT.Copy).then_inc(feat_T_ready, 1)

        @block.vector
        def _(dve):
            def link(ins):
                LAYER0_STEPS[0] += 1
                ins.then_inc(step, 1)
                dve.wait_ge(step, LAYER0_STEPS[0])

            nc.vector.memset(zeros, 0.0).then_inc(zeros_set, 1)
            nc.vector.memset(gate_w2_sb[:, :, :], 0.0).then_inc(weights_set, 1)
            for j in range(2):
                link(nc.vector.memset(terms0[j][:, :, W0 - 1:W0], 1.0))

            def norm(n):
                def wide(k):
                    return stat[:, k, :].unsqueeze(2).broadcast_to([P, NT, D])
                link(nc.vector.tensor_reduce(out=stat[:, 0, :], in_=x_sb[:, :, :], axis=AX.X, op=ALU.add))
                link(nc.vector.tensor_scalar(stat[:, 0, :], stat[:, 0, :], 1.0 / D, None, ALU.mult))
                link(nc.vector.tensor_tensor(centered[:, :, :], x_sb[:, :, :], wide(0), ALU.subtract))
                link(nc.vector.tensor_tensor(squares, centered[:, :, :], centered[:, :, :], ALU.mult))
                link(nc.vector.tensor_reduce(out=stat[:, 1, :], in_=squares, axis=AX.X, op=ALU.add))
                nc.vector.tensor_scalar(stat[:, 1, :], stat[:, 1, :], 1.0 / D, EPS, ALU.mult, ALU.add).then_inc(sqrt_in, 1)
                dve.wait_ge(sqrt_out, n)
                link(nc.vector.reciprocal(stat[:, 3, :], stat[:, 2, :]))
                link(nc.vector.tensor_tensor(centered[:, :, :], centered[:, :, :], wide(3), ALU.mult))
                link(nc.vector.tensor_scalar(centered[:, :, :], centered[:, :, :], 0.0, None, ALU.max))

            dve.wait_ge(loaded, 16 * LOADS)
            norm(1)
            link(nc.vector.tensor_copy(table_sb[:, :, 0:D], centered[:, :, :]))
            link(nc.vector.tensor_copy(table_sb[:, :, D:D + 1], pos_sb[:, :].unsqueeze(2)))
            assert LAYER0_STEPS[0] == STEPS_TABLE0
            dve.wait_ge(made, 7)

            def find_targets(b, j, keys, here, before_equal, before_target):
                before_equal()
                nc.vector.tensor_tensor(equal[j][:, :, :], key_rows[j][:, :, :],
                                        keys[j][:, :].unsqueeze(2).broadcast_to([P, T, P]),
                                        ALU.is_equal).then_inc(here, 1)
                dve.wait_ge(here, 4 * b + 1)
                nc.vector.tensor_tensor(earlier[:, :, :], equal[j][:, :, :].bitcast(F32),
                                        before[:, :].unsqueeze(1).broadcast_to([P, T, P]), ALU.mult).then_inc(here, 1)
                dve.wait_ge(here, 4 * b + 2)
                nc.vector.tensor_reduce(out=earlier_max[:, :], in_=earlier[:, :, :], axis=AX.X,
                                        op=ALU.max).then_inc(here, 1)
                dve.wait_ge(here, 4 * b + 3)
                before_target()
                nc.vector.tensor_tensor(target[j][:, :], earlier_max[:, :], keys[j][:, :], ALU.max).then_inc(here, 1)

            def turn_ends(b, j):
                dve.wait_ge(transposed, b + 1)
                wait(dve, hidden_done, NK * (b - 1))
                nc.vector.tensor_copy(ends_T[j][:, :], ps_T[:, :]).then_inc(ends_ready, 1)

            def rectify_chunk(b, k):
                dve.wait_ge(scaled_ready, NK * b + k + 1)
                if not (isinstance(b, int) and b == 0):
                    dve.wait_ge(second_done, NK * (b - 1) + k + 1)
                nc.vector.tensor_tensor(hidden[k][:, :], scaled[k % NL][:, :], ps_hidden[k % NL][:, :],
                                        ALU.max).then_inc(hidden_ready, 1)

            def rectify_beta(b, half):
                dve.wait_ge(beta_scaled_ready, 2 * b + half + 1)
                wait(dve, terms_ready, b)
                nc.vector.tensor_tensor(beta[:, :, :, :].rearrange("p t h d -> p (t h d)")[:, half * B:(half + 1) * B],
                                        beta_scaled[:, half * B:(half + 1) * B], ps_beta[half][:, :],
                                        ALU.max).then_inc(beta_ready, 1)

            def weigh_beta(b, j):
                dve.wait_ge(beta_ready, 2 * b + 2)
                dve.wait_ge(weight_ready, b + 1)
                nc.vector.tensor_tensor(
                    terms0[j][:, :, 0:H * D].rearrange("p t (h d) -> p t h d", h=H), beta[:, :, :, :],
                    terms0[j][:, :, H * D:H * D + H].unsqueeze(3).broadcast_to([P, T, H, D]),
                    ALU.mult).then_inc(terms_ready, 1)

            def targets0(b, j):
                def before_equal():
                    wait_in(b, j)
                    if not (isinstance(b, int) and b < 2):
                        dve.wait_ge(summed, 4 * (b - 1))
                def before_target():
                    if not (isinstance(b, int) and b < 2):
                        for k in range(COPIES):
                            dve.wait_ge(scattered[k], added(b - 1))
                find_targets(b, j, src_sb, dup_step, before_equal, before_target)

            halves = {}

            def wait_in(b, j):
                dve.wait_ge(edge_in[j], 48 * (halves["half"] + 1))

            def edges0(b, half, j):
                halves["half"] = half
                begun = not (isinstance(b, int) and b == 0)
                if begun:
                    rectify_beta(b - 1, 0)
                rectify_chunk(b, 0)
                if begun:
                    rectify_beta(b - 1, 1)
                rectify_chunk(b, 1)
                if begun:
                    weigh_beta(b - 1, 1 - j)
                rectify_chunk(b, 2)
                rectify_chunk(b, 3)
                dve.wait_ge(alpha_scaled_ready, b + 1)
                wait(dve, exp_ready, b)
                nc.vector.tensor_tensor(alpha[:, :], alpha_scaled[:, :], ps_alpha[:, 0:T * H],
                                        ALU.max).then_inc(alpha_ready, 1)
                targets0(b, j)
                rectify_chunk(b, 4)
                dve.wait_ge(exp_ready, b + 1)
                if not (isinstance(b, int) and b < 2):
                    dve.wait_ge(summed, 4 * (b - 1))
                nc.vector.tensor_tensor(terms0[j][:, :, H * D:H * D + H], alpha_exp[:, :, :],
                                        ends[j][:, :, 2 * D:2 * D + 1].broadcast_to([P, T, H]),
                                        ALU.mult).then_inc(weight_ready, 1)
                rectify_chunk(b, 5)
                if not is_last(b):
                    turn_ends(b + 1, 1 - j)

            def match_dst(b, half, j):
                dve.wait_ge(window_in[j], 48 * (half + 1))
                wait(dve, hidden_done, NK * (b - 1))
                nc.vector.tensor_scalar(ends_hot[j][D:P, :], dst_rows_sb[j][D:P, :, :].rearrange("p t e -> p (t e)"),
                                        window[j][D:P, HID:HID + 1].bitcast(F32), None,
                                        ALU.is_equal).then_inc(hot_T_ready, 1)

            def round_off(b, half):
                two = slice(2 * half, 2 * half + 2)
                dve.wait_ge(terms_high_ready, 2 * b + half + 1)
                nc.vector.tensor_tensor(terms_parts[1][:, two, 0:W0], terms0[0][:, two, :],
                                        terms_parts[0][:, two, 0:W0].bitcast(F32), ALU.subtract).then_inc(terms_low_ready, 1)

            def find_earlier(b):
                dve.wait_ge(earlier_ready, b + 1)
                nc.vector.tensor_reduce(out=earlier_max[:, :], in_=earlier[:, :, :], axis=AX.X,
                                        op=ALU.max).then_inc(dup_step, 1)

            def spare_earlier(b):
                dve.wait_ge(dup_step, 4 * b + 2)
                nc.vector.tensor_scalar(earlier_max[:, :], earlier_max[:, :], spare[:, 0:1], None,
                                        ALU.mult).then_inc(dup_step, 1)

            def choose_target(b, j):
                dve.wait_ge(dup_step, 4 * b + 3)
                if not early(b):
                    for k in range(COPIES):
                        dve.wait_ge(scattered[k], added(b - 1))
                nc.vector.tensor_tensor(target[j][:, :], earlier_max[:, :], src_sb[j][:, :], ALU.max).then_inc(dup_step, 1)

            def edges0_windows(b, half, j):
                begun = not (isinstance(b, int) and b == 0)
                if begun:
                    rectify_beta(b - 1, 0)
                    rectify_beta(b - 1, 1)
                rectify_chunk(b, 2)
                if begun:
                    weigh_beta(b - 1, 0)
                rectify_chunk(b, 3)
                dve.wait_ge(alpha_scaled_ready, b + 1)
                wait(dve, exp_ready, b)
                nc.vector.tensor_tensor(alpha[:, :], alpha_scaled[:, :], ps_alpha[:, 0:T * H],
                                        ALU.max).then_inc(alpha_ready, 1)
                if not is_last(b):
                    match_dst(b + 1, half + j, 1 - j)
                if begun:
                    find_earlier(b - 1)
                    round_off(b - 1, 0)
                rectify_chunk(b, 4)
                if begun:
                    spare_earlier(b - 1)
                    round_off(b - 1, 1)
                rectify_chunk(b, 5)
                if begun:
                    choose_target(b - 1, 1 - j)
                dve.wait_ge(edge_in[j], 32 * (half + 1))
                if not early(b):
                    dve.wait_ge(summed, 4 * (b - 1))
                nc.vector.tensor_tensor(equal[j][:, :, :], key_rows[j][:, :, :],
                                        src_sb[j][:, :].unsqueeze(2).broadcast_to([P, T, P]),
                                        ALU.is_equal).then_inc(dup_step, 1)
                dve.wait_ge(exp_ready, b + 1)
                wait(dve, terms_low_ready, 2 * b)
                nc.vector.tensor_tensor(terms0[0][:, :, H * D:H * D + H], alpha_exp[:, :, :],
                                        ps_alpha[:, T * H:T * H + 2 * T].rearrange("p (t a) -> p t a", a=2)[:, :, 0:1]
                                        .broadcast_to([P, T, H]), ALU.mult).then_inc(weight_ready, 1)
                if not is_last(b):
                    rectify_chunk(b + 1, 0)
                    rectify_chunk(b + 1, 1)

            dst_blocks = dst_all_sb.rearrange("p (w e) -> p w e", e=T)
            dst_fours = dst_all_sb.rearrange("p (w e) -> p w e", e=4 * T)
            nc.vector.memset(ones[:, :], 1.0).then_inc(fits_step, 1)
            nc.vector.tensor_copy(first_dst[:, :], dst_blocks[0:1, :, 0]).then_inc(firsts_ready, 1)
            nc.vector.tensor_copy(first_node[:, :], dst_blocks[0:1, :, 0]).then_inc(fits_step, 1)
            dve.wait_ge(firsts_spread, 1)
            nc.vector.tensor_tensor(offset0.rearrange("p (w e) -> p w e", e=T), dst_blocks,
                                    ps_sum[:, 0:NB].unsqueeze(2).broadcast_to([P, NB, T]),
                                    ALU.subtract).then_inc(fits_step, 1)
            nc.vector.tensor_tensor(offset[:, :].rearrange("p (w e) -> p w e", e=4 * T), dst_fours,
                                    ps_sum[:, 0:NB].rearrange("p (w a) -> p w a", a=4)[:, :, 0:1]
                                    .broadcast_to([P, NB // 4, 4 * T]), ALU.subtract).then_inc(fits_step, 1)
            dve.wait_ge(fits_step, 4)
            for k, o in enumerate((offset0, offset[:, :])):
                nc.vector.tensor_reduce(out=reach[:, k:k + 1], in_=o, axis=AX.X, op=ALU.max).then_inc(fits_step, 1)
                nc.vector.tensor_reduce(out=reach[:, 2 + k:3 + k], in_=o, axis=AX.X, op=ALU.min).then_inc(fits_step, 1)
            dve.wait_ge(fits_step, 8)
            nc.vector.tensor_scalar(reach[:, 4:5], reach[:, 0:1], float(WIN - WIN0), None, ALU.add).then_inc(fits_step, 1)
            nc.vector.tensor_scalar(reach[:, 5:7], reach[:, 2:4], -1.0, float(WIN - 1), ALU.mult, ALU.add).then_inc(fits_step, 1)
            nc.vector.tensor_copy(reach[:, 7:8], reach[:, 1:2]).then_inc(fits_step, 1)
            dve.wait_ge(fits_step, 11)
            nc.vector.tensor_reduce(out=reach[:, 0:1], in_=reach[:, 4:8], axis=AX.X, op=ALU.max).then_inc(reach_ready, 1)
            dve.wait_ge(reach_turned, 1)
            nc.vector.tensor_reduce(out=first_dst[0:1, 0:1], in_=ps_sum[0:1, 0:P], axis=AX.X,
                                    op=ALU.max).then_inc(fits_step, 1)
            dve.wait_ge(fits_step, 12)
            nc.vector.tensor_scalar(fits_sb[:, :], first_dst[0:1, 0:1], float(WIN - 1), None,
                                    ALU.is_le).then_inc(fits_ready, 1)

            fit = fits(dve)
            with dve.If(fit):
                dve.wait_ge(step, STEPS_TABLE0)
                nc.vector.tensor_copy(h_parts[0].bitcast(F32R), centered[:, :, :]).then_inc(parts_split, 1)
                dve.wait_ge(parts_split, 1)
                nc.vector.tensor_tensor(h_parts[1], centered[:, :, :], h_parts[0], ALU.subtract).then_inc(parts_split, 1)
                for a in range(2):
                    nc.vector.memset(terms_parts[a][:, :, W0:W0 + 1].bitcast(F32), 0.0).then_inc(pad_set, 1)
                nc.vector.memset(tails[:, :, :, :], 0.0).then_inc(tail_step, 1)
                nc.vector.tensor_copy(pos_high[:, :], pos_sb[:, :]).then_inc(tail_step, 1)
                dve.wait_ge(tail_step, 2)
                nc.vector.tensor_copy(tails[:, :, :, 0], node_sb[:, :].unsqueeze(2).broadcast_to([P, NT, 2])).then_inc(tail_step, 1)
                nc.vector.tensor_copy(tails[:, :, 0, 2], pos_high[:, :].bitcast(F32)).then_inc(tail_step, 1)
                nc.vector.tensor_tensor(tails[:, :, 1, 2], pos_sb[:, :], pos_high[:, :].bitcast(F32),
                                        ALU.subtract).then_inc(tail_step, 1)
                dve.wait_ge(w_high_ready, 1)
                for j in range(2):
                    nc.vector.tensor_tensor(window[j][0:D, 0:HID], w1_src[0:D, :], w1_high[0:D, :].bitcast(F32),
                                            ALU.subtract).then_inc(w_low_ready, 1)
                for t in range(NT):
                    j = t % 2
                    for k, n in enumerate((B, HID - B)):
                        dve.wait_ge(high_ready, 2 * t + k + 1)
                        nc.vector.tensor_tensor(table_row[j][:, 1, k * B:k * B + n], project_bank(t, k)[:, 0:n],
                                                table_row[j][:, 0, k * B:k * B + n].bitcast(F32),
                                                ALU.subtract).then_inc(low_ready, 1)
                match_dst(0, 0, 0)
                rectify_chunk(0, 0)
                rectify_chunk(0, 1)
                blocks(dve, edges0_windows)
                rectify_beta(NB - 1, 0)
                rectify_beta(NB - 1, 1)
                weigh_beta(NB - 1, 0)
                find_earlier(NB - 1)
                spare_earlier(NB - 1)
                choose_target(NB - 1, 1)
                round_off(NB - 1, 0)
                round_off(NB - 1, 1)
            with dve.Else():
                turn_ends(0, 0)
                blocks(dve, edges0)
                rectify_beta(NB - 1, 0)
                rectify_beta(NB - 1, 1)
                weigh_beta(NB - 1, 1)

            for c in range(NCH):
                q = parts[c % 2]
                dve.wait_ge(part_sum, c + 1)
                link(nc.vector.tensor_scalar(empty[:, :].unsqueeze(2), q[:, 0, :, W0 - 1:W0], 0.0, None, ALU.is_equal))
                link(nc.vector.tensor_tensor(inverse[:, :, :], q[:, 0, :, H * D:H * D + H],
                                             empty[:, :].unsqueeze(2).broadcast_to([P, CH, H]), ALU.add))
                link(nc.vector.reciprocal(inverse[:, :, :], inverse[:, :, :]))
                link(nc.vector.tensor_scalar(inverse[:, :, :], inverse[:, :, :], 1e-16, 1.0 / H, ALU.add, ALU.mult))
                for t in range(CH):
                    last = nc.vector.tensor_tensor(q[:, 1, t, 0:H * D].rearrange("p (h d) -> p h d", h=H),
                                                   q[:, 0, t, 0:H * D].rearrange("p (h d) -> p h d", h=H),
                                                   inverse[:, t, :].unsqueeze(2).broadcast_to([P, H, D]), ALU.mult)
                link(last)
                for t in range(CH):
                    last = nc.vector.tensor_reduce(out=mean[:, t, :], in_=q[:, 1, t, 0:H * D].rearrange("p (h d) -> p d h", h=H),
                                                   axis=AX.X, op=ALU.add)
                last.then_inc(part_free, 1)
                dve.wait_ge(part_free, c + 1)
                link(nc.vector.tensor_tensor(x_sb[:, c * CH:(c + 1) * CH, :], x_sb[:, c * CH:(c + 1) * CH, :],
                                             mean[:, :, :], ALU.add))
            norm(2)
            link(nc.vector.tensor_tensor(table_sb[:, :, 0:D], centered[:, :, :],
                                         cj_sb[:, :].unsqueeze(2).broadcast_to([P, NT, D]), ALU.mult))
            link(nc.vector.tensor_copy(table_sb[:, :, D:D + 1], cj_sb[:, :].unsqueeze(2)))
            assert LAYER0_STEPS[0] == STEPS_TABLE1

            def edges1(b, half, j):
                def before_equal():
                    dve.wait_ge(edge_in1[j], 80 * (half + 1))
                    if not (isinstance(b, int) and b < 2):
                        dve.wait_ge(summed1_done, b - 1)
                    elif b < 2:
                        dve.wait_ge(summed, 4 * NB)
                def before_target():
                    for t in range(T):
                        if isinstance(b, int) and b < 2:
                            dve.wait_ge(scattered[t % COPIES], added(NB))
                        else:
                            dve.wait_ge(scattered1[t], 16 * (b - 1))
                dve.wait_ge(edge_in1[j], 80 * (half + 1))
                wait(dve, dot_step, 4 * b)
                for a in range(2):
                    nc.vector.tensor_tensor(products[:, a, :, :], feat[j][:, :, :],
                                            dots_w[:, a, :].unsqueeze(1).broadcast_to([P, T, D]),
                                            ALU.mult).then_inc(dot_step, 1)
                wait(dve, gates_ready, b)
                for a in range(2):
                    dve.wait_ge(dot_step, 4 * b + 1 + a)
                    nc.vector.tensor_reduce(out=dots[:, a, :], in_=products[:, a, :, :], axis=AX.X,
                                            op=ALU.add).then_inc(dot_step, 1)
                find_targets(b, j, dst_sb, dup_step1, before_equal, before_target)
                dve.wait_ge(gates_ready, b + 1)
                nc.vector.tensor_tensor(feat_gate[:, :], gates[:, 1, :], attn[j][:, :], ALU.mult).then_inc(terms1_step, 1)
                dve.wait_ge(gathered1[j], 64 * (half + 1))
                if not (isinstance(b, int) and b < 2):
                    dve.wait_ge(summed1_done, b - 1)
                nc.vector.tensor_tensor(terms1[j][:, :, 0:D], ends1[j][:, :, 0:D],
                                        gates[:, 0, :].unsqueeze(2).broadcast_to([P, T, D]), ALU.mult).then_inc(terms1_step, 1)
                dve.wait_ge(terms1_step, 4 * b + 2)
                nc.vector.tensor_tensor(feat_gate[:, :].unsqueeze(2), feat_gate[:, :].unsqueeze(2),
                                        ends1[j][:, :, D:D + 1], ALU.mult).then_inc(terms1_step, 1)
                dve.wait_ge(terms1_step, 4 * b + 3)
                nc.vector.tensor_tensor(terms1[j][:, :, D:W1], feat[j][:, :, :],
                                        feat_gate[:, :].unsqueeze(2).broadcast_to([P, T, D]), ALU.mult).then_inc(terms1_step, 1)

            def edge_gates(b, quad, m):
                dve.wait_ge(edge_in1w[m], 48 * (quad + 1))
                wait(dve, dot_step, 4 * b)
                for a in range(2):
                    nc.vector.tensor_tensor(products[:, a, :, :], feat_windows[m][:, :, :],
                                            dots_w[:, a, :].unsqueeze(1).broadcast_to([P, T, D]),
                                            ALU.mult).then_inc(dot_step, 1)
                wait(dve, gates_ready, b)
                for a in range(2):
                    dve.wait_ge(dot_step, 4 * b + 1 + a)
                    nc.vector.tensor_reduce(out=dots[:, a, :], in_=products[:, a, :, :], axis=AX.X,
                                            op=ALU.add).then_inc(dot_step, 1)

            def edges1_windows(b, quad, m):
                edge_gates(b, quad, m)
                if not early(b):
                    dve.wait_ge(summed1_done, b - 1)
                nc.vector.tensor_tensor(hot[m % 2][:, :, :], columns[:, :].unsqueeze(1).broadcast_to([P, T, WIN]),
                                        offset[:, bass.ds(b * T, T)].unsqueeze(2).broadcast_to([P, T, WIN]),
                                        ALU.is_equal).then_inc(hot_ready, 1)
                dve.wait_ge(gates_ready, b + 1)
                nc.vector.tensor_tensor(feat_gate[:, :], gates[:, 1, :], attn_windows[m][:, :], ALU.mult).then_inc(terms1_step, 1)
                dve.wait_ge(gathered1w[m], 64 * (quad + 1))
                nc.vector.tensor_tensor(terms1_windows[m][:, :, 0:D], ends1_windows[m][:, :, 0:D],
                                        gates[:, 0, :].unsqueeze(2).broadcast_to([P, T, D]), ALU.mult).then_inc(terms1_step, 1)
                dve.wait_ge(terms1_step, 4 * b + 2)
                nc.vector.tensor_tensor(feat_gate[:, :].unsqueeze(2), feat_gate[:, :].unsqueeze(2),
                                        ends1_windows[m][:, :, D:D + 1], ALU.mult).then_inc(terms1_step, 1)
                dve.wait_ge(terms1_step, 4 * b + 3)
                nc.vector.tensor_tensor(terms1_windows[m][:, :, D:W1], feat_windows[m][:, :, :],
                                        feat_gate[:, :].unsqueeze(2).broadcast_to([P, T, D]), ALU.mult).then_inc(terms1_step, 1)

            with dve.If(fit):
                fours(dve, edges1_windows)
            with dve.Else():
                blocks(dve, edges1)

            def add_copies(c):
                q = parts[c % 2]
                dve.wait_ge(part_in1[c % 2], 64 * (c // 2 + 1))
                nc.vector.tensor_tensor(q[:, 0, :, 0:W1], q[:, 0, :, 0:W1], q[:, 1, :, 0:W1], ALU.add).then_inc(copies_added, 1)
                dve.wait_ge(part_sum1, c + 1)
                dve.wait_ge(copies_added, 2 * c + 1)
                nc.vector.tensor_tensor(q[:, 0, :, 0:W1], q[:, 0, :, 0:W1], q[:, 2, :, 0:W1], ALU.add).then_inc(copies_added, 1)
                dve.wait_ge(copies_added, 2 * c + 2)

            def finish_chunk(c, add):
                q = parts[c % 2]
                if add:
                    add_copies(c)
                else:
                    dve.wait_ge(part_in1[c % 2], 16 * (c // 2 + 1))
                dve.wait_ge(review_done, c + 1)
                nc.vector.tensor_tensor(mean[:, :, :], q[:, 0, :, 0:D],
                                        ps_sum[:, 0:CH * D].rearrange("p (t d) -> p t d", t=CH), ALU.add).then_inc(mean_step, 1)
                dve.wait_ge(mean_step, c + 1)
                nc.vector.tensor_tensor(mean[:, :, :], mean[:, :, :],
                                        ci_sb[:, c * CH:(c + 1) * CH].unsqueeze(2).broadcast_to([P, CH, D]),
                                        ALU.mult).then_inc(part_free, 1)
                dve.wait_ge(part_free, NCH + c + 1)
                nc.vector.tensor_tensor(x_sb[:, c * CH:(c + 1) * CH, :], x_sb[:, c * CH:(c + 1) * CH, :],
                                        mean[:, :, :], ALU.add).then_inc(chunk_out, 1)
                dve.wait_ge(chunk_out, c + 1)

            with dve.If(fit):
                for c in range(NCH):
                    finish_chunk(c, False)
            with dve.Else():
                for c in range(NCH):
                    finish_chunk(c, True)

        @block.tensor
        def _(pe):
            def transpose_ends(b, half, j):
                pe.wait_ge(gathered[j], 128 * (half + 1))
                wait(pe, ends_ready, b)
                for t in range(T):
                    last = nc.tensor.transpose(ps_T[:, t * P:(t + 1) * P], ends[j][:, t, 0:2 * D], ident[:, :])
                last.then_inc(transposed, 1)

            def first_product(b, k, j):
                if k == 0:
                    pe.wait_ge(ends_ready, b + 1)
                wait(pe, hidden_ready, NK * b + k + 1 - NL)
                nc.tensor.matmul(ps_hidden[k % NL][:, :], w1_sb[:, k * P:(k + 1) * P], ends_T[j][:, :],
                                 start=True, stop=True).then_inc(hidden_done, 1)

            def turn_src(b, half, j):
                pe.wait_ge(gathered[j], 64 * (half + 1))
                wait(pe, ends_hot_ready, b)
                if not (isinstance(b, int) and b < 3):
                    pe.wait_ge(summed_ready, 4 * (b - 3) + 3)
                settle(pe)
                for t in range(T):
                    last = nc.tensor.transpose(ps_T[:, t * P:(t + 1) * P],
                                               ends[j][:, t, 0:2 * D], ident[:, :])
                last.then_inc(transposed, 1)

            def first_product_windows(b, k, half, j):
                if k == 0:
                    pe.wait_ge(ends_hot_ready, b + 1)
                    pe.wait_ge(hot_T_ready, b + 1)
                    pe.wait_ge(window_in[j], 48 * (half + 1))
                wait(pe, hidden_ready, NK * b + k + 1 - NL)
                o = ps_hidden[k % NL][:, :]
                nc.tensor.matmul(o, w1_high[:, k * P:(k + 1) * P], ends_parts[j][:, :], start=True, stop=False)
                nc.tensor.matmul(o, window[j][:, k * P:(k + 1) * P], ends_hot[j][:, :],
                                 start=False, stop=True).then_inc(hidden_done, 1)

            def dst_vec(b, j):
                wait(pe, weight_ready, b)
                for t in range(T):
                    nc.tensor.matmul(ps_alpha[:, T * H + 2 * t:T * H + 2 * t + 2],
                                     ends_hot[j][D:P, t * P:(t + 1) * P], window[j][D:P, HID + 2:WT], start=True, stop=True)

            def second_product(b, k):
                pe.wait_ge(hidden_ready, NK * b + k + 1)
                if k == 0:
                    wait(pe, alpha_ready, b)
                if k == 2:
                    wait(pe, beta_ready, 2 * b)
                for t in range(T):
                    if k < 2:
                        o, w = ps_alpha[:, t * H + 2 * k:t * H + 2 * k + 2], gate_w2_sb[:, k, :]
                    else:
                        at = (t % 2) * H * D + (k - 2) * D
                        o, w = ps_beta[t // 2][:, at:at + D], msg_w2_sb[:, k - 2, :]
                    last = nc.tensor.matmul(o, hidden[k][:, t * P:(t + 1) * P], w, start=True, stop=True)
                last.then_inc(second_done, 1)

            def sum_tile(b, t, j):
                if t == 0:
                    pe.wait_ge(terms_ready, b + 1)
                    pe.wait_ge(dup_step, 4 * b + 1)
                wait(pe, summed_ready, 4 * b + t)
                nc.tensor.matmul(ps_sum[:, 0:W0], equal[j][:, t, :].bitcast(F32), terms0[j][:, t, :],
                                 start=True, stop=True).then_inc(summed, 1)

            def sum_parts(b, t, j):
                if t % 2 == 0:
                    pe.wait_ge(terms_low_ready, 2 * b + t // 2 + 1)
                if t == 0:
                    pe.wait_ge(pad_set, 2)
                    pe.wait_ge(dup_step, 4 * b + 1)
                wait(pe, summed_ready, 4 * b + t - 1)
                if t == 0:
                    pe.wait_ge(ends_hot_ready, min(b + 3, NB) if isinstance(b, int) else b + 3)
                for a in range(2):
                    last = nc.tensor.matmul((ps_T, ps_sum)[t % 2][:, 0:W0 + 1], equal[j][:, t, :], terms_parts[a][:, t, :],
                                            start=(a == 0), stop=(a == 1))
                last.then_inc(summed, 1)

            def edges0_windows(b, half, j):
                begun = not (isinstance(b, int) and b == 0)
                first_product_windows(b, 2, half, j)
                dst_vec(b, j)
                if not is_last(b):
                    turn_src(b + 1, half + j, 1 - j)
                first_product_windows(b, 3, half, j)
                second_product(b, 0)
                first_product_windows(b, 4, half, j)
                second_product(b, 1)
                second_product(b, 2)
                first_product_windows(b, 5, half, j)
                second_product(b, 3)
                if not is_last(b):
                    first_product_windows(b + 1, 0, half + j, 1 - j)
                if begun:
                    sum_parts(b - 1, 0, 1 - j)
                second_product(b, 4)
                if begun:
                    sum_parts(b - 1, 1, 1 - j)
                if not is_last(b):
                    first_product_windows(b + 1, 1, half + j, 1 - j)
                if begun:
                    sum_parts(b - 1, 2, 1 - j)
                second_product(b, 5)
                if begun:
                    sum_parts(b - 1, 3, 1 - j)

            def edges0(b, half, j):
                begun = not (isinstance(b, int) and b == 0)
                first_product(b, 0, j)
                first_product(b, 1, j)
                first_product(b, 2, j)
                second_product(b, 0)
                first_product(b, 3, j)
                second_product(b, 1)
                if begun:
                    sum_tile(b - 1, 0, 1 - j)
                first_product(b, 4, j)
                second_product(b, 2)
                if begun:
                    sum_tile(b - 1, 1, 1 - j)
                first_product(b, 5, j)
                second_product(b, 3)
                if begun:
                    sum_tile(b - 1, 2, 1 - j)
                if not is_last(b):
                    transpose_ends(b + 1, half + j, 1 - j)
                second_product(b, 4)
                if begun:
                    sum_tile(b - 1, 3, 1 - j)
                second_product(b, 5)

            pe.wait_ge(made, 7)
            pe.wait_ge(loaded, 16 * LOADS)
            pe.wait_ge(fits_step, 1)
            pe.wait_ge(firsts_ready, 1)
            nc.tensor.matmul(ps_sum[:, 0:NB], ones[:, :], first_dst[:, :], start=True,
                             stop=True).then_inc(firsts_spread, 1)
            pe.wait_ge(reach_ready, 1)
            nc.tensor.transpose(ps_sum[0:1, 0:P], reach[:, 0:1], ident[:, :]).then_inc(reach_turned, 1)

            def turn_column(t):
                wait(pe, h_T_ready, t - 1)
                nc.tensor.transpose(column_bank(t)[0:D, 0:P], centered[:, t, :], ident[:, :]).then_inc(h_turned, 1)

            fit = fits(pe)
            with pe.If(fit):
                pe.wait_ge(step, STEPS_TABLE0 - 2)
                pe.wait_ge(w_low_ready, 2)
                for t in range(NT):
                    if t == 0:
                        turn_column(0)
                    if t < NT - 1:
                        turn_column(t + 1)
                    pe.wait_ge(h_T_ready, t + 1)
                    for k, n in enumerate((B, HID - B)):
                        wait(pe, low_ready, 2 * (t - 2) + k + 1)
                        nc.tensor.matmul(project_bank(t, k)[:, 0:n], h_T[t % 2][:, :], w1_dst[:, k * B:k * B + n],
                                         start=True, stop=True).then_inc(projected, 1)
                turn_src(0, 0, 0)
                first_product_windows(0, 0, 0, 0)
                first_product_windows(0, 1, 0, 0)
                blocks(pe, edges0_windows)
                for t in range(T):
                    sum_parts(NB - 1, t, 1)
            with pe.Else():
                transpose_ends(0, 0, 0)
                blocks(pe, edges0)
                for t in range(T):
                    sum_tile(NB - 1, t, 1)

            def edges1(b, half, j):
                pe.wait_ge(terms1_step, 4 * b + 4)
                pe.wait_ge(dup_step1, 4 * b + 1)
                if isinstance(b, int) and b < 2:
                    pe.wait_ge(beta_ready, 2 * NB)
                else:
                    pe.wait_ge(summed1_ready, b - 1)
                for t in range(T):
                    last = nc.tensor.matmul(ps_beta[j][:, t * W1:(t + 1) * W1], equal[j][:, t, :].bitcast(F32), terms1[j][:, t, :],
                                            start=True, stop=True)
                last.then_inc(summed1_done, 1)

            def edges1_windows(b, quad, m):
                pe.wait_ge(terms1_step, 4 * b + 4)
                pe.wait_ge(hot_ready, b + 1)
                if m == 0:
                    if first_four(b):
                        pe.wait_ge(beta_ready, 2 * NB)
                    else:
                        pe.wait_ge(window_copied, quad)
                for t in range(T):
                    last = nc.tensor.matmul(ps_beta[0][0:WIN, 0:W1], hot[m % 2][:, t, :].bitcast(F32), terms1_windows[m][:, t, :],
                                            start=(m == 0 and t == 0), stop=(m == 3 and t == T - 1))
                last.then_inc(summed1_done, 1)

            with pe.If(fit):
                fours(pe, edges1_windows)
            with pe.Else():
                blocks(pe, edges1)

            def project_sums(c, added):
                if added:
                    pe.wait_ge(copies_added, 2 * c + 2)
                else:
                    pe.wait_ge(part_in1[c % 2], 16 * (c // 2 + 1))
                wait(pe, feat_T_ready, 2 * c)
                for t in range(CH):
                    last = nc.tensor.transpose(ps_hidden[t // 4][0:D, (t % 4) * P:(t % 4 + 1) * P],
                                               parts[c % 2][:, 0, t, D:W1], ident[:, :])
                last.then_inc(feat_T_done, 1)
                pe.wait_ge(feat_T_ready, 2 * c + 2)
                wait(pe, mean_step, c)
                for t in range(CH):
                    last = nc.tensor.matmul(ps_sum[:, t * D:(t + 1) * D], feat_T[:, t, :], review_w_sb[:, :],
                                            start=True, stop=True)
                last.then_inc(review_done, 1)

            with pe.If(fit):
                for c in range(NCH):
                    project_sums(c, False)
            with pe.Else():
                for c in range(NCH):
                    project_sums(c, True)


NORM_STEPS = 8
STEPS_TABLE0 = 2 + NORM_STEPS + 2
STEPS_TABLE1 = STEPS_TABLE0 + 6 * NCH + NORM_STEPS + 2


def kernel(x, src, dst, edge_attr_64, edge_weight, node_vec, node_vec1, node_vec1_n2, L0_gnn_gate_w1,
           L0_gnn_gate_w2, L0_gnn_msg_w1, L0_gnn_msg_w2, L1_gnn_prob_w, L1_gnn_review_score_w, L1_gnn_review_w):
    import concourse.bacc as bacc
    from concourse.bass_utils import run_bass_kernel_spmd

    def padded(a, n, value=0):
        a = np.asarray(a)
        return np.concatenate([a, np.full((n - a.shape[0],) + a.shape[1:], value, a.dtype)])

    src, dst = padded(src, EP, N), padded(dst, EP, N)
    first = np.concatenate([np.asarray(L0_gnn_gate_w1).reshape(2 * P, P), np.asarray(L0_gnn_msg_w1).reshape(4 * P, P)])
    arrays = {
        "x": padded(x, NP),
        "src": src.reshape(NB, P, T), "dst": dst.reshape(NB, P, T),
        "src_rows": src.reshape(NB, P, T).transpose(0, 2, 1), "dst_rows": dst.reshape(NB, P, T).transpose(0, 2, 1),
        "dst_all": dst.reshape(NB, P, T).transpose(1, 0, 2).reshape(P, NB * T),
        "edge_attr": padded(edge_attr_64, EP).reshape(NB, P, T, D),
        "edge_weight": padded(edge_weight, EP).reshape(NB, P, T),
        "node_vec": padded(node_vec, NP, 1).reshape(P, NT),
        "node_vec1": padded(node_vec1, NP).reshape(P, NT),
        "node_vec1_n2": padded(node_vec1_n2, NP).reshape(P, NT),
        "w1": first.T,
        "gate_w2": np.asarray(L0_gnn_gate_w2).reshape(H, D, 1),
        "msg_w2": np.asarray(L0_gnn_msg_w2).transpose(2, 0, 1),
        "prob_w": np.asarray(L1_gnn_prob_w), "score_w": np.asarray(L1_gnn_review_score_w),
        "review_w": np.asarray(L1_gnn_review_w).T,
    }
    arrays = {f"in_{k}": np.ascontiguousarray(a) for k, a in arrays.items()}
    nc = bacc.Bacc("TRN2", target_bir_lowering=False, num_devices=1)
    args = [nc.dram_tensor(k, a.shape, mybir.dt.from_np(a.dtype), kind="ExternalInput").ap() for k, a in arrays.items()]
    out = nc.dram_tensor("out", (NP, D), F32, kind="ExternalOutput").ap()
    gnn(nc, *args, out)
    r = run_bass_kernel_spmd(nc, [arrays], core_ids=[0])
    return r.results[0]["out"][:N]
```
